# Optimizing a Trainium2 kernel written in Bass

```python
import numpy as np
import jax
import jax.numpy as jnp

def _softmax(x, axis=-1):
    return jax.nn.softmax(x, axis=axis)

def _gelu(x):
    return jax.nn.gelu(x, approximate=True)

def _silu(x):
    return jax.nn.silu(x)

def _sigmoid(x):
    return jax.nn.sigmoid(x)

def _layernorm(x, axis=-1, eps=1e-05):
    m = jnp.mean(x, axis=axis, keepdims=True)
    v = jnp.var(x, axis=axis, keepdims=True)
    return (x - m) / jnp.sqrt(v + eps)

def _scatter_add(tgt, idx, src, axis=0):
    return tgt.at[idx].add(src)

def _segment_sum(src, seg, n):
    return jax.ops.segment_sum(src, seg, n)
kernel_name = 'mk_conv_seq_d4_conv_nhwc192_r2_57855a'

def setup_inputs(seed: int=0):
    np.random.seed(seed)
    _w = jnp.asarray

    def _rec_inputs():
        import jax
        import jax.numpy as jnp
        _gk = jax.random.key(seed)
        x = -0.000357 + 1 * jax.random.normal(jax.random.fold_in(_gk, 1), (32, 56, 56, 96), jnp.float32)
        return x
    x = _rec_inputs()

    def _L0_conv_setup():
        import jax, jax.numpy as jnp
        import numpy as np
        from jax import lax
        B, H, W, C = (32, 56, 56, 96)
        EXPAND = 2
        D_INNER = C * EXPAND
        EPS = 1e-05

        def _forward(x, gamma, beta, sel_w1, sel_b1, sel_w2, sel_b2, fc1_w, fc1_b, dw_w, dw_b, fc2_w, fc2_b):
            b, h, w, c = x.shape
            mu = x.mean(-1, keepdims=True)
            var = ((x - mu) ** 2).mean(-1, keepdims=True)
            x_norm = (x - mu) / jnp.sqrt(var + EPS) * gamma + beta
            x_gray = x_norm.mean(-1)
            grad_h = jnp.abs(x_gray[:, :, 1:] - x_gray[:, :, :-1]).mean(axis=(1, 2))
            grad_v = jnp.abs(x_gray[:, 1:, :] - x_gray[:, :-1, :]).mean(axis=(1, 2))
            scores = jnp.stack([grad_h, grad_v, 0.8 * (grad_h + grad_v) * 0.5, jnp.abs(grad_h - grad_v)], axis=1)
            logits = jax.nn.relu(scores @ sel_w1 + sel_b1) @ sel_w2 + sel_b2
            probs = jax.nn.softmax(logits, axis=-1)
            idx = jnp.argmax(probs, axis=-1) % 4
            is_v = (idx == 1)[:, None, None, None]
            x_sel = jnp.where(is_v, jnp.swapaxes(x_norm, 1, 2), x_norm)
            seq = x_sel.reshape(b, h * w, c)
            t = seq @ fc1_w + fc1_b
            t = jnp.swapaxes(t, 1, 2)
            t = lax.conv_general_dilated(t, dw_w, window_strides=(1,), padding=((1, 1),), feature_group_count=D_INNER, dimension_numbers=('NCH', 'OIH', 'NCH')) + dw_b[None, :, None]
            t = jnp.swapaxes(t, 1, 2)
            t = jax.nn.gelu(t, approximate=False)
            out_seq = t @ fc2_w + fc2_b
            out = out_seq.reshape(b, h, w, c)
            return x + out
        key = jax.random.key(seed)
        ks = jax.random.split(key, 12)

        def init(k, shape, fan_in):
            return jax.random.normal(k, shape, dtype=jnp.float32) / np.sqrt(fan_in)
        return {'x': jax.random.normal(ks[0], (B, H, W, C), dtype=jnp.float32), 'gamma': jnp.ones((C,), jnp.float32), 'beta': jnp.zeros((C,), jnp.float32), 'sel_w1': init(ks[1], (4, 16), 4), 'sel_b1': jnp.zeros((16,), jnp.float32), 'sel_w2': init(ks[2], (16, 4), 16), 'sel_b2': jnp.zeros((4,), jnp.float32), 'fc1_w': init(ks[3], (C, D_INNER), C), 'fc1_b': jnp.zeros((D_INNER,), jnp.float32), 'dw_w': init(ks[4], (D_INNER, 1, 3), 3), 'dw_b': jnp.zeros((D_INNER,), jnp.float32), 'fc2_w': init(ks[5], (D_INNER, C), D_INNER), 'fc2_b': jnp.zeros((C,), jnp.float32)}
    _L0_conv_all = _L0_conv_setup()
    _L0_conv_in = {k: v for k, v in _L0_conv_all.items() if k in ('gamma', 'beta', 'sel_w1', 'sel_b1', 'sel_w2', 'sel_b2', 'fc1_w', 'fc1_b', 'dw_w', 'dw_b', 'fc2_w', 'fc2_b')}
    del _L0_conv_all

    def _L1_conv_setup():
        import jax, jax.numpy as jnp
        import numpy as np
        DIM = 96
        HEADS = 6
        WS = 7
        SHIFT = 3
        EPS = 1e-05

        def _ln(x, g, b):
            m = jnp.mean(x, axis=-1, keepdims=True)
            v = jnp.var(x, axis=-1, keepdims=True)
            return (x - m) * jax.lax.rsqrt(v + EPS) * g + b
        key = jax.random.key(seed)
        ks = jax.random.split(key, 8)
        C, Hd = (DIM, DIM * 4)
        s = lambda n: 1.0 / np.sqrt(n)
        return {'x': jax.random.normal(ks[0], (32, 56, 56, C), jnp.float32), 'g1': jnp.ones((C,), jnp.float32), 'b1': jnp.zeros((C,), jnp.float32), 'w_qkv': jax.random.normal(ks[1], (C, 3 * C), jnp.float32) * s(C), 'b_qkv': jnp.zeros((3 * C,), jnp.float32), 'w_proj': jax.random.normal(ks[2], (C, C), jnp.float32) * s(C), 'b_proj': jnp.zeros((C,), jnp.float32), 'g2': jnp.ones((C,), jnp.float32), 'b2': jnp.zeros((C,), jnp.float32), 'w_fc1': jax.random.normal(ks[3], (C, Hd), jnp.float32) * s(C), 'b_fc1': jnp.zeros((Hd,), jnp.float32), 'w_fc2': jax.random.normal(ks[4], (Hd, C), jnp.float32) * s(Hd), 'b_fc2': jnp.zeros((C,), jnp.float32)}
    _L1_conv_all = _L1_conv_setup()
    _L1_conv_in = {k: v for k, v in _L1_conv_all.items() if k in ('g1', 'b1', 'w_qkv', 'b_qkv', 'w_proj', 'b_proj', 'g2', 'b2', 'w_fc1', 'b_fc1', 'w_fc2', 'b_fc2')}
    del _L1_conv_all

    def _L2_conv_setup():
        import jax, jax.numpy as jnp
        import numpy as np
        WS = 7
        SHIFT = 3
        HEADS = 6
        DIM = 96
        B, H, W = (32, 56, 56)
        EPS = 1e-05

        def _rel_pos_index(ws):
            coords = np.stack(np.meshgrid(np.arange(ws), np.arange(ws), indexing='ij'))
            cf = coords.reshape(2, -1)
            rel = cf[:, :, None] - cf[:, None, :]
            rel = rel.transpose(1, 2, 0).astype(np.int64)
            rel[:, :, 0] += ws - 1
            rel[:, :, 1] += ws - 1
            rel[:, :, 0] *= 2 * ws - 1
            return rel.sum(-1)
        REL_IDX = jnp.asarray(_rel_pos_index(WS))

        def _win_partition(x, ws):
            b, h, w, c = x.shape
            x = x.reshape(b, h // ws, ws, w // ws, ws, c)
            return x.transpose(0, 1, 3, 2, 4, 5).reshape(-1, ws * ws, c)

        def _win_reverse(wins, ws, b, h, w):
            c = wins.shape[-1]
            x = wins.reshape(b, h // ws, w // ws, ws, ws, c)
            return x.transpose(0, 1, 3, 2, 4, 5).reshape(b, h, w, c)
        key = jax.random.key(seed)
        ks = jax.random.split(key, 9)
        C = DIM
        return {'x': jax.random.normal(ks[0], (B, H, W, C), jnp.float32), 'mask_matrix': jnp.zeros((H // WS * (W // WS), WS * WS, WS * WS), jnp.float32), 'norm_gamma': jnp.ones((C,), jnp.float32), 'norm_beta': jnp.zeros((C,), jnp.float32), 'qkv_w': jax.random.normal(ks[1], (3 * C, C), jnp.float32) * 0.02, 'qkv_b': jnp.zeros((3 * C,), jnp.float32), 'proj_w': jax.random.normal(ks[2], (C, C), jnp.float32) * 0.02, 'proj_b': jnp.zeros((C,), jnp.float32), 'rpb_table': jax.random.normal(ks[3], ((2 * WS - 1) ** 2, HEADS), jnp.float32) * 0.02, 'dw_w': jax.random.normal(ks[4], (7, 7, 1, C), jnp.float32) * 0.02, 'dw_b': jnp.zeros((C,), jnp.float32)}
    _L2_conv_all = _L2_conv_setup()
    _L2_conv_in = {k: v for k, v in _L2_conv_all.items() if k in ('mask_matrix', 'norm_gamma', 'norm_beta', 'qkv_w', 'qkv_b', 'proj_w', 'proj_b', 'rpb_table', 'dw_w', 'dw_b')}
    del _L2_conv_all

    def _L3_conv_setup():
        import jax, jax.numpy as jnp
        import numpy as np
        WS = 7
        SHIFT = 3
        NH = 6

        def layernorm(x, w, b, eps=1e-05):
            mu = jnp.mean(x, axis=-1, keepdims=True)
            var = jnp.var(x, axis=-1, keepdims=True)
            return (x - mu) * jax.lax.rsqrt(var + eps) * w + b
        key = jax.random.key(seed)
        ks = jax.random.split(key, 8)
        B, H, W, C = (16, 56, 56, 96)
        hid = 4 * C
        s = lambda k, shape, fan: jax.random.normal(k, shape, jnp.float32) * fan ** (-0.5)
        return {'x': jax.random.normal(ks[0], (B, H, W, C), jnp.float32), 'ln1_w': jnp.ones((C,), jnp.float32), 'ln1_b': jnp.zeros((C,), jnp.float32), 'qkv_w': s(ks[1], (C, 3 * C), C), 'qkv_b': jnp.zeros((3 * C,), jnp.float32), 'proj_w': s(ks[2], (C, C), C), 'proj_b': jnp.zeros((C,), jnp.float32), 'ln2_w': jnp.ones((C,), jnp.float32), 'ln2_b': jnp.zeros((C,), jnp.float32), 'mlp_w1': s(ks[3], (C, hid), C), 'mlp_b1': jnp.zeros((hid,), jnp.float32), 'mlp_w2': s(ks[4], (hid, C), hid), 'mlp_b2': jnp.zeros((C,), jnp.float32)}
    _L3_conv_all = _L3_conv_setup()
    _L3_conv_in = {k: v for k, v in _L3_conv_all.items() if k in ('ln1_w', 'ln1_b', 'qkv_w', 'qkv_b', 'proj_w', 'proj_b', 'ln2_w', 'ln2_b', 'mlp_w1', 'mlp_b1', 'mlp_w2', 'mlp_b2')}
    del _L3_conv_all
    return {'x': x, 'L0_conv_gamma': _L0_conv_in['gamma'], 'L0_conv_beta': _L0_conv_in['beta'], 'L0_conv_sel_w1': _L0_conv_in['sel_w1'], 'L0_conv_sel_b1': _L0_conv_in['sel_b1'], 'L0_conv_sel_w2': _L0_conv_in['sel_w2'], 'L0_conv_sel_b2': _L0_conv_in['sel_b2'], 'L0_conv_fc1_w': _L0_conv_in['fc1_w'], 'L0_conv_fc1_b': _L0_conv_in['fc1_b'], 'L0_conv_dw_w': _L0_conv_in['dw_w'], 'L0_conv_dw_b': _L0_conv_in['dw_b'], 'L0_conv_fc2_w': _L0_conv_in['fc2_w'], 'L0_conv_fc2_b': _L0_conv_in['fc2_b'], 'L1_conv_g1': _L1_conv_in['g1'], 'L1_conv_b1': _L1_conv_in['b1'], 'L1_conv_w_qkv': _L1_conv_in['w_qkv'], 'L1_conv_b_qkv': _L1_conv_in['b_qkv'], 'L1_conv_w_proj': _L1_conv_in['w_proj'], 'L1_conv_b_proj': _L1_conv_in['b_proj'], 'L1_conv_g2': _L1_conv_in['g2'], 'L1_conv_b2': _L1_conv_in['b2'], 'L1_conv_w_fc1': _L1_conv_in['w_fc1'], 'L1_conv_b_fc1': _L1_conv_in['b_fc1'], 'L1_conv_w_fc2': _L1_conv_in['w_fc2'], 'L1_conv_b_fc2': _L1_conv_in['b_fc2'], 'L2_conv_mask_matrix': _L2_conv_in['mask_matrix'], 'L2_conv_norm_gamma': _L2_conv_in['norm_gamma'], 'L2_conv_norm_beta': _L2_conv_in['norm_beta'], 'L2_conv_qkv_w': _L2_conv_in['qkv_w'], 'L2_conv_qkv_b': _L2_conv_in['qkv_b'], 'L2_conv_proj_w': _L2_conv_in['proj_w'], 'L2_conv_proj_b': _L2_conv_in['proj_b'], 'L2_conv_rpb_table': _L2_conv_in['rpb_table'], 'L2_conv_dw_w': _L2_conv_in['dw_w'], 'L2_conv_dw_b': _L2_conv_in['dw_b'], 'L3_conv_ln1_w': _L3_conv_in['ln1_w'], 'L3_conv_ln1_b': _L3_conv_in['ln1_b'], 'L3_conv_qkv_w': _L3_conv_in['qkv_w'], 'L3_conv_qkv_b': _L3_conv_in['qkv_b'], 'L3_conv_proj_w': _L3_conv_in['proj_w'], 'L3_conv_proj_b': _L3_conv_in['proj_b'], 'L3_conv_ln2_w': _L3_conv_in['ln2_w'], 'L3_conv_ln2_b': _L3_conv_in['ln2_b'], 'L3_conv_mlp_w1': _L3_conv_in['mlp_w1'], 'L3_conv_mlp_b1': _L3_conv_in['mlp_b1'], 'L3_conv_mlp_w2': _L3_conv_in['mlp_w2'], 'L3_conv_mlp_b2': _L3_conv_in['mlp_b2']}

def reference(x, L0_conv_gamma, L0_conv_beta, L0_conv_sel_w1, L0_conv_sel_b1, L0_conv_sel_w2, L0_conv_sel_b2, L0_conv_fc1_w, L0_conv_fc1_b, L0_conv_dw_w, L0_conv_dw_b, L0_conv_fc2_w, L0_conv_fc2_b, L1_conv_g1, L1_conv_b1, L1_conv_w_qkv, L1_conv_b_qkv, L1_conv_w_proj, L1_conv_b_proj, L1_conv_g2, L1_conv_b2, L1_conv_w_fc1, L1_conv_b_fc1, L1_conv_w_fc2, L1_conv_b_fc2, L2_conv_mask_matrix, L2_conv_norm_gamma, L2_conv_norm_beta, L2_conv_qkv_w, L2_conv_qkv_b, L2_conv_proj_w, L2_conv_proj_b, L2_conv_rpb_table, L2_conv_dw_w, L2_conv_dw_b, L3_conv_ln1_w, L3_conv_ln1_b, L3_conv_qkv_w, L3_conv_qkv_b, L3_conv_proj_w, L3_conv_proj_b, L3_conv_ln2_w, L3_conv_ln2_b, L3_conv_mlp_w1, L3_conv_mlp_b1, L3_conv_mlp_w2, L3_conv_mlp_b2):
    import jax
    import jax.numpy as jnp

    def _L0_conv_ref(x, gamma, beta, sel_w1, sel_b1, sel_w2, sel_b2, fc1_w, fc1_b, dw_w, dw_b, fc2_w, fc2_b):
        import jax, jax.numpy as jnp
        import numpy as np
        from jax import lax
        B, H, W, C = (32, 56, 56, 96)
        EXPAND = 2
        D_INNER = C * EXPAND
        EPS = 1e-05

        def _forward(x, gamma, beta, sel_w1, sel_b1, sel_w2, sel_b2, fc1_w, fc1_b, dw_w, dw_b, fc2_w, fc2_b):
            b, h, w, c = x.shape
            mu = x.mean(-1, keepdims=True)
            var = ((x - mu) ** 2).mean(-1, keepdims=True)
            x_norm = (x - mu) / jnp.sqrt(var + EPS) * gamma + beta
            x_gray = x_norm.mean(-1)
            grad_h = jnp.abs(x_gray[:, :, 1:] - x_gray[:, :, :-1]).mean(axis=(1, 2))
            grad_v = jnp.abs(x_gray[:, 1:, :] - x_gray[:, :-1, :]).mean(axis=(1, 2))
            scores = jnp.stack([grad_h, grad_v, 0.8 * (grad_h + grad_v) * 0.5, jnp.abs(grad_h - grad_v)], axis=1)
            logits = jax.nn.relu(scores @ sel_w1 + sel_b1) @ sel_w2 + sel_b2
            probs = jax.nn.softmax(logits, axis=-1)
            idx = jnp.argmax(probs, axis=-1) % 4
            is_v = (idx == 1)[:, None, None, None]
            x_sel = jnp.where(is_v, jnp.swapaxes(x_norm, 1, 2), x_norm)
            seq = x_sel.reshape(b, h * w, c)
            t = seq @ fc1_w + fc1_b
            t = jnp.swapaxes(t, 1, 2)
            t = lax.conv_general_dilated(t, dw_w, window_strides=(1,), padding=((1, 1),), feature_group_count=D_INNER, dimension_numbers=('NCH', 'OIH', 'NCH')) + dw_b[None, :, None]
            t = jnp.swapaxes(t, 1, 2)
            t = jax.nn.gelu(t, approximate=False)
            out_seq = t @ fc2_w + fc2_b
            out = out_seq.reshape(b, h, w, c)
            return x + out
        return _forward(x, gamma, beta, sel_w1, sel_b1, sel_w2, sel_b2, fc1_w, fc1_b, dw_w, dw_b, fc2_w, fc2_b)

    def _L1_conv_ref(x, g1, b1, w_qkv, b_qkv, w_proj, b_proj, g2, b2, w_fc1, b_fc1, w_fc2, b_fc2):
        import jax, jax.numpy as jnp
        import numpy as np
        DIM = 96
        HEADS = 6
        WS = 7
        SHIFT = 3
        EPS = 1e-05

        def _ln(x, g, b):
            m = jnp.mean(x, axis=-1, keepdims=True)
            v = jnp.var(x, axis=-1, keepdims=True)
            return (x - m) * jax.lax.rsqrt(v + EPS) * g + b
        B, H, W, C = x.shape
        nh, hd = (HEADS, C // HEADS)
        shortcut = x
        h = _ln(x, g1, b1)
        if SHIFT > 0:
            h = jnp.roll(h, shift=(-SHIFT, -SHIFT), axis=(1, 2))
        nHw, nWw = (H // WS, W // WS)
        h = h.reshape(B, nHw, WS, nWw, WS, C).transpose(0, 1, 3, 2, 4, 5)
        h = h.reshape(B * nHw * nWw, WS * WS, C)
        N = WS * WS
        qkv = (h @ w_qkv + b_qkv).reshape(-1, N, 3, nh, hd)
        q, k, v = jnp.moveaxis(qkv, 2, 0)
        scale = hd ** (-0.5)
        attn = jnp.einsum('wqhd,wkhd->whqk', q, k) * scale
        attn = jax.nn.softmax(attn, axis=-1)
        out = jnp.einsum('whqk,wkhd->wqhd', attn, v).reshape(-1, N, C)
        out = out @ w_proj + b_proj
        out = out.reshape(B, nHw, nWw, WS, WS, C).transpose(0, 1, 3, 2, 4, 5)
        out = out.reshape(B, H, W, C)
        if SHIFT > 0:
            out = jnp.roll(out, shift=(SHIFT, SHIFT), axis=(1, 2))
        x = shortcut + out
        h2 = _ln(x, g2, b2)
        mlp = jax.nn.gelu(h2 @ w_fc1 + b_fc1, approximate=False) @ w_fc2 + b_fc2
        return x + mlp

    def _L2_conv_ref(x, mask_matrix, norm_gamma, norm_beta, qkv_w, qkv_b, proj_w, proj_b, rpb_table, dw_w, dw_b):
        import jax, jax.numpy as jnp
        import numpy as np
        WS = 7
        SHIFT = 3
        HEADS = 6
        DIM = 96
        B, H, W = (32, 56, 56)
        EPS = 1e-05

        def _rel_pos_index(ws):
            coords = np.stack(np.meshgrid(np.arange(ws), np.arange(ws), indexing='ij'))
            cf = coords.reshape(2, -1)
            rel = cf[:, :, None] - cf[:, None, :]
            rel = rel.transpose(1, 2, 0).astype(np.int64)
            rel[:, :, 0] += ws - 1
            rel[:, :, 1] += ws - 1
            rel[:, :, 0] *= 2 * ws - 1
            return rel.sum(-1)
        REL_IDX = jnp.asarray(_rel_pos_index(WS))

        def _win_partition(x, ws):
            b, h, w, c = x.shape
            x = x.reshape(b, h // ws, ws, w // ws, ws, c)
            return x.transpose(0, 1, 3, 2, 4, 5).reshape(-1, ws * ws, c)

        def _win_reverse(wins, ws, b, h, w):
            c = wins.shape[-1]
            x = wins.reshape(b, h // ws, w // ws, ws, ws, c)
            return x.transpose(0, 1, 3, 2, 4, 5).reshape(b, h, w, c)
        b, h, w, c = x.shape
        hd = c // HEADS
        scale = hd ** (-0.5)
        N = WS * WS
        shortcut = x
        mu = jnp.mean(x, -1, keepdims=True)
        var = jnp.mean(jnp.square(x - mu), -1, keepdims=True)
        xn = (x - mu) * jax.lax.rsqrt(var + EPS) * norm_gamma + norm_beta
        shifted = jnp.roll(xn, (-SHIFT, -SHIFT), (1, 2))
        dw = jax.lax.conv_general_dilated(shifted, dw_w, (1, 1), 'SAME', dimension_numbers=('NHWC', 'HWIO', 'NHWC'), feature_group_count=c) + dw_b
        dw_windows = _win_partition(dw, WS)
        xw = _win_partition(shifted, WS)
        B_ = xw.shape[0]
        qkv = xw @ qkv_w.T + qkv_b
        qkv = qkv.reshape(B_, N, 3, HEADS, hd).transpose(2, 0, 3, 1, 4)
        q, k, v = (qkv[0], qkv[1], qkv[2])
        attn = jnp.einsum('bhnd,bhmd->bhnm', q * scale, k)
        rpb = rpb_table[REL_IDX.reshape(-1)].reshape(N, N, HEADS).transpose(2, 0, 1)
        attn = attn + rpb[None]
        nW = mask_matrix.shape[0]
        attn = attn.reshape(B_ // nW, nW, HEADS, N, N) + mask_matrix[None, :, None]
        attn = jax.nn.softmax(attn.reshape(B_, HEADS, N, N), axis=-1)
        out = jnp.einsum('bhnm,bhmd->bhnd', attn, v)
        out = out.transpose(0, 2, 1, 3).reshape(B_, N, c)
        out = out + dw_windows
        out = out @ proj_w.T + proj_b
        shifted_out = _win_reverse(out, WS, b, h, w)
        xo = jnp.roll(shifted_out, (SHIFT, SHIFT), (1, 2))
        return shortcut + xo

    def _L3_conv_ref(x, ln1_w, ln1_b, qkv_w, qkv_b, proj_w, proj_b, ln2_w, ln2_b, mlp_w1, mlp_b1, mlp_w2, mlp_b2):
        import jax, jax.numpy as jnp
        import numpy as np
        WS = 7
        SHIFT = 3
        NH = 6

        def layernorm(x, w, b, eps=1e-05):
            mu = jnp.mean(x, axis=-1, keepdims=True)
            var = jnp.var(x, axis=-1, keepdims=True)
            return (x - mu) * jax.lax.rsqrt(var + eps) * w + b
        B, H, W, C = x.shape
        hd = C // NH
        scale = hd ** (-0.5)
        N = WS * WS
        shortcut = x
        xn = layernorm(x, ln1_w, ln1_b)
        xs = jnp.roll(xn, shift=(-SHIFT, -SHIFT), axis=(1, 2))
        xw = xs.reshape(B, H // WS, WS, W // WS, WS, C)
        xw = xw.transpose(0, 1, 3, 2, 4, 5).reshape(-1, N, C)
        qkv = xw @ qkv_w + qkv_b
        qkv = qkv.reshape(-1, N, 3, NH, hd).transpose(2, 0, 3, 1, 4)
        q, k, v = (qkv[0], qkv[1], qkv[2])
        attn = jnp.einsum('bhqd,bhkd->bhqk', q, k) * scale
        attn = jax.nn.softmax(attn, axis=-1)
        o = jnp.einsum('bhqk,bhkd->bhqd', attn, v)
        o = o.transpose(0, 2, 1, 3).reshape(-1, N, C)
        o = o @ proj_w + proj_b
        o = o.reshape(B, H // WS, W // WS, WS, WS, C)
        o = o.transpose(0, 1, 3, 2, 4, 5).reshape(B, H, W, C)
        o = jnp.roll(o, shift=(SHIFT, SHIFT), axis=(1, 2))
        x = shortcut + o
        h = layernorm(x, ln2_w, ln2_b)
        h = jax.nn.gelu(h @ mlp_w1 + mlp_b1, approximate=False)
        x = x + (h @ mlp_w2 + mlp_b2)
        return x

    def _gn(v, G=32, eps=1e-05):
        B_, H_, W_, C_ = v.shape
        g = v.reshape(B_, H_, W_, G, C_ // G)
        m = jnp.mean(g, axis=(1, 2, 4), keepdims=True)
        s = jnp.var(g, axis=(1, 2, 4), keepdims=True)
        return ((g - m) / jnp.sqrt(s + eps)).reshape(v.shape)

    def _ln_c(v, eps=1e-06):
        m = jnp.mean(v, axis=-1, keepdims=True)
        s = jnp.var(v, axis=-1, keepdims=True)
        return (v - m) / jnp.sqrt(s + eps)

    def _ln_t(v, eps=1e-05):
        m = jnp.mean(v, axis=-1, keepdims=True)
        s = jnp.var(v, axis=-1, keepdims=True)
        return (v - m) / jnp.sqrt(s + eps)

    def _to_tokens(v):
        B_, H_, W_, C_ = v.shape
        return v.reshape(B_, H_ * W_, C_)

    def _from_tokens(t, like):
        return t.reshape(like.shape)
    x = _L0_conv_ref(x, L0_conv_gamma, L0_conv_beta, L0_conv_sel_w1, L0_conv_sel_b1, L0_conv_sel_w2, L0_conv_sel_b2, L0_conv_fc1_w, L0_conv_fc1_b, L0_conv_dw_w, L0_conv_dw_b, L0_conv_fc2_w, L0_conv_fc2_b)
    x = _L1_conv_ref(x, L1_conv_g1, L1_conv_b1, L1_conv_w_qkv, L1_conv_b_qkv, L1_conv_w_proj, L1_conv_b_proj, L1_conv_g2, L1_conv_b2, L1_conv_w_fc1, L1_conv_b_fc1, L1_conv_w_fc2, L1_conv_b_fc2)
    x = _L2_conv_ref(x, L2_conv_mask_matrix, L2_conv_norm_gamma, L2_conv_norm_beta, L2_conv_qkv_w, L2_conv_qkv_b, L2_conv_proj_w, L2_conv_proj_b, L2_conv_rpb_table, L2_conv_dw_w, L2_conv_dw_b)
    x = _L3_conv_ref(x, L3_conv_ln1_w, L3_conv_ln1_b, L3_conv_qkv_w, L3_conv_qkv_b, L3_conv_proj_w, L3_conv_proj_b, L3_conv_ln2_w, L3_conv_ln2_b, L3_conv_mlp_w1, L3_conv_mlp_b1, L3_conv_mlp_w2, L3_conv_mlp_b2)
    return x

_drawn_inputs = setup_inputs


def setup_inputs(seed=0):
    import zlib

    import numpy as np

    out = dict(_drawn_inputs(seed))
    spreads = {'L0_conv_gamma': (1.0, 0.2),
     'L0_conv_beta': (0.0, 0.1),
     'L0_conv_sel_b1': (0.0, 0.1),
     'L0_conv_sel_b2': (0.0, 0.1),
     'L0_conv_fc1_b': (0.0, 0.1),
     'L0_conv_dw_b': (0.0, 0.1),
     'L0_conv_fc2_b': (0.0, 0.1),
     'L1_conv_g1': (1.0, 0.2),
     'L1_conv_b1': (0.0, 0.1),
     'L1_conv_b_qkv': (0.0, 0.1),
     'L1_conv_b_proj': (0.0, 0.1),
     'L1_conv_g2': (1.0, 0.2),
     'L1_conv_b2': (0.0, 0.1),
     'L1_conv_b_fc1': (0.0, 0.1),
     'L1_conv_b_fc2': (0.0, 0.1),
     'L2_conv_mask_matrix': (0.0, 0.8),
     'L2_conv_norm_gamma': (1.0, 0.6),
     'L2_conv_norm_beta': (0.0, 0.8),
     'L2_conv_qkv_b': (0.0, 0.454),
     'L2_conv_proj_b': (0.0, 0.1),
     'L2_conv_dw_b': (0.0, 0.615),
     'L3_conv_ln1_w': (1.0, 0.2),
     'L3_conv_ln1_b': (0.0, 0.1),
     'L3_conv_qkv_b': (0.0, 0.1),
     'L3_conv_proj_b': (0.0, 0.1),
     'L3_conv_ln2_w': (1.0, 0.2),
     'L3_conv_ln2_b': (0.0, 0.1),
     'L3_conv_mlp_b1': (0.0, 0.1),
     'L3_conv_mlp_b2': (0.0, 0.1)}
    factors = {'L2_conv_qkv_w': 5.233, 'L2_conv_rpb_table': 64.0, 'L2_conv_dw_w': 3.509}
    for name, (base, spread) in spreads.items():
        noise = np.random.default_rng([zlib.crc32(name.encode()), seed]).standard_normal(out[name].shape)
        drawn = base * np.exp(spread * noise) if base else spread * noise
        out[name] = jnp.asarray(drawn.astype(out[name].dtype))
    for name, factor in factors.items():
        out[name] = (out[name] * factor).astype(out[name].dtype)
    return out
```

```python
from contextlib import ExitStack, contextmanager

import numpy as np

import concourse.bass as bass
from concourse import mybir

F32 = mybir.dt.float32
ALU = mybir.AluOpType
ACT = mybir.ActivationFunctionType
AX = mybir.AxisListType

B, H, W, C = 32, 56, 56, 96
WS, SHIFT, HEADS = 7, 3, 6
HD = C // HEADS
TOK = WS * WS
NWIN = W // WS
NROW = H // WS
CH = WS * W
PAIRS = NWIN // 2
G = HEADS // 2
HALF = 64
SPAN = HALF + TOK
HID = 4 * C
HB = HID // 128
VW = 2 * HD + 2
EPS = 1e-5
PW = W + 6

def hold(eng, sem, value, passed):
    eng.wait_ge(sem, value)
    eng.sem_inc(passed, 1)


@contextmanager
def semaphores(nc, prefix):
    given = []
    with ExitStack() as ctx:
        def sem(name):
            given.append(ctx.enter_context(nc.semaphore(f"{prefix}_{name}")))
            return given[-1]

        yield sem
        with nc.Block() as block:
            @block.gpsimd
            def _(pool):
                for q in given:
                    pool.sem_clear(q)


def fold_affine(nc, name, raw, bias_row, gamma, beta, ps, pieces):
    n = raw.shape[1]
    with semaphores(nc, name) as sem:
        product_ready = sem("product_ready")
        with nc.Block() as block:
            if beta is not None:
                @block.tensor
                def _(pe):
                    pe.matmul(ps[C:C + 1, 0:n], beta, raw, start=True, stop=True).then_inc(product_ready, 1)

            @block.vector
            def _(dve):
                for target, view in pieces:
                    if gamma is not None:
                        dve.tensor_scalar(target[0:C], view(raw), gamma, None, ALU.mult)
                    else:
                        dve.tensor_copy(target[0:C], view(raw))
                if beta is not None:
                    dve.wait_ge(product_ready, 1)
                for target, view in pieces:
                    if beta is not None:
                        dve.tensor_tensor(target[C:C + 1], view(bias_row), view(ps[C:C + 1, 0:n]), ALU.add)
                    else:
                        dve.tensor_copy(target[C:C + 1], view(bias_row))


def load_all(nc, name, pairs, zeros=(), ones=(), values=()):
    with semaphores(nc, name) as sem:
        weights_loaded = sem("weights_loaded")
        with nc.Block() as block:
            @block.sync
            def _(sp):
                for dst, src in pairs:
                    sp.dma_start(dst, src).then_inc(weights_loaded, 16)
                sp.wait_ge(weights_loaded, 16 * len(pairs))

            @block.vector
            def _(dve):
                for t in zeros:
                    dve.memset(t, 0.0)
                for t in ones:
                    dve.memset(t, 1.0)
                for t, v in values:
                    dve.memset(t, v)


def column(v):
    return v.rearrange("(c o) -> c o", o=1)


def row(v):
    return v.rearrange("(o c) -> o c", o=1)


def scan_pass(nc, PS, w, x, xa, store_sems):
    RB = 8
    TB = RB * W
    NB = H // RB
    S = H * W
    TP = S // 112
    with ExitStack() as ctx:
        sb = lambda name, shape: ctx.enter_context(nc.sbuf_tensor("scan_" + name, shape, F32))
        sem = ctx.enter_context(semaphores(nc, "scan"))
        raw = sb("raw", [C, 2 * C]); brow = sb("brow", [128, 2 * C])
        gcol = sb("gcol", [C, 1]); becol = sb("becol", [C, 1]); fc2b = sb("fc2b", [C, 1])
        dwb = sb("dwb", [C, 2]); taps = sb("taps", [128, 3, 2 * C])
        W1 = sb("W1", [128, 2 * C]); W1T = sb("W1T", [128, 3, 2 * C])
        W2 = sb("W2", [C, 2, C]); J = sb("J", [C, C]); ident = sb("ident", [128, 128])
        grey = sb("grey", [128, 1]); eps = sb("eps", [C, 1]); ones = sb("ones", [C, 1])
        sw1 = sb("sw1", [4, 16]); sb1 = sb("sb1", [16, 1]); sw2 = sb("sw2", [16, 4]); sb2 = sb("sb2", [1, 4])
        XT = sb("XT", [112, TP, C])
        X = sb("X", [C, S]); XN = sb("XN", [C + 1, S]); XS = sb("XS", [C + 1, S + 2])
        XC = sb("XC", [C, 2, TB]); SQ = sb("SQ", [C, 2, TB]); LV = sb("LV", [C, 2, TB]); RS = sb("RS", [C, 2, TB])
        GR = sb("GR", [1, S]); GH = sb("GH", [H, W]); GN = sb("GN", [H, W])
        DH = sb("DH", [H, W]); DV = sb("DV", [H, W]); JH = sb("JH", [H, W]); JV = sb("JV", [H, W]); GA = sb("GA", [H, 4])
        gone = sb("gone", [H, 1])
        sc = sb("sc", [4, 1]); hid = sb("hid", [16, 1]); lg = sb("lg", [1, 4]); st = sb("st", [1, 16])
        pr = sb("pr", [1, 4]); fl = sb("fl", [1, 2]); fb = sb("fb", [C, 2]); one1 = sb("one1", [1, C])
        Hd = sb("Hd", [C, 2, 2, TB]); OUT = sb("OUT", [C, 2, RB, W])

        load_all(nc, "scan", [
            (raw[:], w["L0_conv_fc1_w"]), (brow[C:C + 1, :], row(w["L0_conv_fc1_b"])),
            (gcol[:], column(w["L0_conv_gamma"])), (becol[:], column(w["L0_conv_beta"])),
            (fc2b[:], column(w["L0_conv_fc2_b"])), (dwb[:, 0:1], column(w["L0_conv_dw_b"][0:C])), (dwb[:, 1:2], column(w["L0_conv_dw_b"][C:2 * C])),
            (W2[:], w["L0_conv_fc2_w"].rearrange("(h c) n -> c h n", h=2)), (ident[:], w["ident"]),
            (sw1[:], w["L0_conv_sel_w1"]), (sb1[:], column(w["L0_conv_sel_b1"])),
            (sw2[:], w["L0_conv_sel_w2"]), (sb2[:], row(w["L0_conv_sel_b2"]))]
            + [(taps[0:C + 1, t, :], w["dw_taps"][t:t + 1, :].broadcast_to([C + 1, 2 * C])) for t in range(3)],
            zeros=[XS[:], GA[:]], ones=[XN[C:C + 1, :], PS[:], ones[:], one1[:]],
            values=[(J[:], 1.0 / C), (eps[:], EPS), (gone[:], 1.0 / (H * (W - 1)))])
        fold_affine(nc, "scan_fc1", raw[:], brow[C:C + 1, :], gcol[:, 0:1], becol[:, 0:1], PS[:, 0, :],
                    [(W1[0:C + 1, :], lambda t: t)])
        grey_bias = sem("grey_bias")
        with nc.Block() as block:
            @block.tensor
            def _(pe):
                pe.matmul(PS[C:C + 1, 1, 0:1], becol[:, 0:1], ones[:, 0:1], start=True, stop=True).then_inc(grey_bias, 1)

            @block.vector
            def _(dve):
                for t in range(3):
                    dve.tensor_tensor(W1T[0:C + 1, t, :], W1[0:C + 1, :], taps[0:C + 1, t, :], ALU.mult)
                dve.tensor_scalar(grey[0:C], gcol[:], 1.0 / C, None, ALU.mult)
                dve.wait_ge(grey_bias, 1)
                dve.tensor_scalar(grey[C:C + 1], PS[C:C + 1, 1, 0:1], 1.0 / C, None, ALU.mult)

        s = {n: sem(n) for n in ("img_loaded", "turned", "x_ready", "mean", "xc", "sq", "var", "lv", "rstd",
                                 "xn", "greyp", "grey_row", "grey_tiles", "diffs", "sums", "sums_ready", "score",
                                 "scores", "sel1", "hidden", "sel2", "dve_chain", "centred", "expo", "flag",
                                 "flagb", "flag_ready", "blend", "xs", "conv0", "conv1", "gelu", "fc2", "out", "last_xn", "out_free")}
        stored, passed = store_sems[0], sem("passed")
        CHAIN = 8
        XTr = x.rearrange("b h w c -> b (h w) c").rearrange("b (p j) c -> b p j c", j=TP)
        def grey_block(pe, m0, m):
            pe.wait_ge(s["xn"], m0 + (m + 1))
            pe.matmul(PS[0:1, 4 + m % 2, 0:TB], grey[0:C + 1, :], XN[:, m * TB:(m + 1) * TB],
                      start=True, stop=True).then_inc(s["greyp"], 1)

        def fc2_block(pe, m0, m):
            v = m % 2
            pe.wait_ge(s["gelu"], m0 * 2 + 2 * (m + 1))
            if m >= 2:
                pe.wait_ge(s["out"], m0 * 2 + (2 * (m - 1) + 2))
            for h in range(2):
                mm = pe.matmul(PS[0:C, 6 + v, 0:TB], W2[:, h, :], Hd[:, v, h], start=(h == 0), stop=(h == 1))
            mm.then_inc(s["fc2"], 1)

        with nc.Block() as block:
            @block.sync
            def _(sp):
                with sp.Fori(0, B) as b:
                    b1 = sp.snap(b + 1)
                    sp.wait_ge(s["turned"], b1 * NB - (NB - 1))
                    sp.dma_start(XT[:], XTr[b]).then_inc(s["img_loaded"], 16)
                    sp.wait_ge(s["grey_row"], b1 * NB)
                    sp.dma_start(GH[:], GR[0:1, :].rearrange("o (h w) -> o h w", w=W)).then_inc(s["grey_tiles"], 16)
                    sp.dma_start(GN[0:H - 1, :], GR[0:1, W:].rearrange("o (h w) -> o h w", w=W)).then_inc(s["grey_tiles"], 16)

            @block.tensor
            def _(pe):
                pe.sem_inc(s["turned"], 1)
                with pe.Fori(0, B) as b:
                    m0 = pe.snap(b * NB)
                    b1 = pe.snap(b + 1)
                    pe.wait_ge(s["img_loaded"], b1 * 16)
                    for m in range(NB):
                        if m >= 2:
                            pe.wait_ge(s["x_ready"], m0 + (m - 1))
                        else:
                            pe.wait_ge(s["out"], m0 * 2 + (2 if m == 0 else 2))
                        for j in range(4):
                            mm = pe.transpose(PS[0:C, m % 2, j * 112:(j + 1) * 112], XT[:, 4 * m + j, :], ident[0:112, 0:112])
                        mm.then_inc(s["turned"], 1)
                    for m in range(NB):
                        if m == 0:
                            pe.wait_ge(s["x_ready"], m0 + NB)
                        else:
                            pass
                        v = m % 2
                        if m >= 2:
                            pe.wait_ge(s["grey_row"], m0 + (m - 1))
                        pe.matmul(PS[0:C, 2 + v, 0:TB], J[:], X[:, m * TB:(m + 1) * TB], start=True, stop=True).then_inc(s["mean"], 1)
                        pe.wait_ge(s["sq"], m0 + (m + 1))
                        pe.matmul(PS[0:C, 2 + v, 0:TB], J[:], SQ[:, v], start=True, stop=True).then_inc(s["var"], 1)
                        if m >= 1:
                            grey_block(pe, m0, m - 1)
                    grey_block(pe, m0, NB - 1)
                    hold(pe, s["sums"], b1, passed)
                    pe.matmul(PS[0:4, 0, 0:1], GA[:], gone[:], start=True, stop=True).then_inc(s["score"], 1)
                    hold(pe, s["scores"], b1, passed)
                    pe.matmul(PS[0:16, 1, 0:1], sw1[:], sc[:], start=True, stop=True).then_inc(s["sel1"], 1)
                    hold(pe, s["hidden"], b1, passed)
                    pe.matmul(PS[0:1, 0, 0:4], hid[:], sw2[:], start=True, stop=True).then_inc(s["sel2"], 1)
                    hold(pe, s["flag"], b1, passed)
                    pe.matmul(PS[0:C, 1, 0:2], one1[:], fl[:], start=True, stop=True).then_inc(s["flagb"], 1)
                    for m in range(NB):
                        v = m % 2
                        pe.wait_ge(s["xs"], m0 + min(m + 2, NB))
                        if m >= 2:
                            pe.wait_ge(s["gelu"], m0 * 2 + 2 * (m - 1))
                        for h in range(2):
                            for t in range(3):
                                mm = pe.matmul(PS[0:C, 2 + 2 * v + h, 0:TB], W1T[0:C + 1, t, h * C:(h + 1) * C],
                                               XS[:, m * TB + t:m * TB + t + TB], start=(t == 0), stop=(t == 2))
                            mm.then_inc(s["conv0"], 1)
                        if m >= 1:
                            fc2_block(pe, m0, m - 1)
                    fc2_block(pe, m0, NB - 1)

            @block.scalar
            def _(act):
                with act.Fori(0, B) as b:
                    m0 = act.snap(b * NB)
                    b1 = act.snap(b + 1)
                    for m in range(NB):
                        v = m % 2
                        act.wait_ge(s["xc"], m0 + (m + 1))
                        act.activation(SQ[:, v], XC[:, v], ACT.Square).then_inc(s["sq"], 1)
                        act.wait_ge(s["var"], m0 + (m + 1))
                        act.activation(LV[:, v], PS[0:C, 2 + v, 0:TB], ACT.Ln, bias=eps[:, 0:1]).then_inc(s["lv"], 1)
                        act.wait_ge(s["lv"], m0 + (m + 1))
                        act.activation(RS[:, v], LV[:, v], ACT.Exp, scale=-0.5).then_inc(s["rstd"], 1)
                        if m >= 1:
                            act.wait_ge(s["greyp"], m0 + m)
                            act.copy(GR[0:1, (m - 1) * TB:m * TB], PS[0:1, 4 + (m - 1) % 2, 0:TB]).then_inc(s["grey_row"], 1)
                    act.wait_ge(s["greyp"], m0 + NB)
                    act.copy(GR[0:1, (NB - 1) * TB:], PS[0:1, 4 + (NB - 1) % 2, 0:TB]).then_inc(s["grey_row"], 1)
                    act.wait_ge(s["diffs"], b1 * 2)
                    act.activation(JH[:, 0:W - 1], DH[:, 0:W - 1], ACT.Abs, accum_out=GA[:, 0:1])
                    act.activation(JV[0:H - 1, :], DV[0:H - 1, :], ACT.Abs, accum_out=GA[0:H - 1, 1:2]).then_inc(s["sums_ready"], 1)
                    act.wait_ge(s["score"], b1)
                    act.activation(sc[:], PS[0:4, 0, 0:1], ACT.Abs).then_inc(s["scores"], 1)
                    act.wait_ge(s["sel1"], b1)
                    act.activation(hid[:], PS[0:16, 1, 0:1], ACT.Relu, bias=sb1[:, 0:1]).then_inc(s["hidden"], 1)
                    act.wait_ge(s["centred"], b1)
                    act.activation(pr[:], lg[:], ACT.Exp).then_inc(s["expo"], 1)
                    for m in range(NB):
                        v = m % 2
                        for h in range(2):
                            act.wait_ge(s["conv0"], m0 * 2 + (2 * m + h + 1))
                            if m >= 2 and h == 0:
                                act.wait_ge(s["fc2"], m0 + (m - 1))
                            act.activation(Hd[:, v, h], PS[0:C, 2 + 2 * v + h, 0:TB], ACT.Gelu, bias=dwb[:, h:h + 1]).then_inc(s["gelu"], 1)

            @block.vector
            def _(dve):
                dve.sem_inc(s["out"], 2)
                dve.sem_inc(s["out_free"], 2)
                with dve.Fori(0, B) as b:
                    m0 = dve.snap(b * NB)
                    b1 = dve.snap(b + 1)
                    k0 = dve.snap(b * CHAIN)
                    k = [0]

                    def link(ins):
                        k[0] += 1
                        ins.then_inc(s["dve_chain"], 1)
                        dve.wait_ge(s["dve_chain"], k0 + k[0])

                    Xv = X[:].rearrange("c (p j) -> c j p", j=TP)
                    for m in range(NB):
                        dve.wait_ge(s["turned"], m0 + (m + 2))
                        dve.tensor_copy(Xv[:, 4 * m:4 * m + 4, :],
                                        PS[0:C, m % 2, 0:TB].rearrange("c (j p) -> c j p", j=4)).then_inc(s["x_ready"], 1)
                    dve.wait_ge(s["x_ready"], m0 + NB)
                    for m in range(NB):
                        v = m % 2
                        cols = slice(m * TB, (m + 1) * TB)
                        dve.wait_ge(s["mean"], m0 + (m + 1))
                        dve.tensor_tensor(XC[:, v], X[:, cols], PS[0:C, 2 + v, 0:TB], ALU.subtract).then_inc(s["xc"], 1)
                        dve.wait_ge(s["rstd"], m0 + (m + 1))
                        dve.tensor_tensor(XN[0:C, cols], XC[:, v], RS[:, v], ALU.mult).then_inc(s["xn"], 1)
                    dve.wait_ge(s["grey_tiles"], b1 * 32)
                    dve.tensor_tensor(DH[:, 0:W - 1], GH[:, 1:W], GH[:, 0:W - 1], ALU.subtract).then_inc(s["diffs"], 1)
                    dve.tensor_tensor(DV[0:H - 1, :], GN[0:H - 1, :], GH[0:H - 1, :], ALU.subtract).then_inc(s["diffs"], 1)
                    dve.wait_ge(s["sums_ready"], b1)
                    link(dve.tensor_tensor(GA[:, 2:3], GA[:, 0:1], GA[:, 1:2], ALU.add))
                    dve.tensor_scalar(GA[:, 2:3], GA[:, 2:3], 0.8, 0.5, ALU.mult, ALU.mult)
                    dve.tensor_tensor(GA[:, 3:4], GA[:, 0:1], GA[:, 1:2], ALU.subtract).then_inc(s["sums"], 1)
                    dve.wait_ge(s["sel2"], b1)
                    link(dve.tensor_tensor(st[:, 0:4], PS[0:1, 0, 0:4], sb2[:], ALU.add))
                    link(dve.tensor_reduce(st[:, 4:5], st[:, 0:4], AX.X, ALU.max))
                    dve.tensor_scalar(lg[:], st[:, 0:4], st[:, 4:5], None, ALU.subtract).then_inc(s["centred"], 1)
                    dve.wait_ge(s["expo"], b1)
                    link(dve.tensor_reduce(st[:, 5:6], pr[:], AX.X, ALU.add))
                    link(dve.reciprocal(st[:, 6:7], st[:, 5:6]))
                    link(dve.tensor_scalar(st[:, 8:12], pr[:], st[:, 6:7], None, ALU.mult))
                    dve.tensor_tensor(st[:, 12:13], st[:, 9:10], st[:, 8:9], ALU.is_gt)
                    link(dve.tensor_tensor(st[:, 13:14], st[:, 10:11], st[:, 11:12], ALU.max))
                    link(dve.tensor_tensor(st[:, 14:15], st[:, 9:10], st[:, 13:14], ALU.is_ge))
                    dve.tensor_tensor(fl[:, 0:1], st[:, 12:13], st[:, 14:15], ALU.mult).then_inc(s["flag_ready"], 1)
                    dve.wait_ge(s["flag_ready"], b1)
                    dve.tensor_scalar(fl[:, 1:2], fl[:, 0:1], -1.0, 1.0, ALU.mult, ALU.add).then_inc(s["flag"], 1)
                    dve.wait_ge(s["flagb"], b1)
                    dve.tensor_copy(fb[:], PS[0:C, 1, 0:2]).then_inc(s["last_xn"], 1)
                    dve.wait_ge(s["last_xn"], b1)
                    XNT = XN[0:C, :].rearrange("c (h w) -> c w h", w=W)
                    for m in range(NB + 1):
                        if m < NB:
                            cols = slice(1 + m * TB, 1 + (m + 1) * TB)
                            dve.tensor_scalar(XS[0:C, cols], XN[0:C, m * TB:(m + 1) * TB], fb[:, 1:2], None, ALU.mult).then_inc(s["blend"], 1)
                            if m == 0:
                                dve.memset(XS[C:C + 1, 1:S + 1], 1.0)
                            dve.wait_ge(s["blend"], m0 + (m + 1))
                            dve.scalar_tensor_tensor(XS[0:C, cols].rearrange("c (a q) -> c a q", q=H), XNT[:, m * RB:(m + 1) * RB, :], fb[:, 0:1],
                                                     XS[0:C, cols].rearrange("c (a q) -> c a q", q=H), ALU.mult, ALU.add).then_inc(s["xs"], 1)
                    for m in range(NB):
                        v = m % 2
                        i0 = m * TB
                        dve.wait_ge(s["fc2"], m0 + (m + 1))
                        dve.wait_ge(s["out_free"], m0 + (m + 1 if m else 2))
                        Xr = X[:, i0:i0 + TB].rearrange("c (a q) -> c a q", q=W)
                        Pr = PS[0:C, 6 + v, 0:TB].rearrange("c (a q) -> c a q", q=W)
                        for dst, src in ((slice(0, W - SHIFT), slice(SHIFT, W)), (slice(W - SHIFT, W), slice(0, SHIFT))):
                            dve.scalar_tensor_tensor(OUT[:, v, :, dst], Pr[:, :, src], fc2b[:, 0:1], Xr[:, :, src],
                                                     ALU.add, ALU.add).then_inc(s["out"], 1)

            @block.gpsimd
            def _(pool):
                with pool.Fori(0, B) as b:
                    m0 = pool.snap(b * NB)
                    for m in range(NB):
                        v = m % 2
                        pool.wait_ge(s["out"], m0 * 2 + (2 * (m + 1) + 2))
                        if m == 0:
                            pool.dma_start(xa[b, :, H - SHIFT:H, :], OUT[:, v, 0:SHIFT, :]).then_inc(stored, 16)
                            pool.dma_start(xa[b, :, 0:RB - SHIFT, :], OUT[:, v, SHIFT:RB, :]).then_inc(stored, 16)
                        else:
                            pool.dma_start(xa[b, :, m * RB - SHIFT:(m + 1) * RB - SHIFT, :], OUT[:, v]).then_inc(stored, 16)
                        pool.wait_ge(stored, b * (16 * (NB + 1)) + 16 * (m + 2))
                        pool.sem_inc(s["out_free"], 1)


def window_pass(nc, PS, w, kind, p, xin, xout, store_sems, xn_io=None, conv=None):
    mlp = kind != "L2"
    N_OUT, N_IN = (B, NROW // 2) if mlp else (NROW, B // 2)
    with ExitStack() as ctx:
        sb = lambda name, shape: ctx.enter_context(nc.sbuf_tensor(f"{kind}_{name}", shape, F32))
        sem = ctx.enter_context(semaphores(nc, kind))
        ident = sb("ident", [128, 128]); mask6 = sb("mask6", [C, HEADS]); J = sb("J", [C, C]); eps = sb("eps", [C, 1])
        rawq = sb("rawq", [C, 3 * C]); brow = sb("brow", [128, HID])
        Wq = sb("Wq", [128, C]); Wk = sb("Wk", [128, C]); Wv = sb("Wv", [128, 2, G, HD]); Wp = sb("Wp", [128, C])
        rawp = sb("rawp", [C, C]); prow = sb("prow", [128, C])
        gb = sb("gb", [C, 8])
        X = sb("X", [C, 2, CH]); XN = sb("XN", [C + 1, 2, CH]); QT = sb("QT", [C, 2, CH]); KT = sb("KT", [C, 2, CH])
        KX = sb("KX", [C, 2, HEADS, CH]); VB = sb("VB", [SPAN, 2, NWIN, G, VW])
        MX = sb("MX", [SPAN, 2, PAIRS * HEADS]); SX = sb("SX", [SPAN, 2, PAIRS * HEADS, TOK])
        PR = sb("PR", [SPAN, 2, PAIRS * HEADS, HALF]); PT = sb("PT", [SPAN, 2, PAIRS * G, SPAN])
        RSUM = sb("RSUM", [SPAN, 2, PAIRS * G, 2]); O = sb("O", [SPAN, 2, PAIRS, C]); OT = sb("OT", [C + 1, 2, CH])
        X1 = sb("X1", [C, 2, CH])
        if mlp:
            raw1 = sb("raw1", [C, HID]); W1 = sb("W1", [128, HID]); W2 = sb("W2", [128, HB, C])
            XC = sb("XC", [C, 2, CH]); SQ = sb("SQ", [C, 2, CH]); LV = sb("LV", [C, 2, CH]); RS = sb("RS", [C, 2, CH])
            XN2 = sb("XN2", [C + 1, 2, CH]); Hd = sb("Hd", [128, 2, HB, CH]); X2 = sb("X2", [C, 2, CH])
        if kind == "L1":
            XH = sb("XH", [C, 2, CH]); XA = sb("XA", [C, 2, CH]); XC3 = sb("XC3", [C, 2, CH])
        if kind == "L2":
            XR = sb("XR", [C, 2, CH]); DW = sb("DW", [C, 2, CH])
            RPB = sb("RPB", [SPAN, HEADS, TOK]); MSK = sb("MSK", [SPAN, PAIRS, TOK]); BIAS = sb("BIAS", [SPAN, PAIRS, HEADS, TOK])
            SR = sb("SR", [SPAN, 2, PAIRS * HEADS, TOK])
        if kind == "L3":
            Y = sb("Y", [W, 2, WS, C])

        pad_ones = [XN[C:C + 1], OT[C:C + 1], VB[0:HALF, :, :, :, 2 * HD], VB[HALF:SPAN, :, :, :, 2 * HD + 1]]
        loads = [(ident[:], w["ident"]), (mask6[:], w["head_mask"]), (rawq[:], p["qkv_w"]), (brow[C:C + 1, 0:3 * C], row(p["qkv_b"])),
                 (rawp[:], p["proj_w"]), (prow[C:C + 1, :], row(p["proj_b"]))]
        if mlp:
            pad_ones += [XN2[C:C + 1]]
            loads += [(gb[:, i:i + 1], column(p[n])) for i, n in enumerate(("g1", "b1", "g2", "b2", "fc2_b"))]
            loads += [(raw1[:], p["fc1_w"]), (W2[:], p["fc2_w"].rearrange("(j h) n -> h j n", j=HB))]
        if kind == "L1":
            loads += [(gb[:, 5:6], column(w["L2_conv_norm_gamma"])), (gb[:, 6:7], column(w["L2_conv_norm_beta"]))]
        if kind == "L2":
            loads += [(gb[:, 0:1], column(p["dw_b"]))]
        load_all(nc, kind, loads, zeros=[VB[:], PR[:]] + ([RPB[:], MSK[:]] if kind == "L2" else []), values=[(J[:], 1.0 / C), (eps[:], EPS)])
        with nc.Block() as block:
            @block.vector
            def _(dve):
                for t in pad_ones:
                    dve.memset(t, 1.0)
        if kind == "L2":
            load_all(nc, "L2b", [(RPB[HALF * i:HALF * i + TOK], p["rpb"]) for i in range(2)])
        third = lambda i: (lambda t: t[:, i * C:(i + 1) * C])
        vhalf = lambda par: (lambda t: t[:, 2 * C:3 * C].rearrange("c (g q d) -> c q g d", g=G, q=2)[:, par])
        fold_affine(nc, kind + "_qkv", rawq[:], brow[C:C + 1, 0:3 * C], gb[:, 0:1] if mlp else None, gb[:, 1:2] if mlp else None,
                    PS[:, 0, :], [(Wq[0:C + 1], third(0)), (Wk[0:C + 1], third(1)), (Wv[0:C + 1, 0], vhalf(0)), (Wv[0:C + 1, 1], vhalf(1))])
        fold_affine(nc, kind + "_proj", rawp[:], prow[C:C + 1, :], None, gb[:, 0:1] if kind == "L2" else None,
                    PS[:, 1, :], [(Wp[0:C + 1], lambda t: t)])
        if mlp:
            load_all(nc, kind + "c", [(brow[C:C + 1, 0:HID], row(p["fc1_b"]))])
            fold_affine(nc, kind + "_fc1", raw1[:], brow[C:C + 1, :], gb[:, 2:3], gb[:, 3:4], PS[:, 2, :], [(W1[0:C + 1, :], lambda t: t)])

        names = ["mean", "xc", "sq", "var", "lv", "rstd", "xn", "q", "k", "v", "qt", "kt", "kx", "v_even", "v_odd",
                 "scores", "biased", "rowmax", "centred", "probs", "turned", "pt_dve", "pt_act", "heads", "rsum", "normed",
                 "heads_t", "ot", "proj", "x1", "tail_read", "bias_ready", "out_free"]
        if mlp:
            names += ["mean2", "xc2", "sq2", "var2", "lv2", "rstd2", "xn2", "fc2", "x2"]
            names += [f"fc1_{j}" for j in range(HB)] + [f"gelu_{j}" for j in range(HB)]
        if kind == "L1":
            names += ["mean3", "xc3", "sq3", "var3", "lv3", "rstd3", "xh", "xa"]
        if kind == "L3":
            names += ["yt"]
        s = {n: sem(n) for n in names}
        loaded = [sem(f"loaded{u}") for u in range(2)]
        stored = store_sems
        mask_loaded, passed = sem("mask_loaded"), sem("passed")
        bank = lambda u, k: PS[:, 4 * u + k, :]
        N_LOADS = 1 if mlp else 3
        N_STORES = {"L1": 2, "L2": 1, "L3": 4}[kind]

        def rows_of(t, b, r):
            return t[b, :, bass.ds(r * WS, WS), :]

        def where(o, i, u):
            return (o, i * 2 + u) if mlp else (i * 2 + u, o)

        class Turn:
            def __init__(self, eng, o, i):
                self.eng = eng
                first = o * (2 * N_IN) + i * 2
                self.v = [eng.snap(first + (u + 1)) for u in range(2)]
                self.credited = [eng.snap(first + (u + 3)) for u in range(2)]
                self.turns = eng.snap(o * N_IN + i + 1)

            def wait(self, name, u):
                self.eng.wait_ge(s[name], self.v[u])

            def wait_credited(self, name, u):
                self.eng.wait_ge(s[name], self.credited[u])

        def win(t):
            return t.rearrange("c (i q j) -> c q i j", i=WS, j=WS)

        def seen(t):
            return t.rearrange("c (q i j) -> c q i j", i=WS, j=WS)

        def window_columns(bk):
            v = bk[0:C, 0:PAIRS * SPAN].rearrange("c (k m) -> c k m", m=SPAN)
            return bass.AP(v.tensor, v.offset, [v.ap[0], [SPAN, PAIRS], [HALF, 2], [1, TOK]])

        def odd_windows(bk, e):
            v = bk[0:C, 0:PAIRS * SPAN]
            return bass.AP(v.tensor, v.offset + e * HALF, [v.ap[0], [SPAN, PAIRS], [WS, WS], [1, WS]])

        with nc.Block() as block:
            @block.sync
            def _(sp):
                with sp.Fori(0, N_OUT) as o:
                    if kind == "L2":
                        sp.wait_ge(s["bias_ready"], o + 1)
                        for par in range(2):
                            sp.dma_start(MSK[HALF * par:HALF * par + TOK], p["mask"][o, par]).then_inc(mask_loaded, 16)
                    with sp.Fori(0, N_IN) as i:
                        t = Turn(sp, o, i)
                        for u in range(2):
                            b, r = where(o, i, u)
                            t.wait("x1", u)
                            sp.dma_start(X[:, u], rows_of(xin, b, r)).then_inc(loaded[u], 16)
                            if kind == "L2":
                                sp.dma_start(XR[:, u], rows_of(xn_io, b, r)).then_inc(loaded[u], 16)
                                sp.dma_start(DW[:, u], rows_of(conv, b, r)).then_inc(loaded[u], 16)

            @block.tensor
            def _(pe):
                with pe.Fori(0, N_OUT) as o:
                    with pe.Fori(0, N_IN) as i:
                        t = Turn(pe, o, i)

                        def mean_of(src, k, u, done):
                            pe.matmul(bank(u, k)[0:C, 0:CH], J[:], src, start=True, stop=True).then_inc(s[done], 1)

                        if mlp:
                            for u in range(2):
                                pe.wait_ge(loaded[u], t.turns * 16)
                                t.wait("tail_read", u)
                                mean_of(X[:, u], 0, u, "mean")
                            for u in range(2):
                                t.wait("sq", u)
                                mean_of(SQ[:, u], 0, u, "var")
                        for u in range(2):
                            t.wait("xn", u)
                            if not mlp:
                                t.wait("tail_read", u)
                            pe.matmul(bank(u, 1)[0:C, 0:CH], Wk[0:C + 1, :], XN[:, u], start=True, stop=True).then_inc(s["k"], 1)
                            pe.matmul(bank(u, 0)[0:C, 0:CH], Wq[0:C + 1, :], XN[:, u], start=True, stop=True).then_inc(s["q"], 1)
                            for q in range(NWIN):
                                for par in range(2):
                                    mm = pe.matmul(bank(u, 2)[HALF * par:HALF * par + TOK, q * G * HD:(q + 1) * G * HD],
                                                   XN[:, u, q * TOK:(q + 1) * TOK], Wv[0:C + 1, par].rearrange("c g d -> c (g d)"),
                                                   start=True, stop=True)
                            mm.then_inc(s["v"], 1)
                        for u in range(2):
                            for name in ("qt", "kx", "v_even", "v_odd"):
                                t.wait(name, u)
                            for q in range(NWIN):
                                p0 = HALF * (q % 2)
                                mm = pe.matmul(bank(u, q // 2)[p0:p0 + TOK, 0:HEADS * TOK].rearrange("c (h k) -> c h k", h=HEADS),
                                               QT[:, u, q * TOK:(q + 1) * TOK], KX[:, u, :, q * TOK:(q + 1) * TOK],
                                               start=True, stop=True)
                            mm.then_inc(s["scores"], 1)
                        for u in range(2):
                            t.wait("probs", u)
                            for k in range(PAIRS * G):
                                mm = pe.transpose(bank(u, k // 4)[0:SPAN, (k % 4) * SPAN:(k % 4 + 1) * SPAN],
                                                  PR[:, u, 2 * k:2 * k + 2, :].rearrange("c h k -> c (h k)")[:, 0:SPAN], ident[0:SPAN, 0:SPAN])
                            mm.then_inc(s["turned"], 1)
                        for u in range(2):
                            t.wait("pt_dve", u)
                            t.wait("pt_act", u)
                            for q in range(NWIN):
                                p0 = HALF * (q % 2)
                                for g in range(G):
                                    col = (q // 2 * G + g) * VW
                                    mm = pe.matmul(bank(u, 3)[p0:p0 + TOK, col:col + VW],
                                                   PT[:, u, q // 2 * G + g, p0:p0 + TOK], VB[:, u, q, g, :], start=True, stop=True)
                            mm.then_inc(s["heads"], 1)
                        for u in range(2):
                            t.wait("normed", u)
                            for k in range(PAIRS):
                                mm = pe.transpose(bank(u, 0)[0:C, k * SPAN:(k + 1) * SPAN], O[:, u, k, :], ident[0:SPAN, 0:SPAN])
                            mm.then_inc(s["heads_t"], 1)
                        for u in range(2):
                            t.wait("ot", u)
                            pe.matmul(bank(u, 1)[0:C, 0:CH], Wp[0:C + 1, :], OT[:, u], start=True, stop=True).then_inc(s["proj"], 1)
                        if mlp:
                            for u in range(2):
                                t.wait_credited("x1", u)
                                mean_of(X1[:, u], 0, u, "mean2")
                            for u in range(2):
                                t.wait("sq2", u)
                                mean_of(SQ[:, u], 0, u, "var2")
                            for u in range(2):
                                t.wait("xn2", u)
                                for j in range(HB):
                                    pe.matmul(bank(u, 1 + j)[:, 0:CH], W1[0:C + 1, j * 128:(j + 1) * 128], XN2[:, u],
                                              start=True, stop=True).then_inc(s[f"fc1_{j}"], 1)
                            for u in range(2):
                                for j in range(HB):
                                    t.wait(f"gelu_{j}", u)
                                    mm = pe.matmul(bank(u, 0)[0:C, 0:CH], W2[:, j, :], Hd[:, u, j], start=(j == 0), stop=(j == HB - 1))
                                mm.then_inc(s["fc2"], 1)
                        if kind == "L1":
                            for u in range(2):
                                t.wait("x2", u)
                                mean_of(X2[:, u], 0, u, "mean3")
                            for u in range(2):
                                t.wait("sq3", u)
                                mean_of(SQ[:, u], 0, u, "var3")
                        if kind == "L3":
                            for u in range(2):
                                hold(pe, s["x2"], t.v[u], passed)
                                for k in range(WS):
                                    mm = pe.transpose(bank(u, 1 + k // 5)[0:W, (k % 5) * C:(k % 5 + 1) * C],
                                                      X2[:, u, k * W:(k + 1) * W], ident[0:C, 0:C])
                                mm.then_inc(s["yt"], 1)

            @block.scalar
            def _(act):
                with act.Fori(0, N_OUT) as o:
                    with act.Fori(0, N_IN) as i:
                        t = Turn(act, o, i)

                        def squares(n, u):
                            t.wait("xc" + n, u)
                            act.activation(SQ[:, u], (XC3 if n == "3" else XC)[:, u], ACT.Square).then_inc(s["sq" + n], 1)

                        def rstd(n, u, also=None):
                            t.wait("var" + n, u)
                            act.activation(LV[:, u], bank(u, 0)[0:C, 0:CH], ACT.Ln, bias=eps[:, 0:1]).then_inc(s["lv" + n], 1)
                            t.wait("lv" + n, u)
                            act.activation(RS[:, u], LV[:, u], ACT.Exp, scale=-0.5).then_inc(s["rstd" + n], 1)

                        if mlp:
                            for u in range(2):
                                squares("", u)
                            for u in range(2):
                                rstd("", u)
                        for u in range(2):
                            t.wait("q", u)
                            act.mul(QT[:, u], bank(u, 0)[0:C, 0:CH], HD ** -0.5).then_inc(s["qt"], 1)
                            t.wait("v", u)
                            act.copy(VB[0:TOK, u, :, :, 0:HD].rearrange("c q g d -> c (q g) d"),
                                     bank(u, 2)[0:TOK, 0:NWIN * G * HD].rearrange("c (k d) -> c k d", d=HD)).then_inc(s["v_even"], 1)
                        for u in range(2):
                            t.wait("centred", u)
                            act.activation(PR[:, u, :, 0:TOK], SX[:, u], ACT.Exp).then_inc(s["probs"], 1)
                        for u in range(2):
                            t.wait("turned", u)
                            act.copy(PT[:, u, 4:12, :].rearrange("c (a k) q -> c a (k q)", a=2),
                                     PS[0:SPAN, 4 * u + 1:4 * u + 3, 0:4 * SPAN]).then_inc(s["pt_act"], 1)
                        if mlp:
                            for u in range(2):
                                t.wait("heads_t", u)
                                act.copy(OT[0:C, u].rearrange("c (k e q) -> c k e q", k=PAIRS, e=2), window_columns(bank(u, 0))).then_inc(s["ot"], 1)
                            for u in range(2):
                                squares("2", u)
                            for u in range(2):
                                rstd("2", u)
                            for u in range(2):
                                for j in range(HB):
                                    t.wait(f"fc1_{j}", u)
                                    act.activation(Hd[:, u, j], bank(u, 1 + j)[:, 0:CH], ACT.Gelu).then_inc(s[f"gelu_{j}"], 1)
                        if kind == "L1":
                            for u in range(2):
                                squares("3", u)
                            for u in range(2):
                                t.wait("var3", u)
                                act.activation(LV[:, u], bank(u, 0)[0:C, 0:CH], ACT.Ln, bias=eps[:, 0:1]).then_inc(s["tail_read"], 1)
                                t.wait_credited("tail_read", u)
                                act.activation(RS[:, u], LV[:, u], ACT.Exp, scale=-0.5).then_inc(s["rstd3"], 1)
                            for u in range(2):
                                t.wait("xh", u)
                                t.wait("out_free", u)
                                act.activation(XA[:, u], XH[:, u], ACT.Identity, bias=gb[:, 6:7], scale=gb[:, 5:6]).then_inc(s["xa"], 1)

            @block.vector
            def _(dve):
                for name in ("x1", "tail_read", "out_free"):
                    dve.sem_inc(s[name], 2)
                if kind == "L2":
                    dve.sem_inc(s["bias_ready"], 1)
                with dve.Fori(0, N_OUT) as o:
                    if kind == "L2":
                        dve.wait_ge(mask_loaded, o * 32 + 32)
                        for k in range(PAIRS):
                            ins = dve.tensor_tensor(BIAS[:, k], RPB[:], MSK[:, k].unsqueeze(1).broadcast_to([SPAN, HEADS, TOK]), ALU.add)
                        ins.then_inc(s["bias_ready"], 1)
                        hold(dve, s["bias_ready"], o + 2, passed)
                    with dve.Fori(0, N_IN) as i:
                        t = Turn(dve, o, i)

                        def centre(n, src, u):
                            t.wait("mean" + n, u)
                            dve.tensor_tensor((XC3 if n == "3" else XC)[:, u], src, bank(u, 0)[0:C, 0:CH], ALU.subtract).then_inc(s["xc" + n], 1)

                        if mlp:
                            for u in range(2):
                                centre("", X[:, u], u)
                            for u in range(2):
                                t.wait("rstd", u)
                                dve.tensor_tensor(seen(XN[0:C, u]), win(XC[:, u]), win(RS[:, u]), ALU.mult).then_inc(s["xn"], 1)
                        for u in range(2):
                            t.wait("k", u)
                            dve.tensor_copy(KT[:, u], bank(u, 1)[0:C, 0:CH]).then_inc(s["kt"], 1)
                            t.wait("kt", u)
                            for h in range(HEADS):
                                ins = dve.tensor_scalar(KX[:, u, h], KT[:, u], mask6[:, h:h + 1], None, ALU.mult)
                            ins.then_inc(s["kx"], 1)
                            t.wait("v", u)
                            dve.tensor_copy(VB[HALF:SPAN, u, :, :, HD:2 * HD].rearrange("c q g d -> c (q g) d"),
                                            bank(u, 2)[HALF:SPAN, 0:NWIN * G * HD].rearrange("c (k d) -> c k d", d=HD)).then_inc(s["v_odd"], 1)
                        for u in range(2):
                            t.wait("scores", u)
                            ps_s = PS[0:SPAN, 4 * u:4 * u + 4, 0:HEADS * TOK]
                            if kind == "L2":
                                dve.tensor_tensor(SR[:, u].rearrange("c (k h) t -> c k (h t)", k=PAIRS), ps_s,
                                                  BIAS[:].rearrange("c k h t -> c k (h t)"), ALU.add).then_inc(s["biased"], 1)
                                t.wait("biased", u)
                                src = SR[:, u]
                                dve.tensor_reduce(MX[:, u], src, AX.X, ALU.max).then_inc(s["rowmax"], 1)
                                t.wait("rowmax", u)
                                dve.tensor_tensor(SX[:, u], src, MX[:, u].unsqueeze(2).broadcast_to([SPAN, PAIRS * HEADS, TOK]), ALU.subtract).then_inc(s["centred"], 1)
                            else:
                                src = ps_s.rearrange("c k (h t) -> c k h t", h=HEADS)
                                mx = MX[:, u].rearrange("c (k h) -> c k h", k=PAIRS)
                                dve.tensor_reduce(mx, src, AX.X, ALU.max).then_inc(s["rowmax"], 1)
                                t.wait("rowmax", u)
                                dve.tensor_tensor(SX[:, u].rearrange("c (k h) t -> c k h t", k=PAIRS), src,
                                                  mx.unsqueeze(3).broadcast_to([SPAN, PAIRS, HEADS, TOK]), ALU.subtract).then_inc(s["centred"], 1)
                        for u in range(2):
                            t.wait("turned", u)
                            dve.tensor_copy(PT[:, u, 0:4, :].rearrange("c k q -> c (k q)"), bank(u, 0)[0:SPAN, 0:4 * SPAN]).then_inc(s["pt_dve"], 1)
                        for u in range(2):
                            t.wait("heads", u)
                            ho = bank(u, 3)[0:SPAN, 0:PAIRS * G * VW].rearrange("c (k n) -> c k n", n=VW)
                            dve.reciprocal(RSUM[:, u], ho[:, :, 2 * HD:VW]).then_inc(s["rsum"], 1)
                            t.wait("rsum", u)
                            dve.tensor_tensor(O[:, u].rearrange("c k (g e d) -> c (k g) e d", g=G, e=2),
                                              ho[:, :, 0:2 * HD].rearrange("c k (e d) -> c k e d", e=2),
                                              RSUM[:, u].unsqueeze(3).broadcast_to([SPAN, PAIRS * G, 2, HD]), ALU.mult).then_inc(s["normed"], 1)
                        if kind == "L2":
                            for u in range(2):
                                t.wait("heads_t", u)
                                dwv = win(DW[:, u])
                                for e in range(2):
                                    ins = dve.tensor_tensor(seen(OT[0:C, u])[:, e::2], odd_windows(bank(u, 0), e), dwv[:, e::2], ALU.add)
                                ins.then_inc(s["ot"], 1)
                        for u in range(2):
                            t.wait("proj", u)
                            if kind == "L2":
                                t.wait("out_free", u)
                            ins = dve.tensor_tensor(win(X1[:, u]), seen(bank(u, 1)[0:C, 0:CH]), win(X[:, u]), ALU.add)
                            ins.then_inc(s["x1"], 1)
                            if kind == "L2":
                                dve.sem_inc(s["tail_read"], 1)
                        if mlp:
                            for u in range(2):
                                centre("2", X1[:, u], u)
                            for u in range(2):
                                t.wait("rstd2", u)
                                dve.tensor_tensor(XN2[0:C, u], XC[:, u], RS[:, u], ALU.mult).then_inc(s["xn2"], 1)
                            for u in range(2):
                                t.wait("fc2", u)
                                if kind == "L1":
                                    t.wait("out_free", u)
                                dve.scalar_tensor_tensor(X2[:, u], bank(u, 0)[0:C, 0:CH], gb[:, 4:5], X1[:, u], ALU.add, ALU.add).then_inc(s["x2"], 1)
                        if kind == "L1":
                            for u in range(2):
                                t.wait("x2", u)
                                centre("3", X2[:, u], u)
                            for u in range(2):
                                t.wait("rstd3", u)
                                dve.tensor_tensor(XH[:, u], XC3[:, u], RS[:, u], ALU.mult).then_inc(s["xh"], 1)
                        if kind == "L3":
                            for u in range(2):
                                t.wait("yt", u)
                                t.wait("out_free", u)
                                dve.tensor_copy(Y[:, u, 0:5, :].rearrange("c k n -> c (k n)"), bank(u, 1)[0:W, 0:5 * C])
                                dve.tensor_copy(Y[:, u, 5:7, :].rearrange("c k n -> c (k n)"), bank(u, 2)[0:W, 0:2 * C]).then_inc(s["tail_read"], 1)

            @block.gpsimd
            def _(pool):
                with pool.Fori(0, N_OUT) as o:
                    with pool.Fori(0, N_IN) as i:
                        t = Turn(pool, o, i)
                        if kind == "L2":
                            for u in range(2):
                                hold(pool, loaded[u], t.turns * (16 * N_LOADS), passed)
                                pool.tensor_copy(seen(XN[0:C, u]), win(XR[:, u])).then_inc(s["xn"], 1)
                        for u in range(2):
                            b, r = where(o, i, u)
                            if kind == "L1":
                                t.wait("x2", u)
                                pool.dma_start(rows_of(xout, b, r), X2[:, u]).then_inc(stored[u], 16)
                                t.wait("xa", u)
                                pool.dma_start(xn_io[b, :, bass.ds(r * WS + 3, WS), :], XA[:, u]).then_inc(stored[u], 16)
                            if kind == "L2":
                                t.wait_credited("x1", u)
                                pool.dma_start(rows_of(xout, b, r), X1[:, u]).then_inc(stored[u], 16)
                            if kind == "L3":
                                t.wait_credited("tail_read", u)
                                low = r * WS + 3
                                high = (i * (2 * WS) + 7) if u == 0 else None
                                for rows, k0, k1 in ((low, 0, 4), (((r + 1) % NROW) * WS if u else r * WS + 7, 4, 7)):
                                    for q0, q1, col in ((0, W - SHIFT, SHIFT), (W - SHIFT, W, 0)):
                                        pool.dma_start(xout[b, bass.ds(rows, k1 - k0), col:col + q1 - q0, :].rearrange("h q c -> q h c"),
                                                       Y[q0:q1, u, k0:k1, :]).then_inc(stored[u], 16)
                        for u in range(2):
                            pool.wait_ge(stored[u], t.turns * (16 * N_STORES))
                            pool.sem_inc(s["out_free"], 1)


CG, CR = 6, 14
CK = CR + 6
NG, NBK = C // CG, H // CR
IMG = 8
NIG = B // IMG


def conv_pass(nc, PS, w, xn, cv, store_sems):
    KP, MP = CG * CK, CG * CR
    with ExitStack() as ctx:
        sb = lambda name, shape: ctx.enter_context(nc.sbuf_tensor("conv_" + name, shape, F32))
        sem = ctx.enter_context(semaphores(nc, "conv"))
        WB = sb("WB", [KP, 2, 7, MP]); T = sb("T", [KP, NIG, IMG, PW]); D = sb("D", [MP, NIG, IMG, W])
        BM = sb("BM", [KP, 7, MP]); WC = sb("WC", [KP, NG, 49])
        load_all(nc, "conv", [(BM[:], w["band_mask"])]
                 + [(WC[c * CK:(c + 1) * CK], w["dw_by_channel"].rearrange("(g c) t -> c g t", c=CG)[c:c + 1].broadcast_to([CK, NG, 49]))
                    for c in range(CG)], zeros=[T[:]])
        band_step, band_ready = sem("band_step"), sem("band_ready")
        loaded = [sem(f"loaded{k}") for k in range(NIG)]
        product, read = sem("product"), sem("read")
        stored, out_free = store_sems, sem("out_free")
        passed = sem("passed")
        PER = NBK * NIG
        CREDIT = PER + 1
        with nc.Block() as block:
            @block.vector
            def _(dve):
                with dve.Fori(0, NG // 2) as gg:
                    for e in range(2):
                        dve.wait_ge(product, gg * (2 * PER) + (PER * e + 1))
                        for kh in range(7):
                            for kw in range(7):
                                tap = WC[:, bass.ds(gg * 2 + e, 1), kh * 7 + kw:kh * 7 + kw + 1].rearrange("p a b -> p (a b)")
                                if kh == 0:
                                    ins = dve.tensor_scalar(WB[:, e, kw, :], BM[:, kh, :], tap, None, ALU.mult)
                                else:
                                    ins = dve.scalar_tensor_tensor(WB[:, e, kw, :], BM[:, kh, :], tap, WB[:, e, kw, :], ALU.mult, ALU.add)
                            ins.then_inc(band_step if kh < 6 else band_ready, 1)
                            if kh < 6:
                                dve.wait_ge(band_step, gg * 12 + (6 * e + kh + 1))

            @block.sync
            def _(sp):
                sp.sem_inc(product, CREDIT)
                with sp.Fori(0, NG // 2) as gg:
                    for e in range(2):
                        with sp.Fori(0, NBK) as blk:
                            for k in range(NIG):
                                sp.wait_ge(product, gg * (2 * PER) + blk * NIG + (PER * e + k + 1 + CREDIT - NIG))
                                for im in range(IMG):
                                    src = xn[k * IMG + im, bass.ds(gg * (2 * CG) + e * CG, CG), bass.ds(blk * CR, CK), :]
                                    sp.dma_start(T[:, k, im, 3:3 + W], src).then_inc(loaded[k], 16)

            @block.tensor
            def _(pe):
                with pe.Fori(0, NG // 2) as gg:
                    for e in range(2):
                        hold(pe, band_ready, gg * 2 + (e + 1), passed)
                        with pe.Fori(0, NBK) as blk:
                            for k in range(NIG):
                                pe.wait_ge(loaded[k], gg * (2 * NBK * 16 * IMG) + blk * (16 * IMG) + (NBK * e + 1) * 16 * IMG)
                                pe.wait_ge(read, gg * (2 * PER) + blk * NIG + (PER * e + k + 1))
                                for kw in range(7):
                                    mm = pe.matmul(PS[0:MP, k, 0:IMG * W].rearrange("m (i q) -> m i q", i=IMG), WB[:, e, kw, :],
                                                   T[:, k, :, kw:kw + W], start=(kw == 0), stop=(kw == 6))
                                mm.then_inc(product, 1)

            @block.scalar
            def _(act):
                act.sem_inc(read, NIG)
                act.sem_inc(out_free, NIG)
                with act.Fori(0, NG) as g:
                    with act.Fori(0, NBK) as blk:
                        for k in range(NIG):
                            act.wait_ge(product, g * PER + blk * NIG + (k + 1 + CREDIT))
                            act.wait_ge(out_free, g * PER + blk * NIG + (k + 1))
                            act.copy(D[:, k].rearrange("m i q -> m (i q)"), PS[0:MP, k, 0:IMG * W]).then_inc(read, 1)

            @block.gpsimd
            def _(pool):
                with pool.Fori(0, NG) as g:
                    with pool.Fori(0, NBK) as blk:
                        for k in range(NIG):
                            pool.wait_ge(read, g * PER + blk * NIG + (k + 1 + NIG))
                            for im in range(IMG):
                                pool.dma_start(cv[k * IMG + im, bass.ds(g * CG, CG), bass.ds(blk * CR, CR), :], D[:, k, im]).then_inc(stored[k], 16)
                        for k in range(NIG):
                            pool.wait_ge(stored[k], g * (NBK * 16 * IMG) + blk * (16 * IMG) + 16 * IMG)
                            pool.sem_inc(out_free, 1)


def clear_margin(nc, xn):
    with semaphores(nc, "margin") as sem, nc.sbuf_tensor("margin_zero", [C, B * 3 * W], F32) as zero:
        zeroed, cleared = sem("zeroed"), sem("cleared")
        with nc.Block() as block:
            @block.vector
            def _(dve):
                dve.memset(zero[:], 0.0).then_inc(zeroed, 1)

            @block.sync
            def _(sp):
                sp.wait_ge(zeroed, 1)
                for rows in (slice(0, 3), slice(3 + H, 6 + H)):
                    sp.dma_start(xn[:, :, rows, :].rearrange("b c h q -> c b (h q)"),
                                 zero[:].rearrange("c (b n) -> c b n", b=B)).then_inc(cleared, 16)
                sp.wait_ge(cleared, 32)


def build(nc, w, x, out):
    xa = nc.dram_tensor("after_L0", [B, C, H, W], F32).ap()
    xb = nc.dram_tensor("after_L1", [B, C, H, W], F32).ap()
    xn = nc.dram_tensor("L2_norm", [B, C, H + 6, W], F32).ap()
    cv = nc.dram_tensor("L2_conv", [B, C, H, W], F32).ap()
    xc = nc.dram_tensor("after_L2", [B, C, H, W], F32).ap()
    with ExitStack() as ctx:
        PS = ctx.enter_context(nc.psum_tensor("banks", [128, 8, 512], F32))
        stores = lambda name, n: [ctx.enter_context(nc.semaphore(f"{name}_stored{k}")) for k in range(n)]
        clear_margin(nc, xn)
        scan_pass(nc, PS, w, x, xa, stores("scan", 1))
        window_pass(nc, PS, w, "L1", dict(qkv_w=w["L1_conv_w_qkv"], qkv_b=w["L1_conv_b_qkv"], proj_w=w["L1_conv_w_proj"], proj_b=w["L1_conv_b_proj"],
                                          g1=w["L1_conv_g1"], b1=w["L1_conv_b1"], g2=w["L1_conv_g2"], b2=w["L1_conv_b2"], fc1_w=w["L1_conv_w_fc1"],
                                          fc1_b=w["L1_conv_b_fc1"], fc2_w=w["L1_conv_w_fc2"], fc2_b=w["L1_conv_b_fc2"]), xa, xb, stores("L1", 2), xn_io=xn)
        conv_pass(nc, PS, w, xn, cv, stores("conv", NIG))
        window_pass(nc, PS, w, "L2", dict(qkv_w=w["L2_conv_qkv_w"], qkv_b=w["L2_conv_qkv_b"], proj_w=w["L2_conv_proj_w"], proj_b=w["L2_conv_proj_b"],
                                          dw_b=w["L2_conv_dw_b"], rpb=w["rpb"], mask=w["mask"]), xb, xc, stores("L2", 2), xn_io=xn[:, :, 3:3 + H, :], conv=cv)
        window_pass(nc, PS, w, "L3", dict(qkv_w=w["L3_conv_qkv_w"], qkv_b=w["L3_conv_qkv_b"], proj_w=w["L3_conv_proj_w"], proj_b=w["L3_conv_proj_b"],
                                          g1=w["L3_conv_ln1_w"], b1=w["L3_conv_ln1_b"], g2=w["L3_conv_ln2_w"], b2=w["L3_conv_ln2_b"], fc1_w=w["L3_conv_mlp_w1"],
                                          fc1_b=w["L3_conv_mlp_b1"], fc2_w=w["L3_conv_mlp_w2"], fc2_b=w["L3_conv_mlp_b2"]), xc, out, stores("L3", 2))


def position_index():
    i = np.arange(TOK)
    dy = i[:, None] // WS - i[None, :] // WS + WS - 1
    dx = i[:, None] % WS - i[None, :] % WS + WS - 1
    return dy * (2 * WS - 1) + dx


def kernel(**inputs):
    import concourse.bacc as bacc
    from concourse.bass_utils import run_bass_kernel_spmd

    a = {k: np.ascontiguousarray(v) for k, v in inputs.items()}
    a["L2_conv_qkv_w"] = np.ascontiguousarray(a["L2_conv_qkv_w"].T)
    a["L2_conv_proj_w"] = np.ascontiguousarray(a["L2_conv_proj_w"].T)
    a["dw_taps"] = np.ascontiguousarray(a.pop("L0_conv_dw_w")[:, 0, :].T)
    a["rpb"] = np.ascontiguousarray(a.pop("L2_conv_rpb_table")[position_index()].transpose(0, 2, 1))
    a["mask"] = np.ascontiguousarray(a.pop("L2_conv_mask_matrix").reshape(NROW, PAIRS, 2, TOK, TOK).transpose(0, 2, 3, 1, 4))
    a["dw_by_channel"] = np.ascontiguousarray(a.pop("L2_conv_dw_w").reshape(49, C).T)
    feeds = np.zeros((CG, CK, 7, CG, CR), np.float32)
    for kh in range(7):
        for a_ in range(CR):
            feeds[np.arange(CG), a_ + kh, kh, np.arange(CG), a_] = 1.0
    a["band_mask"] = feeds.reshape(CG * CK, 7, CG * CR)
    a["ident"] = np.eye(128, dtype=np.float32)
    a["head_mask"] = np.repeat(np.eye(HEADS, dtype=np.float32), HD, axis=0)
    nc = bacc.Bacc("TRN2", target_bir_lowering=False, num_devices=1)
    arrays, aps = {}, {}
    for name, v in a.items():
        arrays["in_" + name] = v
        aps[name] = nc.dram_tensor("in_" + name, v.shape, F32, kind="ExternalInput").ap()
    out = nc.dram_tensor("out", [B, H, W, C], F32, kind="ExternalOutput").ap()
    build(nc, aps, aps["x"], out)
    return run_bass_kernel_spmd(nc, [arrays], core_ids=[0]).results[0]["out"]
```

```python
from contextlib import ExitStack, contextmanager

import numpy as np

import concourse.bass as bass
from concourse import mybir

F32 = mybir.dt.float32
ALU = mybir.AluOpType
ACT = mybir.ActivationFunctionType
AX = mybir.AxisListType

B, H, W, C = 32, 56, 56, 96
WS, SHIFT, HEADS = 7, 3, 6
HD = C // HEADS
TOK = WS * WS
NWIN = W // WS
NROW = H // WS
CH = WS * W
PAIRS = NWIN // 2
G = HEADS // 2
HALF = 64
SPAN = HALF + TOK
HID = 4 * C
HB = HID // 128
VW = 2 * HD + 2
NCH = B * NROW
EPS = 1e-5
PW = W + 6

def hold(eng, sem, value, passed):
    eng.wait_ge(sem, value)
    eng.sem_inc(passed, 1)


@contextmanager
def semaphores(nc, prefix):
    given = []
    with ExitStack() as ctx:
        def sem(name):
            given.append(ctx.enter_context(nc.semaphore(f"{prefix}_{name}")))
            return given[-1]

        yield sem
        with nc.Block() as block:
            @block.gpsimd
            def _(pool):
                for q in given:
                    pool.sem_clear(q)


def fold_affine(nc, name, raw, bias_row, gamma, beta, ps, pieces):
    n = raw.shape[1]
    with semaphores(nc, name) as sem:
        product_ready = sem("product_ready")
        with nc.Block() as block:
            if beta is not None:
                @block.tensor
                def _(pe):
                    pe.matmul(ps[C:C + 1, 0:n], beta, raw, start=True, stop=True).then_inc(product_ready, 1)

            @block.vector
            def _(dve):
                for target, view in pieces:
                    if gamma is not None:
                        dve.tensor_scalar(target[0:C], view(raw), gamma, None, ALU.mult)
                    else:
                        dve.tensor_copy(target[0:C], view(raw))
                if beta is not None:
                    dve.wait_ge(product_ready, 1)
                for target, view in pieces:
                    if beta is not None:
                        dve.tensor_tensor(target[C:C + 1], view(bias_row), view(ps[C:C + 1, 0:n]), ALU.add)
                    else:
                        dve.tensor_copy(target[C:C + 1], view(bias_row))


def load_all(nc, name, pairs, zeros=(), ones=(), values=()):
    with semaphores(nc, name) as sem:
        weights_loaded = sem("weights_loaded")
        with nc.Block() as block:
            @block.sync
            def _(sp):
                for dst, src in pairs:
                    sp.dma_start(dst, src).then_inc(weights_loaded, 16)
                sp.wait_ge(weights_loaded, 16 * len(pairs))

            @block.vector
            def _(dve):
                for t in zeros:
                    dve.memset(t, 0.0)
                for t in ones:
                    dve.memset(t, 1.0)
                for t, v in values:
                    dve.memset(t, v)


def column(v):
    return v.rearrange("(c o) -> c o", o=1)


def row(v):
    return v.rearrange("(o c) -> o c", o=1)


def scan_pass(nc, PS, w, x, xa, store_sems):
    RB = 8
    TB = RB * W
    NB = H // RB
    S = H * W
    TP = S // 112
    with ExitStack() as ctx:
        sb = lambda name, shape: ctx.enter_context(nc.sbuf_tensor("scan_" + name, shape, F32))
        sem = ctx.enter_context(semaphores(nc, "scan"))
        raw = sb("raw", [C, 2 * C]); brow = sb("brow", [128, 2 * C])
        gcol = sb("gcol", [C, 1]); becol = sb("becol", [C, 1]); fc2b = sb("fc2b", [C, 1])
        dwb = sb("dwb", [C, 2]); taps = sb("taps", [128, 3, 2 * C])
        W1 = sb("W1", [128, 2 * C]); W1T = sb("W1T", [128, 3, 2 * C])
        W2 = sb("W2", [C, 2, C]); J = sb("J", [C, C]); ident = sb("ident", [128, 128])
        grey = sb("grey", [128, 1]); eps = sb("eps", [C, 1]); ones = sb("ones", [C, 1])
        sw1 = sb("sw1", [4, 16]); sb1 = sb("sb1", [16, 1]); sw2 = sb("sw2", [16, 4]); sb2 = sb("sb2", [1, 4])
        XT = sb("XT", [112, TP, C])
        X = sb("X", [C, S]); XN = sb("XN", [C + 1, S]); XS = sb("XS", [C + 1, S + 2])
        XC = sb("XC", [C, 2, TB]); SQ = sb("SQ", [C, 2, TB]); LV = sb("LV", [C, 2, TB]); RS = sb("RS", [C, 2, TB])
        GR = sb("GR", [1, S]); GH = sb("GH", [H, W]); GN = sb("GN", [H, W])
        DH = sb("DH", [H, W]); DV = sb("DV", [H, W]); JH = sb("JH", [H, W]); JV = sb("JV", [H, W]); GA = sb("GA", [H, 4])
        gone = sb("gone", [H, 1])
        sc = sb("sc", [4, 1]); hid = sb("hid", [16, 1]); lg = sb("lg", [1, 4]); st = sb("st", [1, 16])
        pr = sb("pr", [1, 4]); fl = sb("fl", [1, 2]); fb = sb("fb", [C, 2]); one1 = sb("one1", [1, C])
        Hd = sb("Hd", [C, 2, 2, TB]); OUT = sb("OUT", [C, 2, RB, W])

        load_all(nc, "scan", [
            (raw[:], w["L0_conv_fc1_w"]), (brow[C:C + 1, :], row(w["L0_conv_fc1_b"])),
            (gcol[:], column(w["L0_conv_gamma"])), (becol[:], column(w["L0_conv_beta"])),
            (fc2b[:], column(w["L0_conv_fc2_b"])), (dwb[:, 0:1], column(w["L0_conv_dw_b"][0:C])), (dwb[:, 1:2], column(w["L0_conv_dw_b"][C:2 * C])),
            (W2[:], w["L0_conv_fc2_w"].rearrange("(h c) n -> c h n", h=2)), (ident[:], w["ident"]),
            (sw1[:], w["L0_conv_sel_w1"]), (sb1[:], column(w["L0_conv_sel_b1"])),
            (sw2[:], w["L0_conv_sel_w2"]), (sb2[:], row(w["L0_conv_sel_b2"]))]
            + [(taps[0:C + 1, t, :], w["dw_taps"][t:t + 1, :].broadcast_to([C + 1, 2 * C])) for t in range(3)],
            zeros=[XS[:], GA[:]], ones=[XN[C:C + 1, :], PS[:], ones[:], one1[:]],
            values=[(J[:], 1.0 / C), (eps[:], EPS), (gone[:], 1.0 / (H * (W - 1)))])
        fold_affine(nc, "scan_fc1", raw[:], brow[C:C + 1, :], gcol[:, 0:1], becol[:, 0:1], PS[:, 0, :],
                    [(W1[0:C + 1, :], lambda t: t)])
        grey_bias = sem("grey_bias")
        with nc.Block() as block:
            @block.tensor
            def _(pe):
                pe.matmul(PS[C:C + 1, 1, 0:1], becol[:, 0:1], ones[:, 0:1], start=True, stop=True).then_inc(grey_bias, 1)

            @block.vector
            def _(dve):
                for t in range(3):
                    dve.tensor_tensor(W1T[0:C + 1, t, :], W1[0:C + 1, :], taps[0:C + 1, t, :], ALU.mult)
                dve.tensor_scalar(grey[0:C], gcol[:], 1.0 / C, None, ALU.mult)
                dve.wait_ge(grey_bias, 1)
                dve.tensor_scalar(grey[C:C + 1], PS[C:C + 1, 1, 0:1], 1.0 / C, None, ALU.mult)

        s = {n: sem(n) for n in ("img_loaded", "turned", "x_ready", "mean", "xc", "sq", "var", "lv", "rstd",
                                 "xn", "greyp", "grey_row", "grey_tiles", "diffs", "sums", "sums_ready", "score",
                                 "scores", "sel1", "hidden", "sel2", "dve_chain", "centred", "expo", "flag",
                                 "flagb", "flag_ready", "blend", "xs", "conv0", "conv1", "gelu", "fc2", "out", "last_xn", "out_free")}
        stored, passed = store_sems[0], sem("passed")
        CHAIN = 8
        XTr = x.rearrange("b h w c -> b (h w) c").rearrange("b (p j) c -> b p j c", j=TP)
        def grey_block(pe, m0, m):
            pe.wait_ge(s["xn"], m0 + (m + 1))
            pe.matmul(PS[0:1, 4 + m % 2, 0:TB], grey[0:C + 1, :], XN[:, m * TB:(m + 1) * TB],
                      start=True, stop=True).then_inc(s["greyp"], 1)

        def fc2_block(pe, m0, m):
            v = m % 2
            pe.wait_ge(s["gelu"], m0 * 2 + 2 * (m + 1))
            if m >= 2:
                pe.wait_ge(s["out"], m0 * 2 + (2 * (m - 1) + 2))
            for h in range(2):
                mm = pe.matmul(PS[0:C, 6 + v, 0:TB], W2[:, h, :], Hd[:, v, h], start=(h == 0), stop=(h == 1))
            mm.then_inc(s["fc2"], 1)

        with nc.Block() as block:
            @block.sync
            def _(sp):
                with sp.Fori(0, B) as b:
                    b1 = sp.snap(b + 1)
                    sp.wait_ge(s["turned"], b1 * NB - (NB - 1))
                    sp.dma_start(XT[:], XTr[b]).then_inc(s["img_loaded"], 16)
                    sp.wait_ge(s["grey_row"], b1 * NB)
                    sp.dma_start(GH[:], GR[0:1, :].rearrange("o (h w) -> o h w", w=W)).then_inc(s["grey_tiles"], 16)
                    sp.dma_start(GN[0:H - 1, :], GR[0:1, W:].rearrange("o (h w) -> o h w", w=W)).then_inc(s["grey_tiles"], 16)

            @block.tensor
            def _(pe):
                pe.sem_inc(s["turned"], 1)
                with pe.Fori(0, B) as b:
                    m0 = pe.snap(b * NB)
                    b1 = pe.snap(b + 1)
                    pe.wait_ge(s["img_loaded"], b1 * 16)
                    for m in range(NB):
                        if m >= 2:
                            pe.wait_ge(s["x_ready"], m0 + (m - 1))
                        else:
                            pe.wait_ge(s["out"], m0 * 2 + (2 if m == 0 else 2))
                        for j in range(4):
                            mm = pe.transpose(PS[0:C, m % 2, j * 112:(j + 1) * 112], XT[:, 4 * m + j, :], ident[0:112, 0:112])
                        mm.then_inc(s["turned"], 1)
                    for m in range(NB):
                        if m == 0:
                            pe.wait_ge(s["x_ready"], m0 + NB)
                        else:
                            pass
                        v = m % 2
                        if m >= 2:
                            pe.wait_ge(s["grey_row"], m0 + (m - 1))
                        pe.matmul(PS[0:C, 2 + v, 0:TB], J[:], X[:, m * TB:(m + 1) * TB], start=True, stop=True).then_inc(s["mean"], 1)
                        pe.wait_ge(s["sq"], m0 + (m + 1))
                        pe.matmul(PS[0:C, 2 + v, 0:TB], J[:], SQ[:, v], start=True, stop=True).then_inc(s["var"], 1)
                        if m >= 1:
                            grey_block(pe, m0, m - 1)
                    grey_block(pe, m0, NB - 1)
                    hold(pe, s["sums"], b1, passed)
                    pe.matmul(PS[0:4, 0, 0:1], GA[:], gone[:], start=True, stop=True).then_inc(s["score"], 1)
                    hold(pe, s["scores"], b1, passed)
                    pe.matmul(PS[0:16, 1, 0:1], sw1[:], sc[:], start=True, stop=True).then_inc(s["sel1"], 1)
                    hold(pe, s["hidden"], b1, passed)
                    pe.matmul(PS[0:1, 0, 0:4], hid[:], sw2[:], start=True, stop=True).then_inc(s["sel2"], 1)
                    hold(pe, s["flag"], b1, passed)
                    pe.matmul(PS[0:C, 1, 0:2], one1[:], fl[:], start=True, stop=True).then_inc(s["flagb"], 1)
                    for m in range(NB):
                        v = m % 2
                        pe.wait_ge(s["xs"], m0 + min(m + 2, NB))
                        if m >= 2:
                            pe.wait_ge(s["gelu"], m0 * 2 + 2 * (m - 1))
                        for h in range(2):
                            for t in range(3):
                                mm = pe.matmul(PS[0:C, 2 + 2 * v + h, 0:TB], W1T[0:C + 1, t, h * C:(h + 1) * C],
                                               XS[:, m * TB + t:m * TB + t + TB], start=(t == 0), stop=(t == 2))
                            mm.then_inc(s["conv0"], 1)
                        if m >= 1:
                            fc2_block(pe, m0, m - 1)
                    fc2_block(pe, m0, NB - 1)

            @block.scalar
            def _(act):
                with act.Fori(0, B) as b:
                    m0 = act.snap(b * NB)
                    b1 = act.snap(b + 1)
                    for m in range(NB):
                        v = m % 2
                        act.wait_ge(s["xc"], m0 + (m + 1))
                        act.activation(SQ[:, v], XC[:, v], ACT.Square).then_inc(s["sq"], 1)
                        act.wait_ge(s["var"], m0 + (m + 1))
                        act.activation(LV[:, v], PS[0:C, 2 + v, 0:TB], ACT.Ln, bias=eps[:, 0:1]).then_inc(s["lv"], 1)
                        act.wait_ge(s["lv"], m0 + (m + 1))
                        act.activation(RS[:, v], LV[:, v], ACT.Exp, scale=-0.5).then_inc(s["rstd"], 1)
                        if m >= 1:
                            act.wait_ge(s["greyp"], m0 + m)
                            act.copy(GR[0:1, (m - 1) * TB:m * TB], PS[0:1, 4 + (m - 1) % 2, 0:TB]).then_inc(s["grey_row"], 1)
                    act.wait_ge(s["greyp"], m0 + NB)
                    act.copy(GR[0:1, (NB - 1) * TB:], PS[0:1, 4 + (NB - 1) % 2, 0:TB]).then_inc(s["grey_row"], 1)
                    act.wait_ge(s["diffs"], b1 * 2)
                    act.activation(JH[:, 0:W - 1], DH[:, 0:W - 1], ACT.Abs, accum_out=GA[:, 0:1])
                    act.activation(JV[0:H - 1, :], DV[0:H - 1, :], ACT.Abs, accum_out=GA[0:H - 1, 1:2]).then_inc(s["sums_ready"], 1)
                    act.wait_ge(s["score"], b1)
                    act.activation(sc[:], PS[0:4, 0, 0:1], ACT.Abs).then_inc(s["scores"], 1)
                    act.wait_ge(s["sel1"], b1)
                    act.activation(hid[:], PS[0:16, 1, 0:1], ACT.Relu, bias=sb1[:, 0:1]).then_inc(s["hidden"], 1)
                    act.wait_ge(s["centred"], b1)
                    act.activation(pr[:], lg[:], ACT.Exp).then_inc(s["expo"], 1)
                    for m in range(NB):
                        v = m % 2
                        for h in range(2):
                            act.wait_ge(s["conv0"], m0 * 2 + (2 * m + h + 1))
                            if m >= 2 and h == 0:
                                act.wait_ge(s["fc2"], m0 + (m - 1))
                            act.activation(Hd[:, v, h], PS[0:C, 2 + 2 * v + h, 0:TB], ACT.Gelu, bias=dwb[:, h:h + 1]).then_inc(s["gelu"], 1)

            @block.vector
            def _(dve):
                dve.sem_inc(s["out"], 2)
                dve.sem_inc(s["out_free"], 2)
                with dve.Fori(0, B) as b:
                    m0 = dve.snap(b * NB)
                    b1 = dve.snap(b + 1)
                    k0 = dve.snap(b * CHAIN)
                    k = [0]

                    def link(ins):
                        k[0] += 1
                        ins.then_inc(s["dve_chain"], 1)
                        dve.wait_ge(s["dve_chain"], k0 + k[0])

                    Xv = X[:].rearrange("c (p j) -> c j p", j=TP)
                    for m in range(NB):
                        dve.wait_ge(s["turned"], m0 + (m + 2))
                        dve.tensor_copy(Xv[:, 4 * m:4 * m + 4, :],
                                        PS[0:C, m % 2, 0:TB].rearrange("c (j p) -> c j p", j=4)).then_inc(s["x_ready"], 1)
                    dve.wait_ge(s["x_ready"], m0 + NB)
                    for m in range(NB):
                        v = m % 2
                        cols = slice(m * TB, (m + 1) * TB)
                        dve.wait_ge(s["mean"], m0 + (m + 1))
                        dve.tensor_tensor(XC[:, v], X[:, cols], PS[0:C, 2 + v, 0:TB], ALU.subtract).then_inc(s["xc"], 1)
                        dve.wait_ge(s["rstd"], m0 + (m + 1))
                        dve.tensor_tensor(XN[0:C, cols], XC[:, v], RS[:, v], ALU.mult).then_inc(s["xn"], 1)
                    dve.wait_ge(s["grey_tiles"], b1 * 32)
                    dve.tensor_tensor(DH[:, 0:W - 1], GH[:, 1:W], GH[:, 0:W - 1], ALU.subtract).then_inc(s["diffs"], 1)
                    dve.tensor_tensor(DV[0:H - 1, :], GN[0:H - 1, :], GH[0:H - 1, :], ALU.subtract).then_inc(s["diffs"], 1)
                    dve.wait_ge(s["sums_ready"], b1)
                    link(dve.tensor_tensor(GA[:, 2:3], GA[:, 0:1], GA[:, 1:2], ALU.add))
                    dve.tensor_scalar(GA[:, 2:3], GA[:, 2:3], 0.8, 0.5, ALU.mult, ALU.mult)
                    dve.tensor_tensor(GA[:, 3:4], GA[:, 0:1], GA[:, 1:2], ALU.subtract).then_inc(s["sums"], 1)
                    dve.wait_ge(s["sel2"], b1)
                    link(dve.tensor_tensor(st[:, 0:4], PS[0:1, 0, 0:4], sb2[:], ALU.add))
                    link(dve.tensor_reduce(st[:, 4:5], st[:, 0:4], AX.X, ALU.max))
                    dve.tensor_scalar(lg[:], st[:, 0:4], st[:, 4:5], None, ALU.subtract).then_inc(s["centred"], 1)
                    dve.wait_ge(s["expo"], b1)
                    link(dve.tensor_reduce(st[:, 5:6], pr[:], AX.X, ALU.add))
                    link(dve.reciprocal(st[:, 6:7], st[:, 5:6]))
                    link(dve.tensor_scalar(st[:, 8:12], pr[:], st[:, 6:7], None, ALU.mult))
                    dve.tensor_tensor(st[:, 12:13], st[:, 9:10], st[:, 8:9], ALU.is_gt)
                    link(dve.tensor_tensor(st[:, 13:14], st[:, 10:11], st[:, 11:12], ALU.max))
                    link(dve.tensor_tensor(st[:, 14:15], st[:, 9:10], st[:, 13:14], ALU.is_ge))
                    dve.tensor_tensor(fl[:, 0:1], st[:, 12:13], st[:, 14:15], ALU.mult).then_inc(s["flag_ready"], 1)
                    dve.wait_ge(s["flag_ready"], b1)
                    dve.tensor_scalar(fl[:, 1:2], fl[:, 0:1], -1.0, 1.0, ALU.mult, ALU.add).then_inc(s["flag"], 1)
                    dve.wait_ge(s["flagb"], b1)
                    dve.tensor_copy(fb[:], PS[0:C, 1, 0:2]).then_inc(s["last_xn"], 1)
                    dve.wait_ge(s["last_xn"], b1)
                    XNT = XN[0:C, :].rearrange("c (h w) -> c w h", w=W)
                    for m in range(NB + 1):
                        if m < NB:
                            cols = slice(1 + m * TB, 1 + (m + 1) * TB)
                            dve.tensor_scalar(XS[0:C, cols], XN[0:C, m * TB:(m + 1) * TB], fb[:, 1:2], None, ALU.mult).then_inc(s["blend"], 1)
                            if m == 0:
                                dve.memset(XS[C:C + 1, 1:S + 1], 1.0)
                            dve.wait_ge(s["blend"], m0 + (m + 1))
                            dve.scalar_tensor_tensor(XS[0:C, cols].rearrange("c (a q) -> c a q", q=H), XNT[:, m * RB:(m + 1) * RB, :], fb[:, 0:1],
                                                     XS[0:C, cols].rearrange("c (a q) -> c a q", q=H), ALU.mult, ALU.add).then_inc(s["xs"], 1)
                    for m in range(NB):
                        v = m % 2
                        i0 = m * TB
                        dve.wait_ge(s["fc2"], m0 + (m + 1))
                        dve.wait_ge(s["out_free"], m0 + (m + 1 if m else 2))
                        Xr = X[:, i0:i0 + TB].rearrange("c (a q) -> c a q", q=W)
                        Pr = PS[0:C, 6 + v, 0:TB].rearrange("c (a q) -> c a q", q=W)
                        for dst, src in ((slice(0, W - SHIFT), slice(SHIFT, W)), (slice(W - SHIFT, W), slice(0, SHIFT))):
                            dve.scalar_tensor_tensor(OUT[:, v, :, dst], Pr[:, :, src], fc2b[:, 0:1], Xr[:, :, src],
                                                     ALU.add, ALU.add).then_inc(s["out"], 1)

            @block.gpsimd
            def _(pool):
                with pool.Fori(0, B) as b:
                    m0 = pool.snap(b * NB)
                    for m in range(NB):
                        v = m % 2
                        pool.wait_ge(s["out"], m0 * 2 + (2 * (m + 1) + 2))
                        if m == 0:
                            pool.dma_start(xa[b, :, H - SHIFT:H, :], OUT[:, v, 0:SHIFT, :]).then_inc(stored, 16)
                            pool.dma_start(xa[b, :, 0:RB - SHIFT, :], OUT[:, v, SHIFT:RB, :]).then_inc(stored, 16)
                        else:
                            pool.dma_start(xa[b, :, m * RB - SHIFT:(m + 1) * RB - SHIFT, :], OUT[:, v]).then_inc(stored, 16)
                        pool.wait_ge(stored, b * (16 * (NB + 1)) + 16 * (m + 2))
                        pool.sem_inc(s["out_free"], 1)


class Step:

    def __init__(self, eng, sems, t, u, static):
        self.eng, self.sems, self.static = eng, sems, static
        self.u, self.v = u, 1 - u
        self.t = t if static else eng.snap(t)
        self.f = not static or t < NCH
        self.k = not static or 1 <= t <= NCH
        self.m = not static or 2 <= t
        self.count = {}

    def value(self, lag):
        if self.static:
            return self.t - lag + 1
        if lag not in self.count:
            self.count[lag] = self.eng.snap(self.t + (1 - lag)) if lag != 1 else self.t
        return self.count[lag]

    def wait(self, name, lag):
        if not self.static or self.value(lag) >= 1:
            self.eng.wait_ge(self.sems[name], self.value(lag))

    def wait_turn(self, sem, lag, per):
        c = self.t - lag
        if not self.static or c >= 0:
            self.eng.wait_ge(sem, (c // 2 + 1) * (16 * per))

    def place(self, lag):
        c = self.t - lag
        if self.static:
            return c // NROW, c % NROW
        c = self.eng.snap(c)
        return self.eng.snap(c // NROW), self.eng.snap(c % NROW)


def over_chunks(eng, sems, step, last):
    for t in range(4):
        step(Step(eng, sems, t, t % 2, True))
    with eng.Fori(0, (NCH - 6) // 2) as i:
        for u in range(2):
            step(Step(eng, sems, i * 2 + (4 + u), u, False))
    for t in range(NCH - 2, NCH + last):
        step(Step(eng, sems, t, t % 2, True))


def window_pass(nc, PS, w, kind, p, xin, xout, xn_io=None, conv=None):
    mlp = kind != "L2"
    LAST = 2 if mlp else 1
    N_STORES = {"L1": 2, "L2": 1, "L3": 4}[kind]
    with ExitStack() as ctx:
        sb = lambda name, shape: ctx.enter_context(nc.sbuf_tensor(f"{kind}_{name}", shape, F32))
        sem = ctx.enter_context(semaphores(nc, kind))
        ident = sb("ident", [128, 128]); mask6 = sb("mask6", [C, HEADS]); eps = sb("eps", [C, 1])
        J = sb("J", [C, C]); IJ = sb("IJ", [C, C])
        rawq = sb("rawq", [C, 3 * C]); brow = sb("brow", [128, HID])
        Wq = sb("Wq", [128, C]); Wk = sb("Wk", [128, C]); Wv = sb("Wv", [128, 2, G, HD]); Wp = sb("Wp", [128, C])
        rawp = sb("rawp", [C, C]); prow = sb("prow", [128, C]); gb = sb("gb", [C, 8])
        X = sb("X", [C, 2, CH]); XN = sb("XN", [C + 1, 2, CH]); QT = sb("QT", [C, 2, CH]); KT = sb("KT", [C, 2, CH])
        KX = sb("KX", [C, 2, HEADS, CH]); VB = sb("VB", [SPAN, 2, NWIN, G, VW])
        MX = sb("MX", [SPAN, 2, 2, HEADS * 2]); SX = sb("SX", [SPAN, 2, PAIRS * HEADS, TOK])
        PR = sb("PR", [SPAN, 2, PAIRS * HEADS, HALF]); PT = sb("PT", [SPAN, 2, PAIRS * G, SPAN])
        RSUM = sb("RSUM", [SPAN, 2, PAIRS * G, 2]); O = sb("O", [SPAN, 2, PAIRS, C]); OT = sb("OT", [C + 1, 2, CH])
        X1 = sb("X1", [C, 2, CH])
        if mlp:
            SQ = sb("SQ", [C, 2, CH]); LV = sb("LV", [C, 2, CH]); RS = sb("RS", [C, 2, CH])
            SQ2 = sb("SQ2", [C, 2, CH]); LV2 = sb("LV2", [C, 2, CH]); RS2 = sb("RS2", [C, 2, CH])
            raw1 = sb("raw1", [C, HID]); W1 = sb("W1", [128, HID]); W2 = sb("W2", [128, HB, C])
            XN2 = sb("XN2", [C + 1, 2, CH]); Hd = sb("Hd", [128, 2, HB, CH]); X2 = sb("X2", [C, 2, CH])
        if kind == "L1":
            SQ3 = sb("SQ3", [C, 2, CH]); LV3 = sb("LV3", [C, 2, CH]); RS3 = sb("RS3", [C, 2, CH])
            XH = sb("XH", [C, 2, CH]); XA = sb("XA", [C, 2, CH])
        if kind == "L2":
            XR = sb("XR", [C, 2, CH]); DW = sb("DW", [C, 2, CH])
            RPB = sb("RPB", [SPAN, HEADS, TOK]); MSK = sb("MSK", [SPAN, NROW, PAIRS, TOK])
            BIAS = sb("BIAS", [SPAN, NROW, PAIRS * HEADS, TOK]); SR = sb("SR", [SPAN, 2, PAIRS * HEADS, TOK])
        if kind == "L3":
            Y = sb("Y", [W, 2, WS, C])

        loads = [(ident[:], w["ident"]), (mask6[:], w["head_mask"]), (rawq[:], p["qkv_w"]), (brow[C:C + 1, 0:3 * C], row(p["qkv_b"])),
                 (rawp[:], p["proj_w"]), (prow[C:C + 1, :], row(p["proj_b"]))]
        pad_ones = [PS[:], PR[:], XN[C:C + 1], OT[C:C + 1], VB[0:TOK, :, :, :, 2 * HD], VB[HALF:SPAN, :, :, :, 2 * HD + 1]]
        if mlp:
            pad_ones += [XN2[C:C + 1]]
            loads += [(gb[:, i:i + 1], column(p[n])) for i, n in enumerate(("g1", "b1", "g2", "b2", "fc2_b"))]
            loads += [(raw1[:], p["fc1_w"]), (W2[:], p["fc2_w"].rearrange("(j h) n -> h j n", j=HB))]
        if kind == "L1":
            loads += [(gb[:, 5:6], column(w["L2_conv_norm_gamma"])), (gb[:, 6:7], column(w["L2_conv_norm_beta"]))]
        if kind == "L2":
            loads += [(gb[:, 0:1], column(p["dw_b"]))]
        load_all(nc, kind, loads, zeros=[VB[:]] + ([RPB[:], MSK[:]] if kind == "L2" else []), values=[(J[:], 1.0 / C), (eps[:], EPS)])
        with nc.Block() as block:
            @block.vector
            def _(dve):
                for t in pad_ones:
                    dve.memset(t, 1.0)
                dve.tensor_tensor(IJ[:], ident[0:C, 0:C], J[:], ALU.subtract)
        if kind == "L2":
            load_all(nc, "L2b", [(RPB[HALF * e:HALF * e + TOK], p["rpb"]) for e in range(2)]
                     + [(MSK[HALF * e:HALF * e + TOK], p["mask"][e]) for e in range(2)])
            with nc.Block() as block:
                @block.vector
                def _(dve):
                    for r in range(NROW):
                        for k in range(PAIRS):
                            dve.tensor_tensor(BIAS[:, r, k * HEADS:(k + 1) * HEADS], RPB[:],
                                              MSK[:, r, k].unsqueeze(1).broadcast_to([SPAN, HEADS, TOK]), ALU.add)
        third = lambda i: (lambda t: t[:, i * C:(i + 1) * C])
        vhalf = lambda e: (lambda t: t[:, 2 * C:3 * C].rearrange("c (g q d) -> c q g d", g=G, q=2)[:, e])
        fold_affine(nc, kind + "_qkv", rawq[:], brow[C:C + 1, 0:3 * C], gb[:, 0:1] if mlp else None, gb[:, 1:2] if mlp else None,
                    PS[:, 0, :], [(Wq[0:C + 1], third(0)), (Wk[0:C + 1], third(1)), (Wv[0:C + 1, 0], vhalf(0)), (Wv[0:C + 1, 1], vhalf(1))])
        fold_affine(nc, kind + "_proj", rawp[:], prow[C:C + 1, :], None, gb[:, 0:1] if kind == "L2" else None,
                    PS[:, 1, :], [(Wp[0:C + 1], lambda t: t)])
        if mlp:
            load_all(nc, kind + "c", [(brow[C:C + 1, 0:HID], row(p["fc1_b"]))])
            fold_affine(nc, kind + "_fc1", raw1[:], brow[C:C + 1, :], gb[:, 2:3], gb[:, 3:4], PS[:, 2, :], [(W1[0:C + 1, :], lambda t: t)])

        names = ["xn", "k", "q", "v", "qt", "kt", "kx", "v_even", "v_odd", "scores0", "scores1", "rowmax0", "rowmax1",
                 "centred0", "centred1", "probs0", "probs1"]
        names += ["turned0", "turned1", "turned2", "pt0", "pt1", "pt2", "heads", "rsum", "normed", "heads_t", "ot", "proj", "x1"]
        if mlp:
            names += ["xc", "sq", "var", "lv", "rstd", "xc2", "sq2", "var2", "lv2", "rstd2", "xn2", "fc2", "x2"]
            names += [f"fc1_{j}" for j in range(HB)] + [f"gelu_{j}" for j in range(HB)]
        if kind == "L1":
            names += ["xc3", "sq3", "var3", "lv3", "rstd3", "xh", "xa"]
        if kind == "L2":
            names += ["biased0", "biased1"]
        if kind == "L3":
            names += ["yt", "y_low", "y"]
        s = {n: sem(n) for n in names}
        loaded = [sem(f"loaded{u}") for u in range(2)]
        norm_loaded = [sem(f"norm_loaded{u}") for u in range(2)] if kind == "L2" else None
        stored = [sem(f"stored{u}") for u in range(2)]
        passed = sem("passed")
        N_LOADS = 1 if mlp else 2
        bank = lambda k: PS[:, k, :]
        TURN = (4, 5, 4) if mlp else (4, 5, 6)
        HEADS_BANK, OT_BANK, PROJ_BANK = (5, 4, 5) if mlp else (7, 4, 5)

        def rows_of(t, place):
            b, r = place
            return t[b, :, bass.ds(r * WS, WS), :]

        def win(t):
            return t.rearrange("c (i q j) -> c q i j", i=WS, j=WS)

        def seen(t):
            return t.rearrange("c (q i j) -> c q i j", i=WS, j=WS)

        def window_columns(bk):
            v = bk[0:C, 0:PAIRS * SPAN]
            return bass.AP(v.tensor, v.offset, [v.ap[0], [SPAN, PAIRS], [HALF, 2], [1, TOK]])

        def parity_windows(bk, e):
            v = bk[0:C, 0:PAIRS * SPAN]
            return bass.AP(v.tensor, v.offset + e * HALF, [v.ap[0], [SPAN, PAIRS], [WS, WS], [1, WS]])

        with nc.Block() as block:
            @block.sync
            def _(sp):
                def load(st, lag):
                    u = st.u if lag % 2 == 0 else st.v
                    place = st.place(lag)
                    st.wait("x1", lag + 2)
                    sp.dma_start(X[:, u], rows_of(xin, place)).then_inc(loaded[u], 16)
                    if kind == "L2":
                        sp.dma_start(DW[:, u], rows_of(conv, place)).then_inc(loaded[u], 16)

                def load_norm(st, lag):
                    place = st.place(lag)
                    st.wait("xn", lag + 2)
                    sp.dma_start(XR[:, st.u], rows_of(xn_io, place)).then_inc(norm_loaded[st.u], 16)

                def step(st):
                    if kind == "L2" and (not st.static or st.t + 2 < NCH):
                        load_norm(st, -2)
                    if not st.static or st.t + 1 < NCH:
                        load(st, -1)
                    if kind == "L2" and st.k:
                        place = st.place(1)
                        st.wait("x1", 1)
                        sp.dma_start(rows_of(xout, place), X1[:, st.v]).then_inc(stored[st.v], 16)
                    if kind == "L1" and st.m:
                        place = st.place(2)
                        st.wait("x2", 2)
                        sp.dma_start(rows_of(xout, place), X2[:, st.u]).then_inc(stored[st.u], 16)
                        st.wait("xa", 2)
                        b, r = place
                        sp.dma_start(xn_io[b, :, bass.ds(r * WS + 3, WS), :], XA[:, st.u]).then_inc(stored[st.u], 16)
                    if kind == "L3" and st.m:
                        b, r = st.place(2)
                        low = r * WS + 3
                        high = ((r + 1) % NROW) * WS
                        if not st.static:
                            low, high = sp.snap(low), sp.snap(high)
                        st.wait("y", 2)
                        for rows, k0, k1 in ((low, 0, 4), (high, 4, 7)):
                            for q0, q1, col in ((0, W - SHIFT, SHIFT), (W - SHIFT, W, 0)):
                                sp.dma_start(xout[b, bass.ds(rows, k1 - k0), col:col + q1 - q0, :].rearrange("h q c -> q h c"),
                                             Y[q0:q1, st.u, k0:k1, :]).then_inc(stored[st.u], 16)

                for c in range(2 if kind == "L2" else 0):
                    load_norm(Step(sp, s, c, c % 2, True), 0)
                load(Step(sp, s, 0, 0, True), 0)
                over_chunks(sp, s, step, LAST)
                for u in range(2):
                    sp.wait_ge(stored[u], 16 * N_STORES * (NCH // 2))

            @block.tensor
            def _(pe):
                def norm(st, src, k, what, ready, guard=None):
                    pe.matmul(bank(k)[0:C, 0:CH], what[:], src, start=True, stop=True).then_inc(s[ready], 1)

                def turn(st, a):
                    for k in range(4 * a, 4 * a + 4):
                        mm = pe.transpose(bank(TURN[a])[0:SPAN, (k % 4) * SPAN:(k % 4 + 1) * SPAN],
                                          PR[:, st.v, 2 * k:2 * k + 2, :].rearrange("c h k -> c (h k)")[:, 0:SPAN], ident[0:SPAN, 0:SPAN])
                    mm.then_inc(s[f"turned{a}"], 1)

                def keys_and_queries(st):
                    pe.matmul(bank(1)[0:C, 0:CH], Wk[0:C + 1, :], XN[:, st.u], start=True, stop=True).then_inc(s["k"], 1)
                    pe.matmul(bank(0)[0:C, 0:CH], Wq[0:C + 1, :], XN[:, st.u], start=True, stop=True).then_inc(s["q"], 1)

                def values(st):
                    st.wait("centred1", 1)
                    for q in range(NWIN):
                        for e in range(2):
                            mm = pe.matmul(bank(2)[HALF * e:HALF * e + TOK, q * G * HD:(q + 1) * G * HD],
                                           XN[:, st.u, q * TOK:(q + 1) * TOK], Wv[0:C + 1, e].rearrange("c g d -> c (g d)"),
                                           start=True, stop=True)
                    mm.then_inc(s["v"], 1)

                def scores(st, half):
                    if half == 0:
                        st.wait("qt", 0)
                        st.wait("kx", 0)
                    else:
                        st.wait("v_even", 0)
                        st.wait("v_odd", 0)
                    for q in range(4 * half, 4 * half + 4):
                        p0 = HALF * (q % 2)
                        mm = pe.matmul(bank(q // 2)[p0:p0 + TOK, 0:HEADS * TOK].rearrange("c (h k) -> c h k", h=HEADS),
                                       QT[:, st.u, q * TOK:(q + 1) * TOK], KX[:, st.u, :, q * TOK:(q + 1) * TOK],
                                       start=True, stop=True)
                    mm.then_inc(s[f"scores{half}"], 1)

                def heads(st):
                    st.wait("pt0", 1)
                    st.wait("pt1", 1)
                    st.wait("pt2", 1)
                    for q in range(NWIN):
                        p0 = HALF * (q % 2)
                        for g in range(G):
                            col = (q // 2 * G + g) * VW
                            mm = pe.matmul(bank(HEADS_BANK)[p0:p0 + TOK, col:col + VW],
                                           PT[:, st.v, q // 2 * G + g, p0:p0 + TOK], VB[:, st.v, q, g, :], start=True, stop=True)
                    mm.then_inc(s["heads"], 1)

                def heads_turned(st):
                    st.wait("normed", 1)
                    for k in range(PAIRS):
                        mm = pe.transpose(bank(OT_BANK)[0:C, k * SPAN:(k + 1) * SPAN], O[:, st.v, k, :], ident[0:SPAN, 0:SPAN])
                    mm.then_inc(s["heads_t"], 1)

                def project(st):
                    st.wait("ot", 1)
                    pe.matmul(bank(PROJ_BANK)[0:C, 0:CH], Wp[0:C + 1, :], OT[:, st.v], start=True, stop=True).then_inc(s["proj"], 1)

                def hidden(st, j):
                    pe.matmul(bank((7, 6, 7)[j])[:, 0:CH], W1[0:C + 1, j * 128:(j + 1) * 128], XN2[:, st.u],
                              start=True, stop=True).then_inc(s[f"fc1_{j}"], 1)

                def mlp_step(st):
                    if st.f:
                        st.wait_turn(loaded[st.u], 0, N_LOADS)
                        st.wait("centred0", 1)
                        norm(st, X[:, st.u], 0, IJ, "xc")
                    if st.m:
                        st.wait("x1", 2)
                        st.wait("lv3" if kind == "L1" else "y", 3)
                        norm(st, X1[:, st.u], 6, IJ, "xc2")
                    if st.f:
                        st.wait("sq", 0)
                        norm(st, SQ[:, st.u], 1, J, "var")
                    if st.k:
                        st.wait("probs0", 1)
                        st.wait("x1", 2)
                        turn(st, 0)
                    if st.m:
                        st.wait("sq2", 2)
                        if kind == "L1":
                            st.wait("xh", 3)
                        norm(st, SQ2[:, st.u], 7, J, "var2")
                    if st.k:
                        st.wait("probs1", 1)
                        turn(st, 1)
                    if st.f:
                        st.wait("xn", 0)
                        keys_and_queries(st)
                    if st.k:
                        st.wait("pt0", 1)
                        turn(st, 2)
                    if st.f:
                        values(st)
                    if st.k:
                        heads(st)
                    if st.m:
                        st.wait("xn2", 2)
                        hidden(st, 0)
                        hidden(st, 1)
                    if st.k:
                        heads_turned(st)
                    if st.f:
                        scores(st, 0)
                    if st.m:
                        st.wait("gelu_0", 2)
                        hidden(st, 2)
                    if st.k:
                        project(st)
                    if st.m:
                        for j in range(HB):
                            if j == 0:
                                st.wait("gelu_1", 2)
                            if j == 2:
                                st.wait("gelu_2", 2)
                            mm = pe.matmul(bank(6)[0:C, 0:CH], W2[:, j, :], Hd[:, st.u, j], start=(j == 0), stop=(j == HB - 1))
                        mm.then_inc(s["fc2"], 1)
                    if st.f:
                        scores(st, 1)
                    if st.m and kind == "L1":
                        st.wait("x2", 2)
                        norm(st, X2[:, st.u], 7, IJ, "xc3")
                        st.wait("sq3", 2)
                        norm(st, SQ3[:, st.u], 6, J, "var3")
                    if st.m and kind == "L3":
                        hold(pe, s["x2"], st.value(2), passed)
                        for k in range(WS):
                            mm = pe.transpose(bank(7 - k // 5)[0:W, (k % 5) * C:(k % 5 + 1) * C],
                                              X2[:, st.u, k * W:(k + 1) * W], ident[0:C, 0:C])
                        mm.then_inc(s["yt"], 1)

                def attention_step(st):
                    if st.f:
                        st.wait("xn", 0)
                        st.wait("centred0", 1)
                        keys_and_queries(st)
                    if st.k:
                        st.wait("x1", 2)
                        st.wait("probs0", 1)
                        turn(st, 0)
                        st.wait("probs1", 1)
                        turn(st, 1)
                        turn(st, 2)
                    if st.f:
                        values(st)
                    if st.k:
                        heads(st)
                    if st.f:
                        scores(st, 0)
                    if st.k:
                        heads_turned(st)
                    if st.f:
                        scores(st, 1)
                    if st.k:
                        project(st)

                over_chunks(pe, s, mlp_step if mlp else attention_step, LAST)

            @block.scalar
            def _(act):
                LOG_EXP = "natural_log_exp_and_others"

                def square(st, lag, n, dst, k):
                    st.wait("xc" + n, lag)
                    act.activation(dst, bank(k)[0:C, 0:CH], ACT.Square).then_inc(s["sq" + n], 1)

                def rstd(st, lag, n, lv, rs, k):
                    st.wait("var" + n, lag)
                    act.activation(lv, bank(k)[0:C, 0:CH], ACT.Ln, bias=eps[:, 0:1]).then_inc(s["lv" + n], 1)
                    st.wait("lv" + n, lag)
                    act.activation(rs, lv, ACT.Exp, scale=-0.5).then_inc(s["rstd" + n], 1)

                def pt_copy(st, a):
                    st.wait(f"turned{a}", 1)
                    act.copy(PT[:, st.v, 4 * a:4 * a + 4, :].rearrange("c k q -> c (k q)"), bank(TURN[a])[0:SPAN, 0:4 * SPAN]).then_inc(s[f"pt{a}"], 1)

                def queries(st):
                    st.wait("q", 0)
                    act.mul(QT[:, st.u], bank(0)[0:C, 0:CH], HD ** -0.5).then_inc(s["qt"], 1)

                def values_even(st):
                    st.wait("v", 0)
                    act.copy(VB[0:TOK, st.u, :, :, 0:HD].rearrange("c q g d -> c (q g) d"),
                             bank(2)[0:TOK, 0:NWIN * G * HD].rearrange("c (k d) -> c k d", d=HD)).then_inc(s["v_even"], 1)

                def probs(st, half):
                    st.wait(f"centred{half}", 0)
                    a = slice(12 * half, 12 * half + 12)
                    act.activation(PR[:, st.u, a, 0:TOK], SX[:, st.u, a], ACT.Exp).then_inc(s[f"probs{half}"], 1)

                def mlp_step(st):
                    if st.f:
                        square(st, 0, "", SQ[:, st.u], 0)
                    if st.m:
                        square(st, 2, "2", SQ2[:, st.u], 6)
                    if st.f:
                        rstd(st, 0, "", LV[:, st.u], RS[:, st.u], 1)
                    if st.m:
                        rstd(st, 2, "2", LV2[:, st.u], RS2[:, st.u], 7)
                    if st.k:
                        pt_copy(st, 1)
                    if st.f:
                        queries(st)
                    if st.k:
                        pt_copy(st, 2)
                    if st.f:
                        values_even(st)
                    if st.m:
                        for j in (0, 1):
                            st.wait(f"fc1_{j}", 2)
                            act.activation(Hd[:, st.u, j], bank((7, 6, 7)[j])[:, 0:CH], ACT.Gelu).then_inc(s[f"gelu_{j}"], 1)
                    if st.k:
                        st.wait("heads_t", 1)
                        act.copy(OT[0:C, st.v].rearrange("c (k e q) -> c k e q", k=PAIRS, e=2), window_columns(bank(OT_BANK))).then_inc(s["ot"], 1)
                    if st.m:
                        st.wait("fc1_2", 2)
                        act.activation(Hd[:, st.u, 2], bank(7)[:, 0:CH], ACT.Gelu).then_inc(s["gelu_2"], 1)
                        act.preload_act_table_set(LOG_EXP)
                    if st.f:
                        probs(st, 0)
                    if st.m and kind == "L1":
                        square(st, 2, "3", SQ3[:, st.u], 7)
                        rstd(st, 2, "3", LV3[:, st.u], RS3[:, st.u], 6)
                    if st.f:
                        probs(st, 1)
                    if st.m and kind == "L1":
                        st.wait("xh", 2)
                        st.wait_turn(stored[st.u], 4, N_STORES)
                        act.activation(XA[:, st.u], XH[:, st.u], ACT.Identity, bias=gb[:, 6:7], scale=gb[:, 5:6]).then_inc(s["xa"], 1)

                def attention_step(st):
                    if st.f:
                        queries(st)
                    if st.k:
                        pt_copy(st, 1)
                        pt_copy(st, 2)
                    if st.f:
                        values_even(st)
                        probs(st, 0)
                        probs(st, 1)

                act.preload_act_table_set(LOG_EXP)
                over_chunks(act, s, mlp_step if mlp else attention_step, LAST)

            @block.vector
            def _(dve):
                def keys(st):
                    st.wait("k", 0)
                    dve.tensor_copy(KT[:, st.u], bank(1)[0:C, 0:CH]).then_inc(s["kt"], 1)
                    st.wait("kt", 0)
                    for h in range(HEADS):
                        ins = dve.tensor_scalar(KX[:, st.u, h], KT[:, st.u], mask6[:, h:h + 1], None, ALU.mult)
                    ins.then_inc(s["kx"], 1)

                def values_odd(st):
                    st.wait("v", 0)
                    dve.tensor_copy(VB[HALF:SPAN, st.u, :, :, HD:2 * HD].rearrange("c q g d -> c (q g) d"),
                                    bank(2)[HALF:SPAN, 0:NWIN * G * HD].rearrange("c (k d) -> c k d", d=HD)).then_inc(s["v_odd"], 1)

                def centre(st, half):
                    rr = st.place(0)[1] if kind == "L2" else None
                    st.wait(f"scores{half}", 0)
                    src = PS[0:SPAN, 2 * half:2 * half + 2, 0:HEADS * TOK]
                    a = slice(12 * half, 12 * half + 12)
                    mx = MX[:, st.u, half]
                    dst = SX[:, st.u, a]
                    if kind == "L2":
                        bias = BIAS[:, rr, a] if st.static else BIAS[:, bass.ds(rr, 1), a].rearrange("c o k t -> c (o k) t")
                        dve.tensor_tensor(SR[:, st.u, a].rearrange("c (k h) t -> c k (h t)", k=2), src,
                                          bias.rearrange("c (k h) t -> c k (h t)", k=2), ALU.add).then_inc(s[f"biased{half}"], 1)
                        st.wait(f"biased{half}", 0)
                        src = SR[:, st.u, a]
                        spread = mx.unsqueeze(2).broadcast_to([SPAN, 2 * HEADS, TOK])
                    else:
                        src = src.rearrange("c k (h t) -> c k h t", h=HEADS)
                        dst = dst.rearrange("c (k h) t -> c k h t", k=2)
                        mx = mx.rearrange("c (k h) -> c k h", k=2)
                        spread = mx.unsqueeze(3).broadcast_to([SPAN, 2, HEADS, TOK])
                    dve.tensor_reduce(mx, src, AX.X, ALU.max).then_inc(s[f"rowmax{half}"], 1)
                    st.wait(f"rowmax{half}", 0)
                    dve.tensor_tensor(dst, src, spread, ALU.subtract).then_inc(s[f"centred{half}"], 1)

                def pt_copy(st, a):
                    st.wait(f"turned{a}", 1)
                    dve.tensor_copy(PT[:, st.v, 4 * a:4 * a + 4, :].rearrange("c k q -> c (k q)"), bank(TURN[a])[0:SPAN, 0:4 * SPAN]).then_inc(s[f"pt{a}"], 1)

                def over_sums(st):
                    st.wait("heads", 1)
                    ho = bank(HEADS_BANK)[0:SPAN, 0:PAIRS * G * VW].rearrange("c (k n) -> c k n", n=VW)
                    dve.reciprocal(RSUM[:, st.v], ho[:, :, 2 * HD:VW]).then_inc(s["rsum"], 1)
                    st.wait("rsum", 1)
                    dve.tensor_tensor(O[:, st.v].rearrange("c k (g e d) -> c (k g) e d", g=G, e=2),
                                      ho[:, :, 0:2 * HD].rearrange("c k (e d) -> c k e d", e=2),
                                      RSUM[:, st.v].unsqueeze(3).broadcast_to([SPAN, PAIRS * G, 2, HD]), ALU.mult).then_inc(s["normed"], 1)

                def residual(st):
                    st.wait("proj", 1)
                    if kind == "L2":
                        st.wait_turn(stored[st.v], 3, N_STORES)
                    dve.tensor_tensor(win(X1[:, st.v]), seen(bank(PROJ_BANK)[0:C, 0:CH]), win(X[:, st.v]), ALU.add).then_inc(s["x1"], 1)

                def mlp_step(st):
                    if st.k:
                        pt_copy(st, 0)
                    if st.f:
                        st.wait("rstd", 0)
                        dve.tensor_tensor(seen(XN[0:C, st.u]), win(bank(0)[0:C, 0:CH]), win(RS[:, st.u]), ALU.mult).then_inc(s["xn"], 1)
                    if st.m:
                        st.wait("rstd2", 2)
                        dve.tensor_tensor(XN2[0:C, st.u], bank(6)[0:C, 0:CH], RS2[:, st.u], ALU.mult).then_inc(s["xn2"], 1)
                    if st.f:
                        keys(st)
                        values_odd(st)
                    if st.k:
                        over_sums(st)
                    if st.f:
                        centre(st, 0)
                    if st.k:
                        residual(st)
                    if st.m:
                        st.wait("fc2", 2)
                        if kind == "L1":
                            st.wait_turn(stored[st.u], 4, N_STORES)
                        dve.scalar_tensor_tensor(X2[:, st.u], bank(6)[0:C, 0:CH], gb[:, 4:5], X1[:, st.u], ALU.add, ALU.add).then_inc(s["x2"], 1)
                    if st.f:
                        centre(st, 1)
                    if st.m and kind == "L1":
                        st.wait("rstd3", 2)
                        dve.tensor_tensor(XH[:, st.u], bank(7)[0:C, 0:CH], RS3[:, st.u], ALU.mult).then_inc(s["xh"], 1)
                    if st.m and kind == "L3":
                        st.wait("yt", 2)
                        st.wait_turn(stored[st.u], 4, N_STORES)
                        dve.tensor_copy(Y[:, st.u, 0:5, :].rearrange("c k n -> c (k n)"), bank(7)[0:W, 0:5 * C])
                        dve.tensor_copy(Y[:, st.u, 5:7, :].rearrange("c k n -> c (k n)"), bank(6)[0:W, 0:2 * C]).then_inc(s["y"], 1)

                def attention_step(st):
                    if st.f:
                        keys(st)
                    if st.k:
                        pt_copy(st, 0)
                    if st.f:
                        values_odd(st)
                    if st.k:
                        over_sums(st)
                    if st.f:
                        centre(st, 0)
                    if st.k:
                        st.wait("heads_t", 1)
                        st.wait_turn(loaded[st.v], 1, N_LOADS)
                        for e in range(2):
                            ins = dve.tensor_tensor(seen(OT[0:C, st.v])[:, e::2], parity_windows(bank(OT_BANK), e), win(DW[:, st.v])[:, e::2], ALU.add)
                        ins.then_inc(s["ot"], 1)
                    if st.f:
                        centre(st, 1)
                    if st.k:
                        residual(st)

                over_chunks(dve, s, mlp_step if mlp else attention_step, LAST)

            if kind == "L2":
                @block.gpsimd
                def _(pool):
                    def to_windows(st, lag, u):
                        st.wait("v", lag + 2)
                        c = st.t - lag
                        hold(pool, norm_loaded[u], (c // 2 + 1) * 16, passed)
                        pool.tensor_copy(seen(XN[0:C, u]), win(XR[:, u])).then_inc(s["xn"], 1)

                    def step(st):
                        if not st.static or st.t + 1 < NCH:
                            to_windows(st, -1, st.v)

                    to_windows(Step(pool, s, 0, 0, True), 0, 0)
                    over_chunks(pool, s, step, LAST)


CG, CR = 6, 14
CK = CR + 6
NG, NBK = C // CG, H // CR
IMG = 8
NIG = B // IMG


def conv_pass(nc, PS, w, xn, cv, store_sems):
    KP, MP = CG * CK, CG * CR
    with ExitStack() as ctx:
        sb = lambda name, shape: ctx.enter_context(nc.sbuf_tensor("conv_" + name, shape, F32))
        sem = ctx.enter_context(semaphores(nc, "conv"))
        WB = sb("WB", [KP, 2, 7, MP]); T = sb("T", [KP, NIG, IMG, PW]); D = sb("D", [MP, NIG, IMG, W])
        BM = sb("BM", [KP, 7, MP]); WC = sb("WC", [KP, NG, 49])
        load_all(nc, "conv", [(BM[:], w["band_mask"])]
                 + [(WC[c * CK:(c + 1) * CK], w["dw_by_channel"].rearrange("(g c) t -> c g t", c=CG)[c:c + 1].broadcast_to([CK, NG, 49]))
                    for c in range(CG)], zeros=[T[:]])
        band_step, band_ready = sem("band_step"), sem("band_ready")
        loaded = [sem(f"loaded{k}") for k in range(NIG)]
        product, read = sem("product"), sem("read")
        stored, out_free = store_sems, sem("out_free")
        passed = sem("passed")
        PER = NBK * NIG
        CREDIT = PER + 1
        with nc.Block() as block:
            @block.vector
            def _(dve):
                with dve.Fori(0, NG // 2) as gg:
                    for e in range(2):
                        dve.wait_ge(product, gg * (2 * PER) + (PER * e + 1))
                        for kh in range(7):
                            for kw in range(7):
                                tap = WC[:, bass.ds(gg * 2 + e, 1), kh * 7 + kw:kh * 7 + kw + 1].rearrange("p a b -> p (a b)")
                                if kh == 0:
                                    ins = dve.tensor_scalar(WB[:, e, kw, :], BM[:, kh, :], tap, None, ALU.mult)
                                else:
                                    ins = dve.scalar_tensor_tensor(WB[:, e, kw, :], BM[:, kh, :], tap, WB[:, e, kw, :], ALU.mult, ALU.add)
                            ins.then_inc(band_step if kh < 6 else band_ready, 1)
                            if kh < 6:
                                dve.wait_ge(band_step, gg * 12 + (6 * e + kh + 1))

            @block.sync
            def _(sp):
                sp.sem_inc(product, CREDIT)
                with sp.Fori(0, NG // 2) as gg:
                    for e in range(2):
                        with sp.Fori(0, NBK) as blk:
                            for k in range(NIG):
                                sp.wait_ge(product, gg * (2 * PER) + blk * NIG + (PER * e + k + 1 + CREDIT - NIG))
                                for im in range(IMG):
                                    src = xn[k * IMG + im, bass.ds(gg * (2 * CG) + e * CG, CG), bass.ds(blk * CR, CK), :]
                                    sp.dma_start(T[:, k, im, 3:3 + W], src).then_inc(loaded[k], 16)

            @block.tensor
            def _(pe):
                with pe.Fori(0, NG // 2) as gg:
                    for e in range(2):
                        hold(pe, band_ready, gg * 2 + (e + 1), passed)
                        with pe.Fori(0, NBK) as blk:
                            for k in range(NIG):
                                pe.wait_ge(loaded[k], gg * (2 * NBK * 16 * IMG) + blk * (16 * IMG) + (NBK * e + 1) * 16 * IMG)
                                pe.wait_ge(read, gg * (2 * PER) + blk * NIG + (PER * e + k + 1))
                                for kw in range(7):
                                    mm = pe.matmul(PS[0:MP, k, 0:IMG * W].rearrange("m (i q) -> m i q", i=IMG), WB[:, e, kw, :],
                                                   T[:, k, :, kw:kw + W], start=(kw == 0), stop=(kw == 6))
                                mm.then_inc(product, 1)

            @block.scalar
            def _(act):
                act.sem_inc(read, NIG)
                act.sem_inc(out_free, NIG)
                with act.Fori(0, NG) as g:
                    with act.Fori(0, NBK) as blk:
                        for k in range(NIG):
                            act.wait_ge(product, g * PER + blk * NIG + (k + 1 + CREDIT))
                            act.wait_ge(out_free, g * PER + blk * NIG + (k + 1))
                            act.copy(D[:, k].rearrange("m i q -> m (i q)"), PS[0:MP, k, 0:IMG * W]).then_inc(read, 1)

            @block.gpsimd
            def _(pool):
                with pool.Fori(0, NG) as g:
                    with pool.Fori(0, NBK) as blk:
                        for k in range(NIG):
                            pool.wait_ge(read, g * PER + blk * NIG + (k + 1 + NIG))
                            for im in range(IMG):
                                pool.dma_start(cv[k * IMG + im, bass.ds(g * CG, CG), bass.ds(blk * CR, CR), :], D[:, k, im]).then_inc(stored[k], 16)
                        for k in range(NIG):
                            pool.wait_ge(stored[k], g * (NBK * 16 * IMG) + blk * (16 * IMG) + 16 * IMG)
                            pool.sem_inc(out_free, 1)


def clear_margin(nc, xn):
    with semaphores(nc, "margin") as sem, nc.sbuf_tensor("margin_zero", [C, B * 3 * W], F32) as zero:
        zeroed, cleared = sem("zeroed"), sem("cleared")
        with nc.Block() as block:
            @block.vector
            def _(dve):
                dve.memset(zero[:], 0.0).then_inc(zeroed, 1)

            @block.sync
            def _(sp):
                sp.wait_ge(zeroed, 1)
                for rows in (slice(0, 3), slice(3 + H, 6 + H)):
                    sp.dma_start(xn[:, :, rows, :].rearrange("b c h q -> c b (h q)"),
                                 zero[:].rearrange("c (b n) -> c b n", b=B)).then_inc(cleared, 16)
                sp.wait_ge(cleared, 32)


def build(nc, w, x, out):
    xa = nc.dram_tensor("after_L0", [B, C, H, W], F32).ap()
    xb = nc.dram_tensor("after_L1", [B, C, H, W], F32).ap()
    xn = nc.dram_tensor("L2_norm", [B, C, H + 6, W], F32).ap()
    cv = nc.dram_tensor("L2_conv", [B, C, H, W], F32).ap()
    xc = nc.dram_tensor("after_L2", [B, C, H, W], F32).ap()
    with ExitStack() as ctx:
        PS = ctx.enter_context(nc.psum_tensor("banks", [128, 8, 512], F32))
        stores = lambda name, n: [ctx.enter_context(nc.semaphore(f"{name}_stored{k}")) for k in range(n)]
        clear_margin(nc, xn)
        scan_pass(nc, PS, w, x, xa, stores("scan", 1))
        window_pass(nc, PS, w, "L1", dict(qkv_w=w["L1_conv_w_qkv"], qkv_b=w["L1_conv_b_qkv"], proj_w=w["L1_conv_w_proj"], proj_b=w["L1_conv_b_proj"],
                                          g1=w["L1_conv_g1"], b1=w["L1_conv_b1"], g2=w["L1_conv_g2"], b2=w["L1_conv_b2"], fc1_w=w["L1_conv_w_fc1"],
                                          fc1_b=w["L1_conv_b_fc1"], fc2_w=w["L1_conv_w_fc2"], fc2_b=w["L1_conv_b_fc2"]), xa, xb, xn_io=xn)
        conv_pass(nc, PS, w, xn, cv, stores("conv", NIG))
        window_pass(nc, PS, w, "L2", dict(qkv_w=w["L2_conv_qkv_w"], qkv_b=w["L2_conv_qkv_b"], proj_w=w["L2_conv_proj_w"], proj_b=w["L2_conv_proj_b"],
                                          dw_b=w["L2_conv_dw_b"], rpb=w["rpb"], mask=w["mask"]), xb, xc, xn_io=xn[:, :, 3:3 + H, :], conv=cv)
        window_pass(nc, PS, w, "L3", dict(qkv_w=w["L3_conv_qkv_w"], qkv_b=w["L3_conv_qkv_b"], proj_w=w["L3_conv_proj_w"], proj_b=w["L3_conv_proj_b"],
                                          g1=w["L3_conv_ln1_w"], b1=w["L3_conv_ln1_b"], g2=w["L3_conv_ln2_w"], b2=w["L3_conv_ln2_b"], fc1_w=w["L3_conv_mlp_w1"],
                                          fc1_b=w["L3_conv_mlp_b1"], fc2_w=w["L3_conv_mlp_w2"], fc2_b=w["L3_conv_mlp_b2"]), xc, out)


def position_index():
    i = np.arange(TOK)
    dy = i[:, None] // WS - i[None, :] // WS + WS - 1
    dx = i[:, None] % WS - i[None, :] % WS + WS - 1
    return dy * (2 * WS - 1) + dx


def kernel(**inputs):
    import concourse.bacc as bacc
    from concourse.bass_utils import run_bass_kernel_spmd

    a = {k: np.ascontiguousarray(v) for k, v in inputs.items()}
    a["L2_conv_qkv_w"] = np.ascontiguousarray(a["L2_conv_qkv_w"].T)
    a["L2_conv_proj_w"] = np.ascontiguousarray(a["L2_conv_proj_w"].T)
    a["dw_taps"] = np.ascontiguousarray(a.pop("L0_conv_dw_w")[:, 0, :].T)
    a["rpb"] = np.ascontiguousarray(a.pop("L2_conv_rpb_table")[position_index()].transpose(0, 2, 1))
    a["mask"] = np.ascontiguousarray(a.pop("L2_conv_mask_matrix").reshape(NROW, PAIRS, 2, TOK, TOK).transpose(2, 3, 0, 1, 4))
    a["dw_by_channel"] = np.ascontiguousarray(a.pop("L2_conv_dw_w").reshape(49, C).T)
    feeds = np.zeros((CG, CK, 7, CG, CR), np.float32)
    for kh in range(7):
        for a_ in range(CR):
            feeds[np.arange(CG), a_ + kh, kh, np.arange(CG), a_] = 1.0
    a["band_mask"] = feeds.reshape(CG * CK, 7, CG * CR)
    a["ident"] = np.eye(128, dtype=np.float32)
    a["head_mask"] = np.repeat(np.eye(HEADS, dtype=np.float32), HD, axis=0)
    nc = bacc.Bacc("TRN2", target_bir_lowering=False, num_devices=1)
    arrays, aps = {}, {}
    for name, v in a.items():
        arrays["in_" + name] = v
        aps[name] = nc.dram_tensor("in_" + name, v.shape, F32, kind="ExternalInput").ap()
    out = nc.dram_tensor("out", [B, H, W, C], F32, kind="ExternalOutput").ap()
    build(nc, aps, aps["x"], out)
    return run_bass_kernel_spmd(nc, [arrays], core_ids=[0]).results[0]["out"]
```

```python
from contextlib import ExitStack, contextmanager

import numpy as np

import concourse.bass as bass
from concourse import mybir

F32 = mybir.dt.float32
ALU = mybir.AluOpType
ACT = mybir.ActivationFunctionType
AX = mybir.AxisListType

B, H, W, C = 32, 56, 56, 96
WS, SHIFT, HEADS = 7, 3, 6
HD = C // HEADS
TOK = WS * WS
NWIN = W // WS
NROW = H // WS
CH = WS * W
PAIRS = NWIN // 2
G = HEADS // 2
HALF = 64
SPAN = HALF + TOK
HID = 4 * C
HB = HID // 128
VW = 2 * HD + 2
NCH = B * NROW
EPS = 1e-5
PW = W + 6

def hold(eng, sem, value, passed):
    eng.wait_ge(sem, value)
    eng.sem_inc(passed, 1)


@contextmanager
def semaphores(nc, prefix):
    given = []
    with ExitStack() as ctx:
        def sem(name):
            given.append(ctx.enter_context(nc.semaphore(f"{prefix}_{name}")))
            return given[-1]

        yield sem
        with nc.Block() as block:
            @block.gpsimd
            def _(pool):
                for q in given:
                    pool.sem_clear(q)


def fold_affine(nc, name, raw, bias_row, gamma, beta, ps, pieces):
    n = raw.shape[1]
    with semaphores(nc, name) as sem:
        product_ready = sem("product_ready")
        with nc.Block() as block:
            if beta is not None:
                @block.tensor
                def _(pe):
                    pe.matmul(ps[C:C + 1, 0:n], beta, raw, start=True, stop=True).then_inc(product_ready, 1)

            @block.vector
            def _(dve):
                for target, view in pieces:
                    if gamma is not None:
                        dve.tensor_scalar(target[0:C], view(raw), gamma, None, ALU.mult)
                    else:
                        dve.tensor_copy(target[0:C], view(raw))
                if beta is not None:
                    dve.wait_ge(product_ready, 1)
                for target, view in pieces:
                    if beta is not None:
                        dve.tensor_tensor(target[C:C + 1], view(bias_row), view(ps[C:C + 1, 0:n]), ALU.add)
                    else:
                        dve.tensor_copy(target[C:C + 1], view(bias_row))


def centre_outputs(nc, name, weights, bias_row=None, bias_column=None, one=None, ps=None):
    tiles = weights + ([bias_row] if bias_row is not None else [])
    with semaphores(nc, name) as sem:
        summed, averaged, centred, column_ready = sem("summed"), sem("averaged"), sem("centred"), sem("column_ready")
        passed = sem("passed")
        with nc.Block() as block:
            @block.vector
            def _(dve):
                for t in tiles:
                    dve.tensor_reduce(t[:, C:C + 1], t[:, 0:C], AX.X, ALU.add).then_inc(summed, 1)
                dve.wait_ge(summed, len(tiles))
                for t in tiles:
                    dve.tensor_scalar(t[:, C:C + 1], t[:, C:C + 1], 1.0 / C, None, ALU.mult).then_inc(averaged, 1)
                dve.wait_ge(averaged, len(tiles))
                for t in tiles:
                    dve.tensor_scalar(t[:, 0:C], t[:, 0:C], t[:, C:C + 1], None, ALU.subtract).then_inc(centred, 1)
                if bias_row is not None:
                    dve.wait_ge(column_ready, 1)
                    dve.tensor_copy(bias_column, ps[0:C + 1, 0:1])

            if bias_row is not None:
                @block.tensor
                def _(pe):
                    hold(pe, centred, len(tiles), passed)
                    pe.matmul(ps[0:C + 1, 0:1], bias_row, one, start=True, stop=True).then_inc(column_ready, 1)


def load_all(nc, name, pairs, zeros=(), ones=(), values=()):
    with semaphores(nc, name) as sem:
        weights_loaded = sem("weights_loaded")
        with nc.Block() as block:
            @block.sync
            def _(sp):
                for dst, src in pairs:
                    sp.dma_start(dst, src).then_inc(weights_loaded, 16)
                sp.wait_ge(weights_loaded, 16 * len(pairs))

            @block.vector
            def _(dve):
                for t in zeros:
                    dve.memset(t, 0.0)
                for t in ones:
                    dve.memset(t, 1.0)
                for t, v in values:
                    dve.memset(t, v)


def column(v):
    return v.rearrange("(c o) -> c o", o=1)


def row(v):
    return v.rearrange("(o c) -> o c", o=1)


def scan_pass(nc, PS, w, x, xa):
    RB = 8
    TB = RB * W
    NB = H // RB
    NGR = (NB + 1) // 2
    S = H * W
    TP = S // 112
    SLOTS = 2 * NB
    GY = C + 2
    MEAN_BEFORE, MEAN_BEHIND = {0: 0, 1: 1}, {2: 2, 3: 3}
    VAR_BEHIND = {1: 0, 2: 1, 4: 2, 5: 3}
    TURN_SLOTS, DIFFS, SUMS, SCORE, SEL1, SEL2, FLAG = (7, 8), 7, 8, 9, 10, 11, 12
    with ExitStack() as ctx:
        sb = lambda name, shape: ctx.enter_context(nc.sbuf_tensor("scan_" + name, shape, F32))
        sem = ctx.enter_context(semaphores(nc, "scan"))
        raw = sb("raw", [C, 2 * C]); brow = sb("brow", [128, 2 * C])
        gcol = sb("gcol", [C, 1]); becol = sb("becol", [C, 1]); fc2row = sb("fc2row", [1, C + 1]); fc2b = sb("fc2b", [C + 1, 1])
        gmean = sb("gmean", [C, 1])
        dwb = sb("dwb", [C, 2]); taps = sb("taps", [128, 3, 2 * C])
        W1 = sb("W1", [128, 2 * C]); W1T = sb("W1T", [128, 3, 2 * C])
        W2 = sb("W2", [C, 2, C + 1]); CM = sb("CM", [C, GY]); J = sb("J", [C, GY]); ident = sb("ident", [128, 128])
        eps = sb("eps", [GY, 1]); one1 = sb("one1", [1, C])
        sw1 = sb("sw1", [4, 16]); sb1 = sb("sb1", [16, 1]); sw2 = sb("sw2", [16, 4]); sb2 = sb("sb2", [1, 4])
        XT = sb("XT", [112, TP, C]); X = sb("X", [C, S])
        XM = sb("XM", [GY, 2, S]); XN = sb("XN", [GY, S]); XS = sb("XS", [C + 1, 2, S + 2])
        SQ = sb("SQ", [C, 2, 2 * TB]); LV = sb("LV", [GY, 2, 2 * TB]); RS = sb("RS", [GY, 2, 2 * TB])
        GH = sb("GH", [H, W]); GN = sb("GN", [H, W])
        DH = sb("DH", [H, W]); DV = sb("DV", [H, W]); JH = sb("JH", [H, W]); JV = sb("JV", [H, W]); GA = sb("GA", [H, 4])
        gone = sb("gone", [H, 1])
        sc = sb("sc", [4, 1]); hid = sb("hid", [16, 1]); lg = sb("lg", [1, 4]); st = sb("st", [1, 16])
        pr = sb("pr", [1, 4]); fl = sb("fl", [1, 2]); fb = sb("fb", [C, 2])
        Hd = sb("Hd", [C, 2, 2, TB]); OUT = sb("OUT", [C + 1, 2, RB, W])

        load_all(nc, "scan", [
            (raw[:], w["L0_conv_fc1_w"]), (brow[C:C + 1, :], row(w["L0_conv_fc1_b"])),
            (gcol[:], column(w["L0_conv_gamma"])), (becol[:], column(w["L0_conv_beta"])),
            (fc2row[:, 0:C], row(w["L0_conv_fc2_b"])), (dwb[:, 0:1], column(w["L0_conv_dw_b"][0:C])), (dwb[:, 1:2], column(w["L0_conv_dw_b"][C:2 * C])),
            (W2[:, :, 0:C], w["L0_conv_fc2_w"].rearrange("(h c) n -> c h n", h=2)), (ident[:], w["ident"]),
            (sw1[:], w["L0_conv_sel_w1"]), (sb1[:], column(w["L0_conv_sel_b1"])),
            (sw2[:], w["L0_conv_sel_w2"]), (sb2[:], row(w["L0_conv_sel_b2"]))]
            + [(taps[0:C + 1, t, :], w["dw_taps"][t:t + 1, :].broadcast_to([C + 1, 2 * C])) for t in range(3)],
            zeros=[XS[:], GA[:]], ones=[PS[:], one1[:]],
            values=[(J[:], 1.0 / C), (CM[:], 1.0 / C), (eps[:], EPS), (gone[:], 1.0 / (H * (W - 1)))])
        fold_affine(nc, "scan_fc1", raw[:], brow[C:C + 1, :], gcol[:, 0:1], becol[:, 0:1], PS[:, 0, :],
                    [(W1[0:C + 1, :], lambda t: t)])
        centre_outputs(nc, "scan_fc2", [W2[:, 0], W2[:, 1]], fc2row[:], fc2b[:], one1[:, 0:1], PS[:, 2, :])
        gamma_mean, gamma_out = sem("gamma_mean"), sem("gamma_out")
        with nc.Block() as block:
            @block.tensor
            def _(pe):
                pe.matmul(PS[0:C, 1, 0:1], J[:, 0:C], gcol[:, 0:1], start=True, stop=True).then_inc(gamma_mean, 1)

            @block.vector
            def _(dve):
                for t in range(3):
                    dve.tensor_tensor(W1T[0:C + 1, t, :], W1[0:C + 1, :], taps[0:C + 1, t, :], ALU.mult)
                for p in range(2):
                    dve.memset(XS[C:C + 1, p, 1:S + 1], 1.0)
                dve.tensor_tensor(CM[:, 0:C], ident[0:C, 0:C], J[:, 0:C], ALU.subtract)
                dve.wait_ge(gamma_mean, 1)
                dve.tensor_copy(gmean[:], PS[0:C, 1, 0:1]).then_inc(gamma_out, 1)
                dve.wait_ge(gamma_out, 1)
                dve.tensor_scalar(CM[:, C + 1:C + 2], gcol[:], gmean[:, 0:1], 1.0 / C, ALU.subtract, ALU.mult)

        s = {n: sem(n) for n in ("img_loaded", "turned", "x_ready", "mean", "xm", "sq", "var", "lv", "rstd",
                                 "xn", "grey_tiles", "diffs", "sums", "sums_ready", "score", "scores", "sel1", "hidden", "sel2",
                                 "dve_chain", "centred", "expo", "flag", "flagb", "flag_ready", "factors", "blend", "xs",
                                 "conv", "gelu", "fc2", "out")}
        stored, passed = [sem("stored0"), sem("stored1")], sem("passed")
        CHAIN = 8
        XTr = x.rearrange("b h w c -> b (h w) c").rearrange("b (p j) c -> b p j c", j=TP)
        blocks_of = lambda g: 2 if 2 * g + 1 < NB else 1
        cols_of = lambda g: slice(2 * g * TB, (2 * g + blocks_of(g)) * TB)

        def pick(t, p):
            return t[:, p] if isinstance(p, int) else t[:, bass.ds(p, 1)].rearrange("c o n -> c (o n)")

        def group_banks(g, rows):
            n = blocks_of(g)
            b0 = 2 * (g % 2)
            return PS[0:rows, b0:b0 + n, 0:TB]

        def over_images(eng, step):
            step(0, True, False, True)
            with eng.Fori(0, B - 2) as k:
                step(eng.snap(k + 1), True, True, True)
            step(B - 1, True, True, False)
            step(B, False, True, False)

        def parity(eng, i):
            return i % 2 if isinstance(i, int) else eng.snap(i % 2)

        def base(eng, v):
            return v if isinstance(v, int) else eng.snap(v)

        with nc.Block() as block:
            @block.sync
            def _(sp):
                def load(i):
                    sp.dma_start(XT[:], XTr[i]).then_inc(s["img_loaded"], 16)

                def store(c, m):
                    v = m % 2
                    sp.wait_ge(s["out"], c * (2 * NB) + 2 * (m + 1))
                    if m == 0:
                        sp.dma_start(xa[c, :, H - SHIFT:H, :], OUT[:, v, 0:SHIFT, :]).then_inc(stored[v], 16)
                        sp.dma_start(xa[c, :, 0:RB - SHIFT, :], OUT[:, v, SHIFT:RB, :]).then_inc(stored[v], 16)
                    else:
                        sp.dma_start(xa[c, :, m * RB - SHIFT:(m + 1) * RB - SHIFT, :], OUT[:, v]).then_inc(stored[v], 16)

                def step(i, norm, conv, turn):
                    c = base(sp, i - 1)
                    if conv:
                        store(c, 0)
                    if norm:
                        sp.wait_ge(s["xn"], i * NGR + NGR)
                        grey = XN[C + 1:C + 2, :]
                        sp.dma_start(GH[:], grey.rearrange("o (h w) -> o h w", w=W)).then_inc(s["grey_tiles"], 16)
                        sp.dma_start(GN[0:H - 1, :], XN[C + 1:C + 2, W:].rearrange("o (h w) -> o h w", w=W)).then_inc(s["grey_tiles"], 16)
                    if conv:
                        store(c, 1)
                    if turn:
                        sp.wait_ge(s["turned"], i * NB + 2 * NB)
                        load(base(sp, (i + 2) % B))
                    if conv:
                        for m in range(2, NB):
                            store(c, m)

                for q in stored:
                    sp.sem_inc(q, 16)
                load(0)
                sp.wait_ge(s["turned"], NB)
                load(1)
                over_images(sp, step)
                sp.wait_ge(s["img_loaded"], (B + 1) * 16)
                for v in range(2):
                    sp.wait_ge(stored[v], 16 + B * 16 * ((NB + 1) // 2 + 1 if v == 0 else NB // 2))

            @block.tensor
            def _(pe):
                def turn_block(n, m):
                    if m == 0:
                        pe.wait_ge(s["img_loaded"], n * 16 + 16)
                    if m >= 4:
                        pe.wait_ge(s["x_ready"], n * NB + (m - 3))
                    for j in range(4):
                        mm = pe.transpose(PS[0:C, m % 4, j * 112:(j + 1) * 112], XT[:, 4 * m + j, :], ident[0:112, 0:112])
                    mm.then_inc(s["turned"], 1)

                def mean(i, g):
                    if g == 0:
                        pe.wait_ge(s["x_ready"], i * NB + NB)
                        if not isinstance(i, int) or i >= 1:
                            pe.wait_ge(s["factors"], i)
                    if g >= 2:
                        pe.wait_ge(s["lv"], i * NGR + (g - 1))
                    for k in range(blocks_of(g)):
                        m = 2 * g + k
                        mm = pe.matmul(PS[0:GY, m % 4, 0:TB], CM[:], X[:, m * TB:(m + 1) * TB], start=True, stop=True)
                    mm.then_inc(s["mean"], 1)

                def variance(i, g):
                    pe.wait_ge(s["sq"], i * NGR + (g + 1))
                    for k in range(blocks_of(g)):
                        mm = pe.matmul(PS[0:GY, (2 * g + k) % 4, 0:TB], J[:], SQ[:, g % 2, k * TB:(k + 1) * TB], start=True, stop=True)
                    mm.then_inc(s["var"], 1)

                def conv_half(c, xs, k):
                    m, h = k // 2, k % 2
                    if h == 0:
                        pe.wait_ge(s["xs"], c * NB + min(m + 2, NB))
                    if k >= 3:
                        pe.wait_ge(s["gelu"], c * SLOTS + (k - 2))
                    elif not isinstance(c, int) or c >= 1:
                        pe.wait_ge(s["gelu"], c * SLOTS)
                    for t in range(3):
                        mm = pe.matmul(PS[0:C, 4 + k % 3, 0:TB], W1T[0:C + 1, t, h * C:(h + 1) * C],
                                       xs[:, m * TB + t:m * TB + t + TB], start=(t == 0), stop=(t == 2))
                    mm.then_inc(s["conv"], 1)

                def fc2_block(c, m):
                    pe.wait_ge(s["gelu"], c * SLOTS + 2 * (m + 1))
                    if m >= 1:
                        pe.wait_ge(s["out"], c * (2 * NB) + 2 * m)
                    elif not isinstance(c, int) or c >= 1:
                        pe.wait_ge(s["out"], c * (2 * NB))
                    for h in range(2):
                        mm = pe.matmul(PS[0:C + 1, 7, 0:TB], W2[:, h, :], Hd[:, m % 2, h], start=(h == 0), stop=(h == 1))
                    mm.then_inc(s["fc2"], 1)

                def step(i, norm, conv, turn):
                    c = base(pe, i - 1)
                    i1 = base(pe, i + 1)
                    xs = pick(XS, parity(pe, c)) if conv else None
                    for k in range(SLOTS):
                        if norm and k in MEAN_BEFORE:
                            mean(i, MEAN_BEFORE[k])
                        if turn:
                            if k == TURN_SLOTS[0]:
                                pe.wait_ge(s["lv"], i * NGR + NGR)
                                for m in range(4):
                                    turn_block(i1, m)
                            if k == TURN_SLOTS[1]:
                                for m in range(4, NB):
                                    turn_block(i1, m)
                        if norm:
                            if k == SCORE:
                                if turn:
                                    pe.wait_ge(s["x_ready"], i1 * NB + (NB - 1))
                                hold(pe, s["sums"], i1, passed)
                                pe.matmul(PS[0:4, 0, 0:1], GA[:], gone[:], start=True, stop=True).then_inc(s["score"], 1)
                            if k == SEL1:
                                hold(pe, s["scores"], i1, passed)
                                pe.matmul(PS[0:16, 1, 0:1], sw1[:], sc[:], start=True, stop=True).then_inc(s["sel1"], 1)
                            if k == SEL2:
                                hold(pe, s["hidden"], i1, passed)
                                pe.matmul(PS[0:1, 0, 0:4], hid[:], sw2[:], start=True, stop=True).then_inc(s["sel2"], 1)
                            if k == FLAG:
                                hold(pe, s["flag"], i1, passed)
                                pe.matmul(PS[0:C, 1, 0:2], one1[:], fl[:], start=True, stop=True).then_inc(s["flagb"], 1)
                        if conv:
                            conv_half(c, xs, k)
                            if k % 2 == 1 and k >= 3:
                                fc2_block(c, k // 2 - 1)
                        if norm and k in VAR_BEHIND:
                            variance(i, VAR_BEHIND[k])
                        if norm and k in MEAN_BEHIND:
                            mean(i, MEAN_BEHIND[k])
                    if conv:
                        fc2_block(c, NB - 1)

                for m in range(NB):
                    turn_block(0, m)
                over_images(pe, step)

            @block.scalar
            def _(act):
                LOG_EXP = "natural_log_exp_and_others"

                def step(i, norm, conv, turn):
                    c = base(act, i - 1)
                    i1 = base(act, i + 1)
                    if norm:
                        xm = pick(XM, parity(act, i))

                    def square(g):
                        act.wait_ge(s["xm"], i * NGR + (g + 1))
                        if g >= 2:
                            act.wait_ge(s["var"], i * NGR + (g - 1))
                        act.activation(SQ[:, g % 2, 0:blocks_of(g) * TB], xm[0:C, cols_of(g)], ACT.Square).then_inc(s["sq"], 1)

                    def rstd(g):
                        n = blocks_of(g) * TB
                        act.wait_ge(s["var"], i * NGR + (g + 1))
                        if g >= 2:
                            act.wait_ge(s["xn"], i * NGR + (g - 1))
                        act.activation(LV[:, g % 2, 0:n].rearrange("c (k n) -> c k n", n=TB), group_banks(g, GY), ACT.Ln, bias=eps[:, 0:1]).then_inc(s["lv"], 1)
                        act.wait_ge(s["lv"], i * NGR + (g + 1))
                        act.activation(RS[:, g % 2, 0:n], LV[:, g % 2, 0:n], ACT.Exp, scale=-0.5).then_inc(s["rstd"], 1)

                    for k in range(SLOTS):
                        if norm and k in MEAN_BEFORE:
                            square(MEAN_BEFORE[k])
                        if norm and k == SUMS:
                            act.wait_ge(s["diffs"], i * 2 + 2)
                            act.activation(JH[:, 0:W - 1], DH[:, 0:W - 1], ACT.Abs, accum_out=GA[:, 0:1])
                            act.activation(JV[0:H - 1, :], DV[0:H - 1, :], ACT.Abs, accum_out=GA[0:H - 1, 1:2]).then_inc(s["sums_ready"], 1)
                        if norm and k == SCORE:
                            act.wait_ge(s["score"], i1)
                            act.activation(sc[:], PS[0:4, 0, 0:1], ACT.Abs).then_inc(s["scores"], 1)
                        if norm and k == SEL1:
                            act.wait_ge(s["sel1"], i1)
                            act.activation(hid[:], PS[0:16, 1, 0:1], ACT.Relu, bias=sb1[:, 0:1]).then_inc(s["hidden"], 1)
                        if norm and k == SEL2:
                            act.wait_ge(s["centred"], i1)
                            act.activation(pr[:], lg[:], ACT.Exp).then_inc(s["expo"], 1)
                        if conv:
                            m, h = k // 2, k % 2
                            act.wait_ge(s["conv"], c * SLOTS + (k + 1))
                            if h == 0 and m >= 2:
                                act.wait_ge(s["fc2"], c * NB + (m - 1))
                            elif h == 0 and (not isinstance(c, int) or c >= 1):
                                act.wait_ge(s["fc2"], c * NB)
                            act.activation(Hd[:, m % 2, h], PS[0:C, 4 + k % 3, 0:TB], ACT.Gelu, bias=dwb[:, h:h + 1]).then_inc(s["gelu"], 1)
                            if norm and k in VAR_BEHIND:
                                act.preload_act_table_set(LOG_EXP)
                        if norm and k in VAR_BEHIND:
                            rstd(VAR_BEHIND[k])
                        if norm and k in MEAN_BEHIND:
                            square(MEAN_BEHIND[k])

                over_images(act, step)

            @block.vector
            def _(dve):
                Xv = X[:].rearrange("c (p j) -> c j p", j=TP)
                XNT = XN[0:C, :].rearrange("c (h w) -> c w h", w=W)

                def copy_turned(n, m):
                    dve.wait_ge(s["turned"], n * NB + (m + 1))
                    if m == 0 and (not isinstance(n, int) or n >= 1):
                        dve.wait_ge(s["mean"], n * NGR)
                    dve.tensor_copy(Xv[:, 4 * m:4 * m + 4, :], PS[0:C, m % 4, 0:TB].rearrange("c (j p) -> c j p", j=4)).then_inc(s["x_ready"], 1)

                def residual(c, xm, m):
                    v = m % 2
                    dve.wait_ge(s["fc2"], c * NB + (m + 1))
                    done = (m + 2) // 2 if m > 1 and v == 0 else m // 2
                    dve.wait_ge(stored[v], c * (16 * ((NB + 1) // 2 + 1 if v == 0 else NB // 2)) + 16 * (1 + done))
                    Xr = xm[0:C + 1, m * TB:(m + 1) * TB].rearrange("c (a q) -> c a q", q=W)
                    Pr = PS[0:C + 1, 7, 0:TB].rearrange("c (a q) -> c a q", q=W)
                    for dst, src in ((slice(0, W - SHIFT), slice(SHIFT, W)), (slice(W - SHIFT, W), slice(0, SHIFT))):
                        dve.scalar_tensor_tensor(OUT[:, v, :, dst], Pr[:, :, src], fc2b[:, 0:1], Xr[:, :, src],
                                                 ALU.add, ALU.add).then_inc(s["out"], 1)

                def step(i, norm, conv, turn):
                    c = base(dve, i - 1)
                    i1 = base(dve, i + 1)
                    k0 = base(dve, i * CHAIN)
                    chained = [0]

                    def link(ins):
                        chained[0] += 1
                        ins.then_inc(s["dve_chain"], 1)
                        dve.wait_ge(s["dve_chain"], k0 + chained[0])

                    if norm:
                        p = parity(dve, i)
                        xm, xs = pick(XM, p), pick(XS, p)
                    old = pick(XM, parity(dve, c)) if conv else None

                    def centred(g):
                        dve.wait_ge(s["mean"], i * NGR + (g + 1))
                        dve.tensor_copy(xm[:, cols_of(g)].rearrange("c (k n) -> c k n", n=TB), group_banks(g, GY)).then_inc(s["xm"], 1)

                    def normed(g):
                        dve.wait_ge(s["rstd"], i * NGR + (g + 1))
                        dve.tensor_tensor(XN[:, cols_of(g)], xm[:, cols_of(g)], RS[:, g % 2, 0:blocks_of(g) * TB], ALU.mult).then_inc(s["xn"], 1)

                    for k in range(SLOTS):
                        if norm and k in MEAN_BEFORE:
                            centred(MEAN_BEFORE[k])
                        if turn and k == TURN_SLOTS[0]:
                            for m in range(4):
                                copy_turned(i1, m)
                        if turn and k == TURN_SLOTS[1]:
                            for m in range(4, NB):
                                copy_turned(i1, m)
                        if norm and k == DIFFS:
                            dve.wait_ge(s["grey_tiles"], i * 32 + 32)
                            dve.tensor_tensor(DH[:, 0:W - 1], GH[:, 1:W], GH[:, 0:W - 1], ALU.subtract).then_inc(s["diffs"], 1)
                            dve.tensor_tensor(DV[0:H - 1, :], GN[0:H - 1, :], GH[0:H - 1, :], ALU.subtract).then_inc(s["diffs"], 1)
                        if norm and k == SUMS:
                            dve.wait_ge(s["sums_ready"], i1)
                            link(dve.tensor_tensor(GA[:, 2:3], GA[:, 0:1], GA[:, 1:2], ALU.add))
                            dve.tensor_scalar(GA[:, 2:3], GA[:, 2:3], 0.8, 0.5, ALU.mult, ALU.mult)
                            dve.tensor_tensor(GA[:, 3:4], GA[:, 0:1], GA[:, 1:2], ALU.subtract).then_inc(s["sums"], 1)
                        if norm and k == SEL2:
                            dve.wait_ge(s["sel2"], i1)
                            link(dve.tensor_tensor(st[:, 0:4], PS[0:1, 0, 0:4], sb2[:], ALU.add))
                            link(dve.tensor_reduce(st[:, 4:5], st[:, 0:4], AX.X, ALU.max))
                            dve.tensor_scalar(lg[:], st[:, 0:4], st[:, 4:5], None, ALU.subtract).then_inc(s["centred"], 1)
                            dve.wait_ge(s["expo"], i1)
                            link(dve.tensor_reduce(st[:, 5:6], pr[:], AX.X, ALU.add))
                            link(dve.reciprocal(st[:, 6:7], st[:, 5:6]))
                            link(dve.tensor_scalar(st[:, 8:12], pr[:], st[:, 6:7], None, ALU.mult))
                            dve.tensor_tensor(st[:, 12:13], st[:, 9:10], st[:, 8:9], ALU.is_gt)
                            link(dve.tensor_tensor(st[:, 13:14], st[:, 10:11], st[:, 11:12], ALU.max))
                            link(dve.tensor_tensor(st[:, 14:15], st[:, 9:10], st[:, 13:14], ALU.is_ge))
                            dve.tensor_tensor(fl[:, 0:1], st[:, 12:13], st[:, 14:15], ALU.mult).then_inc(s["flag_ready"], 1)
                            dve.wait_ge(s["flag_ready"], i1)
                            dve.tensor_scalar(fl[:, 1:2], fl[:, 0:1], -1.0, 1.0, ALU.mult, ALU.add).then_inc(s["flag"], 1)
                        if norm and k == FLAG:
                            dve.wait_ge(s["flagb"], i1)
                            dve.tensor_copy(fb[:], PS[0:C, 1, 0:2]).then_inc(s["factors"], 1)
                            dve.wait_ge(s["factors"], i1)
                        if conv and k % 2 == 1 and k >= 3:
                            residual(c, old, k // 2 - 1)
                        if norm and k >= FLAG:
                            for m in (range(NB // 2), range(NB // 2, NB))[k - FLAG]:
                                cols = slice(1 + m * TB, 1 + (m + 1) * TB)
                                dve.tensor_scalar(xs[0:C, cols], XN[0:C, m * TB:(m + 1) * TB], fb[:, 1:2], None, ALU.mult).then_inc(s["blend"], 1)
                                dve.wait_ge(s["blend"], i * NB + (m + 1))
                                target = xs[0:C, cols].rearrange("c (a q) -> c a q", q=H)
                                dve.scalar_tensor_tensor(target, XNT[:, m * RB:(m + 1) * RB, :], fb[:, 0:1], target, ALU.mult, ALU.add).then_inc(s["xs"], 1)
                        if norm and k in VAR_BEHIND:
                            normed(VAR_BEHIND[k])
                        if norm and k in MEAN_BEHIND:
                            centred(MEAN_BEHIND[k])
                    if conv:
                        residual(c, old, NB - 1)

                for m in range(NB):
                    copy_turned(0, m)
                over_images(dve, step)


class Step:

    def __init__(self, eng, sems, t, turn, static):
        self.eng, self.sems, self.static, self.turn = eng, sems, static, turn
        self.u, self.v = turn % 2, 1 - turn % 2
        self.t = t if static else eng.snap(t)
        self.f = not static or t < NCH
        self.k = not static or 1 <= t <= NCH
        self.m = not static or 2 <= t <= NCH + 1
        self.n = not static or 3 <= t
        self.count = {}

    def ahead(self):
        return Step(self.eng, self.sems, self.t + 1, self.turn + 1, self.static)

    def of4(self, lag):
        return (self.turn - lag) % 4

    def value(self, lag):
        if self.static:
            return self.t - lag + 1
        if lag not in self.count:
            self.count[lag] = self.eng.snap(self.t + (1 - lag)) if lag != 1 else self.t
        return self.count[lag]

    def wait(self, name, lag):
        if not self.static or self.value(lag) >= 1:
            self.eng.wait_ge(self.sems[name], self.value(lag))

    def wait_turn(self, sem, lag, per, buffers=2):
        c = self.t - lag
        if not self.static or c >= 0:
            self.eng.wait_ge(sem, (c // buffers + 1) * (16 * per))

    def place(self, lag):
        c = self.t - lag
        if self.static:
            return c // NROW, c % NROW
        c = self.eng.snap(c)
        return self.eng.snap(c // NROW), self.eng.snap(c % NROW)


FIRST = 6


def over_chunks(eng, sems, step, last):
    for t in range(FIRST):
        step(Step(eng, sems, t, t, True))
    with eng.Fori(0, (NCH - 2 - FIRST) // 4) as i:
        for j in range(4):
            step(Step(eng, sems, i * 4 + (FIRST + j), FIRST + j, False))
    for t in range(NCH - 2, NCH + last):
        step(Step(eng, sems, t, t, True))


def window_pass(nc, PS, w, kind, p, xin, xout, xn_io=None, conv=None):
    mlp = kind != "L2"
    LAST = 3 if mlp else 1
    N_STORES = 4 if kind == "L3" else 1
    with ExitStack() as ctx:
        sb = lambda name, shape: ctx.enter_context(nc.sbuf_tensor(f"{kind}_{name}", shape, F32))
        sem = ctx.enter_context(semaphores(nc, kind))
        ident = sb("ident", [128, 128]); mask6 = sb("mask6", [C, HEADS]); eps = sb("eps", [C, 1])
        J = sb("J", [C, C])
        rawq = sb("rawq", [C, 3 * C]); brow = sb("brow", [128, HID])
        Wq = sb("Wq", [128, C]); Wk = sb("Wk", [128, C]); Wv = sb("Wv", [128, 2, G, HD]); Wp = sb("Wp", [128, C + 1])
        rawp = sb("rawp", [C, C]); prow = sb("prow", [128, C]); gb = sb("gb", [C, 8])
        X = sb("X", [C + 1, 4, CH]); XN = sb("XN", [C + 1, 2, CH]); QT = sb("QT", [C, 2, CH]); KT = sb("KT", [C, 2, CH])
        KX = sb("KX", [C, 2, HEADS, CH]); VB = sb("VB", [SPAN, 2, NWIN, G, VW])
        MX = sb("MX", [SPAN, 2, 2, HEADS * 2]); SX = sb("SX", [SPAN, 2, PAIRS * HEADS, TOK])
        PR = sb("PR", [SPAN, 2, PAIRS * HEADS, HALF]); PT = sb("PT", [SPAN, 2, PAIRS * G, SPAN])
        RSUM = sb("RSUM", [SPAN, 2, PAIRS * G, 2]); O = sb("O", [SPAN, 2, PAIRS, C]); OT = sb("OT", [C + 1, 2, CH])
        X1 = sb("X1", [C + 1, 2, CH])
        if mlp:
            SQ = sb("SQ", [C, 2, CH]); LV = sb("LV", [C, 2, CH]); RS = sb("RS", [C, 2, CH])
            SQ2 = sb("SQ2", [C, 2, CH]); LV2 = sb("LV2", [C, 2, CH]); RS2 = sb("RS2", [C, 2, CH])
            raw1 = sb("raw1", [C, HID]); W1 = sb("W1", [128, HID]); W2 = sb("W2", [128, HB, C + 1])
            fc2row = sb("fc2row", [1, C + 1]); fc2b = sb("fc2b", [C + 1, 1]); one = sb("one", [1, 1])
            XN2 = sb("XN2", [C + 1, 2, CH]); Hd = sb("Hd", [128, 2, HB, CH]); X2 = sb("X2", [C + 1, 2, CH])
        if kind == "L1":
            SQ3 = sb("SQ3", [C, 2, CH]); LV3 = sb("LV3", [C, 2, CH]); RS3 = sb("RS3", [C, 2, CH])
            XH = sb("XH", [C, 2, CH]); XA = sb("XA", [C, 2, CH])
        if kind == "L2":
            XR = sb("XR", [C, 2, CH]); DW = sb("DW", [C, 4, CH])
            RPB = sb("RPB", [SPAN, HEADS, TOK]); MSK = sb("MSK", [SPAN, NROW, PAIRS, TOK])
            BIAS = sb("BIAS", [SPAN, NROW, PAIRS * HEADS, TOK]); SR = sb("SR", [SPAN, 2, PAIRS * HEADS, TOK])
        if kind == "L3":
            Y = sb("Y", [W, 2, WS, C]); SUM = sb("SUM", [C + 1, C])

        loads = [(ident[:], w["ident"]), (mask6[:], w["head_mask"]), (rawq[:], p["qkv_w"]), (brow[C:C + 1, 0:3 * C], row(p["qkv_b"])),
                 (rawp[:], p["proj_w"]), (prow[C:C + 1, :], row(p["proj_b"]))]
        pad_ones = [PS[:], PR[:], XN[C:C + 1], OT[C:C + 1], VB[0:TOK, :, :, :, 2 * HD], VB[HALF:SPAN, :, :, :, 2 * HD + 1]]
        if mlp:
            pad_ones += [XN2[C:C + 1], one[:]]
            loads += [(gb[:, i:i + 1], column(p[n])) for i, n in enumerate(("g1", "b1", "g2", "b2"))]
            loads += [(raw1[:], p["fc1_w"]), (fc2row[:, 0:C], row(p["fc2_b"])), (W2[:, :, 0:C], p["fc2_w"].rearrange("(j h) n -> h j n", j=HB))]
        if kind == "L1":
            loads += [(gb[:, 5:6], column(w["L2_conv_norm_gamma"])), (gb[:, 6:7], column(w["L2_conv_norm_beta"]))]
        if kind == "L2":
            loads += [(gb[:, 0:1], column(p["dw_b"]))]
        load_all(nc, kind, loads, zeros=[VB[:]] + ([RPB[:], MSK[:]] if kind == "L2" else []), values=[(J[:], 1.0 / C), (eps[:], EPS)])
        with nc.Block() as block:
            @block.vector
            def _(dve):
                for t in pad_ones:
                    dve.memset(t, 1.0)
                if kind == "L3":
                    dve.tensor_copy(SUM[0:C], ident[0:C, 0:C])
                    dve.memset(SUM[C:C + 1], 1.0)
        if kind == "L2":
            load_all(nc, "L2b", [(RPB[HALF * e:HALF * e + TOK], p["rpb"]) for e in range(2)]
                     + [(MSK[HALF * e:HALF * e + TOK], p["mask"][e]) for e in range(2)])
            with nc.Block() as block:
                @block.vector
                def _(dve):
                    for r in range(NROW):
                        for k in range(PAIRS):
                            dve.tensor_tensor(BIAS[:, r, k * HEADS:(k + 1) * HEADS], RPB[:],
                                              MSK[:, r, k].unsqueeze(1).broadcast_to([SPAN, HEADS, TOK]), ALU.add)
        third = lambda i: (lambda t: t[:, i * C:(i + 1) * C])
        vhalf = lambda e: (lambda t: t[:, 2 * C:3 * C].rearrange("c (g q d) -> c q g d", g=G, q=2)[:, e])
        fold_affine(nc, kind + "_qkv", rawq[:], brow[C:C + 1, 0:3 * C], gb[:, 0:1] if mlp else None, gb[:, 1:2] if mlp else None,
                    PS[:, 0, :], [(Wq[0:C + 1], third(0)), (Wk[0:C + 1], third(1)), (Wv[0:C + 1, 0], vhalf(0)), (Wv[0:C + 1, 1], vhalf(1))])
        fold_affine(nc, kind + "_proj", rawp[:], prow[C:C + 1, :], None, gb[:, 0:1] if kind == "L2" else None,
                    PS[:, 1, :], [(Wp[0:C + 1, 0:C], lambda t: t)])
        centre_outputs(nc, kind + "_proj_out", [Wp[0:C + 1]])
        if mlp:
            load_all(nc, kind + "c", [(brow[C:C + 1, 0:HID], row(p["fc1_b"]))])
            centre_outputs(nc, kind + "_fc2_out", [W2[:, j] for j in range(HB)], fc2row[:], fc2b[:], one[:], PS[:, 3, :])
            fold_affine(nc, kind + "_fc1", raw1[:], brow[C:C + 1, :], gb[:, 2:3], gb[:, 3:4], PS[:, 2, :], [(W1[0:C + 1, :], lambda t: t)])

        names = ["xn", "k", "q", "v", "qt", "kt", "kx", "v_even", "v_odd", "scores0", "scores1", "rowmax0", "rowmax1",
                 "centred0", "centred1", "probs0", "probs1"]
        names += ["turned0", "turned1", "turned2", "pt0", "pt1", "pt2", "heads", "rsum", "normed", "heads_t", "ot", "proj", "x1"]
        if mlp:
            names += ["sq", "var", "lv", "rstd", "sq2", "var2", "lv2", "rstd2", "xn2", "fc2", "x2"]
            names += [f"fc1_{j}" for j in range(HB)] + [f"gelu_{j}" for j in range(HB)]
        if kind == "L1":
            names += ["sq3", "var3", "lv3", "rstd3", "xh", "xa"]
        if kind == "L2":
            names += ["biased0", "biased1", "kx_act"]
        if kind == "L3":
            names += ["yt", "y"]
        s = {n: sem(n) for n in names}
        loaded = [sem(f"loaded{k}") for k in range(4)]
        norm_loaded = [sem(f"norm_loaded{u}") for u in range(2)] if kind == "L2" else None
        stored = [sem(f"stored{u}") for u in range(2)]
        norm_stored = [sem(f"norm_stored{u}") for u in range(2)] if kind == "L1" else []
        passed = sem("passed")
        N_LOADS = 1 if mlp else 2
        DVE_HEADS = 6 if mlp else 4
        bank = lambda k: PS[:, k, :]
        TURN, OT_BANK, PROJ_BANK = (4, 5, 4), 4, 5
        HEADS_BANK, VALUES_BANK = (5, 2) if mlp else (7, 6)

        def rows_of(t, place):
            b, r = place
            return t[b, :, bass.ds(r * WS, WS), :]

        def win(t):
            return t.rearrange("c (i q j) -> c q i j", i=WS, j=WS)

        def seen(t):
            return t.rearrange("c (q i j) -> c q i j", i=WS, j=WS)

        def window_columns(bk):
            v = bk[0:C, 0:PAIRS * SPAN]
            return bass.AP(v.tensor, v.offset, [v.ap[0], [SPAN, PAIRS], [HALF, 2], [1, TOK]])

        def parity_windows(bk, e):
            v = bk[0:C, 0:PAIRS * SPAN]
            return bass.AP(v.tensor, v.offset + e * HALF, [v.ap[0], [SPAN, PAIRS], [WS, WS], [1, WS]])

        with nc.Block() as block:
            @block.sync
            def _(sp):
                def load(st, lag):
                    k = st.of4(lag)
                    place = st.place(lag)
                    st.wait("x1", lag + 4)
                    sp.dma_start(X[:, k], rows_of(xin, place)).then_inc(loaded[k], 16)
                    if kind == "L2":
                        st.wait("proj", lag + 4)
                        sp.dma_start(DW[:, k], rows_of(conv, place)).then_inc(loaded[k], 16)

                def load_norm(st, lag):
                    place = st.place(lag)
                    st.wait("xn", lag + 2)
                    sp.dma_start(XR[:, st.u], rows_of(xn_io, place)).then_inc(norm_loaded[st.u], 16)

                def step(st):
                    if kind == "L2" and (not st.static or st.t + 2 < NCH):
                        load_norm(st, -2)
                    if not st.static or st.t + 2 < NCH:
                        load(st, -2)
                    if kind == "L2" and st.k:
                        place = st.place(1)
                        st.wait("x1", 1)
                        sp.dma_start(rows_of(xout, place), X1[:, st.v]).then_inc(stored[st.v], 16)
                    if kind == "L1" and st.m:
                        place = st.place(2)
                        st.wait("x2", 2)
                        sp.dma_start(rows_of(xout, place), X2[:, st.u]).then_inc(stored[st.u], 16)
                    if kind == "L1" and st.n:
                        b, r = st.place(3)
                        st.wait("xa", 3)
                        sp.dma_start(xn_io[b, :, bass.ds(r * WS + 3, WS), :], XA[:, st.v]).then_inc(norm_stored[st.v], 16)
                    if kind == "L3" and st.n:
                        b, r = st.place(3)
                        low = r * WS + 3
                        high = ((r + 1) % NROW) * WS
                        if not st.static:
                            low, high = sp.snap(low), sp.snap(high)
                        st.wait("y", 3)
                        for rows, k0, k1 in ((low, 0, 4), (high, 4, 7)):
                            for q0, q1, col in ((0, W - SHIFT, SHIFT), (W - SHIFT, W, 0)):
                                sp.dma_start(xout[b, bass.ds(rows, k1 - k0), col:col + q1 - q0, :].rearrange("h q c -> q h c"),
                                             Y[q0:q1, st.v, k0:k1, :]).then_inc(stored[st.v], 16)

                for c in range(2 if kind == "L2" else 0):
                    load_norm(Step(sp, s, c, c, True), 0)
                for c in range(2):
                    load(Step(sp, s, c, c, True), 0)
                over_chunks(sp, s, step, LAST)
                for u in range(2):
                    sp.wait_ge(stored[u], 16 * N_STORES * (NCH // 2))
                for q in norm_stored:
                    sp.wait_ge(q, 16 * (NCH // 2))

            @block.tensor
            def _(pe):
                def variance(sq, k, ready):
                    pe.matmul(bank(k)[0:C, 0:CH], J[:], sq, start=True, stop=True).then_inc(s[ready], 1)

                def turn(st, a):
                    for k in range(4 * a, 4 * a + 4):
                        mm = pe.transpose(bank(TURN[a])[0:SPAN, (k % 4) * SPAN:(k % 4 + 1) * SPAN],
                                          PR[:, st.v, 2 * k:2 * k + 2, :].rearrange("c h k -> c (h k)")[:, 0:SPAN], ident[0:SPAN, 0:SPAN])
                    mm.then_inc(s[f"turned{a}"], 1)

                def keys_and_queries(st):
                    pe.matmul(bank(1)[0:C, 0:CH], Wk[0:C + 1, :], XN[:, st.u], start=True, stop=True).then_inc(s["k"], 1)
                    pe.matmul(bank(0)[0:C, 0:CH], Wq[0:C + 1, :], XN[:, st.u], start=True, stop=True).then_inc(s["q"], 1)

                def values(st):
                    if mlp:
                        st.wait("centred1", 1)
                    elif not st.static or st.t >= 1:
                        st.wait("v_odd", 1)
                    for q in range(NWIN):
                        for e in range(2):
                            mm = pe.matmul(bank(VALUES_BANK)[HALF * e:HALF * e + TOK, q * G * HD:(q + 1) * G * HD],
                                           XN[:, st.u, q * TOK:(q + 1) * TOK], Wv[0:C + 1, e].rearrange("c g d -> c (g d)"),
                                           start=True, stop=True)
                    mm.then_inc(s["v"], 1)

                def scores(st, half):
                    if half == 0:
                        st.wait("qt", 0)
                        st.wait("kx", 0)
                        if kind == "L2":
                            st.wait("kx_act", 0)
                            st.wait("centred0", 1)
                    elif kind == "L2":
                        st.wait("centred1", 1)
                    else:
                        st.wait("v_even", 0)
                        st.wait("v_odd", 0)
                    for q in range(4 * half, 4 * half + 4):
                        p0 = HALF * (q % 2)
                        mm = pe.matmul(bank(q // 2)[p0:p0 + TOK, 0:HEADS * TOK].rearrange("c (h k) -> c h k", h=HEADS),
                                       QT[:, st.u, q * TOK:(q + 1) * TOK], KX[:, st.u, :, q * TOK:(q + 1) * TOK],
                                       start=True, stop=True)
                    mm.then_inc(s[f"scores{half}"], 1)

                def heads(st):
                    st.wait("pt0", 1)
                    st.wait("pt1", 1)
                    st.wait("pt2", 1)
                    for q in range(NWIN):
                        p0 = HALF * (q % 2)
                        for g in range(G):
                            col = (q // 2 * G + g) * VW
                            mm = pe.matmul(bank(HEADS_BANK)[p0:p0 + TOK, col:col + VW],
                                           PT[:, st.v, q // 2 * G + g, p0:p0 + TOK], VB[:, st.v, q, g, :], start=True, stop=True)
                    mm.then_inc(s["heads"], 1)

                def heads_turned(st):
                    st.wait("normed", 1)
                    for k in range(PAIRS):
                        mm = pe.transpose(bank(OT_BANK)[0:C, k * SPAN:(k + 1) * SPAN], O[:, st.v, k, :], ident[0:SPAN, 0:SPAN])
                    mm.then_inc(s["heads_t"], 1)

                def project(st):
                    if kind == "L2":
                        st.wait_turn(loaded[st.of4(1)], 1, N_LOADS, 4)
                        pe.matmul(bank(PROJ_BANK)[0:C + 1, 0:CH], Wp[0:C, :], DW[:, st.of4(1)], start=True, stop=False)
                    st.wait("ot", 1)
                    pe.matmul(bank(PROJ_BANK)[0:C + 1, 0:CH], Wp[0:C + 1, :], OT[:, st.v], start=mlp, stop=True).then_inc(s["proj"], 1)

                def hidden(st, j):
                    pe.matmul(bank((7, 6, 7)[j])[:, 0:CH], W1[0:C + 1, j * 128:(j + 1) * 128], XN2[:, st.u],
                              start=True, stop=True).then_inc(s[f"fc1_{j}"], 1)

                def to_tokens(st, rows):
                    for k in rows:
                        mm = pe.matmul(bank(6 + k // 5)[0:W, (k % 5) * C:(k % 5 + 1) * C],
                                       X2[:, st.v, k * W:(k + 1) * W], SUM[:], start=True, stop=True)
                    return mm

                def mlp_step(st):
                    if st.f:
                        st.wait("centred0", 1)
                        st.wait("sq", 0)
                        variance(SQ[:, st.u], 0, "var")
                    if st.k:
                        st.wait("probs0", 1)
                        st.wait("x1", 2)
                        turn(st, 0)
                        st.wait("probs1", 1)
                        turn(st, 1)
                    if st.m:
                        st.wait("sq2", 2)
                        variance(SQ2[:, st.u], 7, "var2")
                    if st.n and kind == "L3":
                        hold(pe, s["x2"], st.value(3), passed)
                        to_tokens(st, range(0, 5))
                    if st.f:
                        st.wait("xn", 0)
                        keys_and_queries(st)
                    if st.n and kind == "L1":
                        st.wait("sq3", 3)
                        variance(SQ3[:, st.v], 6, "var3")
                    if st.n and kind == "L3":
                        if st.m:
                            hold(pe, s["lv2"], st.value(2), passed)
                        to_tokens(st, range(5, WS)).then_inc(s["yt"], 1)
                    if st.k:
                        st.wait("pt0", 1)
                        turn(st, 2)
                    if st.f:
                        values(st)
                    if st.m:
                        st.wait("xn2", 2)
                        st.wait("lv3" if kind == "L1" else "y", 3)
                        hidden(st, 0)
                        hidden(st, 1)
                    if st.k:
                        heads(st)
                    if st.f:
                        scores(st, 0)
                    if st.k:
                        heads_turned(st)
                    if st.m:
                        st.wait("gelu_0", 2)
                        hidden(st, 2)
                    if st.k:
                        project(st)
                    if st.f:
                        scores(st, 1)
                    if st.m:
                        for j in range(HB):
                            if j == 0:
                                st.wait("gelu_1", 2)
                            if j == 2:
                                st.wait("gelu_2", 2)
                            mm = pe.matmul(bank(6)[0:C + 1, 0:CH], W2[:, j, :], Hd[:, st.u, j], start=(j == 0), stop=(j == HB - 1))
                        mm.then_inc(s["fc2"], 1)

                def front(st):
                    st.wait("xn", 0)
                    st.wait("centred0", 1)
                    keys_and_queries(st)

                def attention_step(st):
                    if st.k:
                        st.wait("ot", 2)
                        st.wait("probs0", 1)
                        turn(st, 0)
                    if st.f:
                        scores(st, 0)
                    if st.k:
                        st.wait("x1", 2)
                        st.wait("probs1", 1)
                        turn(st, 1)
                    if st.f:
                        values(st)
                    if st.k:
                        st.wait("pt0", 1)
                        turn(st, 2)
                    if st.f:
                        scores(st, 1)
                    if st.k:
                        heads(st)
                    if not st.static or st.t + 1 < NCH:
                        front(st.ahead())
                    if st.k:
                        heads_turned(st)
                        project(st)

                if kind == "L2":
                    front(Step(pe, s, 0, 0, True))
                over_chunks(pe, s, mlp_step if mlp else attention_step, LAST)

            @block.scalar
            def _(act):
                LOG_EXP = "natural_log_exp_and_others"

                def square(n, dst, src):
                    act.activation(dst, src, ACT.Square).then_inc(s["sq" + n], 1)

                def rstd(st, lag, n, lv, rs, k):
                    st.wait("var" + n, lag)
                    act.activation(lv, bank(k)[0:C, 0:CH], ACT.Ln, bias=eps[:, 0:1]).then_inc(s["lv" + n], 1)
                    st.wait("lv" + n, lag)
                    act.activation(rs, lv, ACT.Exp, scale=-0.5).then_inc(s["rstd" + n], 1)

                def pt_copy(st, a):
                    st.wait(f"turned{a}", 1)
                    act.copy(PT[:, st.v, 4 * a:4 * a + 4, :].rearrange("c k q -> c (k q)"), bank(TURN[a])[0:SPAN, 0:4 * SPAN]).then_inc(s[f"pt{a}"], 1)

                def queries(st):
                    st.wait("q", 0)
                    act.mul(QT[:, st.u], bank(0)[0:C, 0:CH], HD ** -0.5).then_inc(s["qt"], 1)

                def values_even(st):
                    st.wait("v", 0)
                    act.copy(VB[0:TOK, st.u, :, :, 0:HD].rearrange("c q g d -> c (q g) d"),
                             bank(VALUES_BANK)[0:TOK, 0:NWIN * G * HD].rearrange("c (k d) -> c k d", d=HD)).then_inc(s["v_even"], 1)

                def probs(st, half, lag):
                    u = st.v if lag else st.u
                    st.wait(f"centred{half}", lag)
                    a = slice(12 * half, 12 * half + 12)
                    act.activation(PR[:, u, a, 0:TOK], SX[:, u, a], ACT.Exp).then_inc(s[f"probs{half}"], 1)

                def mlp_step(st):
                    if st.f:
                        st.wait_turn(loaded[st.of4(0)], 0, N_LOADS, 4)
                        square("", SQ[:, st.u], X[0:C, st.of4(0)])
                    if st.k:
                        probs(st, 1, 1)
                    if st.m:
                        st.wait("x1", 2)
                        square("2", SQ2[:, st.u], X1[0:C, st.u])
                    if st.f:
                        rstd(st, 0, "", LV[:, st.u], RS[:, st.u], 0)
                    if st.m:
                        rstd(st, 2, "2", LV2[:, st.u], RS2[:, st.u], 7)
                    if st.n and kind == "L1":
                        st.wait("x2", 3)
                        square("3", SQ3[:, st.v], X2[0:C, st.v])
                        rstd(st, 3, "3", LV3[:, st.v], RS3[:, st.v], 6)
                    if st.k:
                        pt_copy(st, 1)
                    if st.f:
                        queries(st)
                    if st.n and kind == "L3":
                        st.wait("yt", 3)
                        st.wait_turn(stored[st.v], 5, N_STORES)
                        act.copy(Y[:, st.v, 0:5, :].rearrange("c k n -> c (k n)"), bank(6)[0:W, 0:5 * C])
                        act.copy(Y[:, st.v, 5:7, :].rearrange("c k n -> c (k n)"), bank(7)[0:W, 0:2 * C]).then_inc(s["y"], 1)
                    if st.k:
                        pt_copy(st, 2)
                    if st.f:
                        values_even(st)
                    if st.n and kind == "L1":
                        st.wait("xh", 3)
                        st.wait_turn(norm_stored[st.v], 5, 1)
                        act.activation(XA[:, st.v], XH[:, st.v], ACT.Identity, bias=gb[:, 6:7], scale=gb[:, 5:6]).then_inc(s["xa"], 1)
                    if st.m:
                        for j in (0, 1):
                            st.wait(f"fc1_{j}", 2)
                            act.activation(Hd[:, st.u, j], bank((7, 6, 7)[j])[:, 0:CH], ACT.Gelu).then_inc(s[f"gelu_{j}"], 1)
                    if st.k:
                        st.wait("heads_t", 1)
                        act.copy(OT[0:C, st.v].rearrange("c (k e q) -> c k e q", k=PAIRS, e=2), window_columns(bank(OT_BANK))).then_inc(s["ot"], 1)
                    if st.m:
                        st.wait("fc1_2", 2)
                        act.activation(Hd[:, st.u, 2], bank(7)[:, 0:CH], ACT.Gelu).then_inc(s["gelu_2"], 1)
                        act.preload_act_table_set(LOG_EXP)
                    if st.f:
                        probs(st, 0, 0)

                def front(st):
                    st.wait("k", 0)
                    act.copy(KT[:, st.u], bank(1)[0:C, 0:CH]).then_inc(s["kt"], 1)
                    queries(st)

                def masked_keys(st):
                    st.wait("kt", 0)
                    for h in range(DVE_HEADS, HEADS):
                        ins = act.mul(KX[:, st.u, h], KT[:, st.u], mask6[:, h:h + 1])
                    ins.then_inc(s["kx_act"], 1)

                def attention_step(st):
                    if st.k:
                        pt_copy(st, 0)
                        pt_copy(st, 1)
                    if st.f:
                        values_even(st)
                        act.copy(VB[HALF:SPAN, st.u, :, :, HD:2 * HD].rearrange("c q g d -> c (q g) d"),
                                 bank(VALUES_BANK)[HALF:SPAN, 0:NWIN * G * HD].rearrange("c (k d) -> c k d", d=HD)).then_inc(s["v_odd"], 1)
                        probs(st, 0, 0)
                    if not st.static or st.t + 1 < NCH:
                        front(st.ahead())
                    if st.k:
                        st.wait("heads_t", 1)
                        for e in range(2):
                            ins = act.copy(win(OT[0:C, st.v])[:, e::2], parity_windows(bank(OT_BANK), e))
                        ins.then_inc(s["ot"], 1)
                    if not st.static or st.t + 1 < NCH:
                        masked_keys(st.ahead())
                    if st.f:
                        probs(st, 1, 0)

                act.preload_act_table_set(LOG_EXP)
                if kind == "L2":
                    front(Step(act, s, 0, 0, True))
                    masked_keys(Step(act, s, 0, 0, True))
                over_chunks(act, s, mlp_step if mlp else attention_step, LAST)

            @block.vector
            def _(dve):
                def keys(st):
                    if mlp:
                        st.wait("k", 0)
                        dve.tensor_copy(KT[:, st.u], bank(1)[0:C, 0:CH]).then_inc(s["kt"], 1)
                    st.wait("kt", 0)
                    for h in range(DVE_HEADS):
                        ins = dve.tensor_scalar(KX[:, st.u, h], KT[:, st.u], mask6[:, h:h + 1], None, ALU.mult)
                    ins.then_inc(s["kx"], 1)

                def values_odd(st):
                    st.wait("v", 0)
                    dve.tensor_copy(VB[HALF:SPAN, st.u, :, :, HD:2 * HD].rearrange("c q g d -> c (q g) d"),
                                    bank(2)[HALF:SPAN, 0:NWIN * G * HD].rearrange("c (k d) -> c k d", d=HD)).then_inc(s["v_odd"], 1)

                def centre(st, half):
                    rr = st.place(0)[1] if kind == "L2" else None
                    st.wait(f"scores{half}", 0)
                    src = PS[0:SPAN, 2 * half:2 * half + 2, 0:HEADS * TOK]
                    a = slice(12 * half, 12 * half + 12)
                    mx = MX[:, st.u, half]
                    dst = SX[:, st.u, a]
                    if kind == "L2":
                        bias = BIAS[:, rr, a] if st.static else BIAS[:, bass.ds(rr, 1), a].rearrange("c o k t -> c (o k) t")
                        dve.tensor_tensor(SR[:, st.u, a].rearrange("c (k h) t -> c k (h t)", k=2), src,
                                          bias.rearrange("c (k h) t -> c k (h t)", k=2), ALU.add).then_inc(s[f"biased{half}"], 1)
                        st.wait(f"biased{half}", 0)
                        src = SR[:, st.u, a]
                        spread = mx.unsqueeze(2).broadcast_to([SPAN, 2 * HEADS, TOK])
                    else:
                        src = src.rearrange("c k (h t) -> c k h t", h=HEADS)
                        dst = dst.rearrange("c (k h) t -> c k h t", k=2)
                        mx = mx.rearrange("c (k h) -> c k h", k=2)
                        spread = mx.unsqueeze(3).broadcast_to([SPAN, 2, HEADS, TOK])
                    dve.tensor_reduce(mx, src, AX.X, ALU.max).then_inc(s[f"rowmax{half}"], 1)
                    st.wait(f"rowmax{half}", 0)
                    dve.tensor_tensor(dst, src, spread, ALU.subtract).then_inc(s[f"centred{half}"], 1)

                def pt_copy(st, a):
                    st.wait(f"turned{a}", 1)
                    dve.tensor_copy(PT[:, st.v, 4 * a:4 * a + 4, :].rearrange("c k q -> c (k q)"), bank(TURN[a])[0:SPAN, 0:4 * SPAN]).then_inc(s[f"pt{a}"], 1)

                def over_sums(st):
                    st.wait("heads", 1)
                    ho = bank(HEADS_BANK)[0:SPAN, 0:PAIRS * G * VW].rearrange("c (k n) -> c k n", n=VW)
                    dve.reciprocal(RSUM[:, st.v], ho[:, :, 2 * HD:VW]).then_inc(s["rsum"], 1)
                    st.wait("rsum", 1)
                    dve.tensor_tensor(O[:, st.v].rearrange("c k (g e d) -> c (k g) e d", g=G, e=2),
                                      ho[:, :, 0:2 * HD].rearrange("c k (e d) -> c k e d", e=2),
                                      RSUM[:, st.v].unsqueeze(3).broadcast_to([SPAN, PAIRS * G, 2, HD]), ALU.mult).then_inc(s["normed"], 1)

                def residual(st):
                    st.wait("proj", 1)
                    if kind == "L2":
                        st.wait_turn(stored[st.v], 3, N_STORES)
                    products = bank(PROJ_BANK)[0:C + 1, 0:CH]
                    if kind == "L2":
                        ins = dve.tensor_tensor(X1[:, st.v], products, X[:, st.of4(1)], ALU.add)
                    else:
                        ins = dve.tensor_tensor(win(X1[:, st.v]), seen(products), win(X[:, st.of4(1)]), ALU.add)
                    ins.then_inc(s["x1"], 1)

                def mlp_step(st):
                    if st.k:
                        pt_copy(st, 0)
                    if st.f:
                        st.wait("rstd", 0)
                        dve.tensor_tensor(seen(XN[0:C, st.u]), win(X[0:C, st.of4(0)]), win(RS[:, st.u]), ALU.mult).then_inc(s["xn"], 1)
                    if st.m:
                        st.wait("rstd2", 2)
                        dve.tensor_tensor(XN2[0:C, st.u], X1[0:C, st.u], RS2[:, st.u], ALU.mult).then_inc(s["xn2"], 1)
                    if st.f:
                        keys(st)
                    if st.n and kind == "L1":
                        st.wait("rstd3", 3)
                        dve.tensor_tensor(XH[:, st.v], X2[0:C, st.v], RS3[:, st.v], ALU.mult).then_inc(s["xh"], 1)
                    if st.f:
                        values_odd(st)
                    if st.k:
                        over_sums(st)
                    if st.f:
                        centre(st, 0)
                    if st.k:
                        residual(st)
                    if st.f:
                        centre(st, 1)
                    if st.m:
                        st.wait("fc2", 2)
                        if kind == "L1":
                            st.wait_turn(stored[st.u], 4, N_STORES)
                        dve.scalar_tensor_tensor(X2[:, st.u], bank(6)[0:C + 1, 0:CH], fc2b[:, 0:1], X1[:, st.u], ALU.add, ALU.add).then_inc(s["x2"], 1)

                def attention_step(st):
                    if st.f:
                        centre(st, 0)
                    if st.k:
                        pt_copy(st, 2)
                    if st.f:
                        centre(st, 1)
                    if st.k:
                        over_sums(st)
                    if not st.static or st.t + 1 < NCH:
                        keys(st.ahead())
                    if st.k:
                        residual(st)

                if kind == "L2":
                    keys(Step(dve, s, 0, 0, True))
                over_chunks(dve, s, mlp_step if mlp else attention_step, LAST)

            if kind == "L2":
                @block.gpsimd
                def _(pool):
                    def to_windows(st, lag, u):
                        st.wait("v", lag + 2)
                        c = st.t - lag
                        hold(pool, norm_loaded[u], (c // 2 + 1) * 16, passed)
                        pool.tensor_copy(seen(XN[0:C, u]), win(XR[:, u])).then_inc(s["xn"], 1)

                    def step(st):
                        if not st.static or st.t + 1 < NCH:
                            to_windows(st, -1, st.v)

                    to_windows(Step(pool, s, 0, 0, True), 0, 0)
                    over_chunks(pool, s, step, LAST)


CG, CR = 6, 14
CK = CR + 6
NG, NBK = C // CG, H // CR
IMG = 8
NIG = B // IMG


def conv_pass(nc, PS, w, xn, cv):
    KP, MP = CG * CK, CG * CR
    with ExitStack() as ctx:
        sb = lambda name, shape: ctx.enter_context(nc.sbuf_tensor("conv_" + name, shape, F32))
        sem = ctx.enter_context(semaphores(nc, "conv"))
        WB = sb("WB", [KP, 2, 7, MP]); T = sb("T", [KP, NIG, IMG, PW]); D = sb("D", [MP, NIG, IMG, W])
        BM = sb("BM", [KP, 7, MP]); WC = sb("WC", [KP, NG, 49])
        load_all(nc, "conv", [(BM[:], w["band_mask"])]
                 + [(WC[c * CK:(c + 1) * CK], w["dw_by_channel"].rearrange("(g c) t -> c g t", c=CG)[c:c + 1].broadcast_to([CK, NG, 49]))
                    for c in range(CG)], zeros=[T[:]])
        band_step, band_ready = sem("band_step"), sem("band_ready")
        loaded = [sem(f"loaded{k}") for k in range(NIG)]
        product, read = sem("product"), sem("read")
        stored = [sem(f"stored{k}") for k in range(NIG)]
        passed = sem("passed")
        PER = NBK * NIG
        CREDIT = PER + 1
        with nc.Block() as block:
            @block.vector
            def _(dve):
                with dve.Fori(0, NG // 2) as gg:
                    for e in range(2):
                        dve.wait_ge(product, gg * (2 * PER) + (PER * e + 1))
                        for kh in range(7):
                            for kw in range(7):
                                tap = WC[:, bass.ds(gg * 2 + e, 1), kh * 7 + kw:kh * 7 + kw + 1].rearrange("p a b -> p (a b)")
                                if kh == 0:
                                    ins = dve.tensor_scalar(WB[:, e, kw, :], BM[:, kh, :], tap, None, ALU.mult)
                                else:
                                    ins = dve.scalar_tensor_tensor(WB[:, e, kw, :], BM[:, kh, :], tap, WB[:, e, kw, :], ALU.mult, ALU.add)
                            ins.then_inc(band_step if kh < 6 else band_ready, 1)
                            if kh < 6:
                                dve.wait_ge(band_step, gg * 12 + (6 * e + kh + 1))

            @block.sync
            def _(sp):
                sp.sem_inc(product, CREDIT)
                with sp.Fori(0, NG // 2) as gg:
                    for e in range(2):
                        with sp.Fori(0, NBK) as blk:
                            for k in range(NIG):
                                sp.wait_ge(product, gg * (2 * PER) + blk * NIG + (PER * e + k + 1 + CREDIT - NIG))
                                for c in range(CG):
                                    src = xn[k * IMG:(k + 1) * IMG, bass.ds(gg * (2 * CG) + (e * CG + c), 1), bass.ds(blk * CR, CK), :]
                                    sp.dma_start(T[c * CK:(c + 1) * CK, k, :, 3:3 + W],
                                                 src.rearrange("i c h q -> (c h) i q")).then_inc(loaded[k], 16)

            @block.tensor
            def _(pe):
                with pe.Fori(0, NG // 2) as gg:
                    for e in range(2):
                        hold(pe, band_ready, gg * 2 + (e + 1), passed)
                        with pe.Fori(0, NBK) as blk:
                            for k in range(NIG):
                                pe.wait_ge(loaded[k], gg * (2 * NBK * 16 * CG) + blk * (16 * CG) + (NBK * e + 1) * 16 * CG)
                                pe.wait_ge(read, gg * (2 * PER) + blk * NIG + (PER * e + k + 1))
                                for kw in range(7):
                                    mm = pe.matmul(PS[0:MP, k, 0:IMG * W].rearrange("m (i q) -> m i q", i=IMG), WB[:, e, kw, :],
                                                   T[:, k, :, kw:kw + W], start=(kw == 0), stop=(kw == 6))
                                mm.then_inc(product, 1)

            @block.scalar
            def _(act):
                act.sem_inc(read, NIG)
                for k in range(NIG):
                    act.sem_inc(stored[k], 16 * CG)
                with act.Fori(0, NG) as g:
                    with act.Fori(0, NBK) as blk:
                        for k in range(NIG):
                            act.wait_ge(product, g * PER + blk * NIG + (k + 1 + CREDIT))
                            act.wait_ge(stored[k], g * (NBK * 16 * CG) + blk * (16 * CG) + 16 * CG)
                            act.copy(D[:, k].rearrange("m i q -> m (i q)"), PS[0:MP, k, 0:IMG * W]).then_inc(read, 1)
                            act.wait_ge(read, g * PER + blk * NIG + (k + 1 + NIG))
                            for c in range(CG):
                                dst = cv[k * IMG:(k + 1) * IMG, bass.ds(g * CG + c, 1), bass.ds(blk * CR, CR), :]
                                act.dma_start(dst.rearrange("i c h q -> (c h) i q"), D[c * CR:(c + 1) * CR, k]).then_inc(stored[k], 16)
                for k in range(NIG):
                    act.wait_ge(stored[k], (1 + NG * NBK) * 16 * CG)


def clear_margin(nc, xn):
    with semaphores(nc, "margin") as sem, nc.sbuf_tensor("margin_zero", [C, B * 3 * W], F32) as zero:
        zeroed, cleared = sem("zeroed"), sem("cleared")
        with nc.Block() as block:
            @block.vector
            def _(dve):
                dve.memset(zero[:], 0.0).then_inc(zeroed, 1)

            @block.sync
            def _(sp):
                sp.wait_ge(zeroed, 1)
                for rows in (slice(0, 3), slice(3 + H, 6 + H)):
                    sp.dma_start(xn[:, :, rows, :].rearrange("b c h q -> c b (h q)"),
                                 zero[:].rearrange("c (b n) -> c b n", b=B)).then_inc(cleared, 16)
                sp.wait_ge(cleared, 32)


def build(nc, w, x, out):
    xa = nc.dram_tensor("after_L0", [B, C + 1, H, W], F32).ap()
    xb = nc.dram_tensor("after_L1", [B, C + 1, H, W], F32).ap()
    xn = nc.dram_tensor("L2_norm", [B, C, H + 6, W], F32).ap()
    cv = nc.dram_tensor("L2_conv", [B, C, H, W], F32).ap()
    xc = nc.dram_tensor("after_L2", [B, C + 1, H, W], F32).ap()
    with ExitStack() as ctx:
        PS = ctx.enter_context(nc.psum_tensor("banks", [128, 8, 512], F32))
        clear_margin(nc, xn)
        scan_pass(nc, PS, w, x, xa)
        window_pass(nc, PS, w, "L1", dict(qkv_w=w["L1_conv_w_qkv"], qkv_b=w["L1_conv_b_qkv"], proj_w=w["L1_conv_w_proj"], proj_b=w["L1_conv_b_proj"],
                                          g1=w["L1_conv_g1"], b1=w["L1_conv_b1"], g2=w["L1_conv_g2"], b2=w["L1_conv_b2"], fc1_w=w["L1_conv_w_fc1"],
                                          fc1_b=w["L1_conv_b_fc1"], fc2_w=w["L1_conv_w_fc2"], fc2_b=w["L1_conv_b_fc2"]), xa, xb, xn_io=xn)
        conv_pass(nc, PS, w, xn, cv)
        window_pass(nc, PS, w, "L2", dict(qkv_w=w["L2_conv_qkv_w"], qkv_b=w["L2_conv_qkv_b"], proj_w=w["L2_conv_proj_w"], proj_b=w["L2_conv_proj_b"],
                                          dw_b=w["L2_conv_dw_b"], rpb=w["rpb"], mask=w["mask"]), xb, xc, xn_io=xn[:, :, 3:3 + H, :], conv=cv)
        window_pass(nc, PS, w, "L3", dict(qkv_w=w["L3_conv_qkv_w"], qkv_b=w["L3_conv_qkv_b"], proj_w=w["L3_conv_proj_w"], proj_b=w["L3_conv_proj_b"],
                                          g1=w["L3_conv_ln1_w"], b1=w["L3_conv_ln1_b"], g2=w["L3_conv_ln2_w"], b2=w["L3_conv_ln2_b"], fc1_w=w["L3_conv_mlp_w1"],
                                          fc1_b=w["L3_conv_mlp_b1"], fc2_w=w["L3_conv_mlp_w2"], fc2_b=w["L3_conv_mlp_b2"]), xc, out)


def position_index():
    i = np.arange(TOK)
    dy = i[:, None] // WS - i[None, :] // WS + WS - 1
    dx = i[:, None] % WS - i[None, :] % WS + WS - 1
    return dy * (2 * WS - 1) + dx


def kernel(**inputs):
    import concourse.bacc as bacc
    from concourse.bass_utils import run_bass_kernel_spmd

    a = {k: np.ascontiguousarray(v) for k, v in inputs.items()}
    a["L2_conv_qkv_w"] = np.ascontiguousarray(a["L2_conv_qkv_w"].T)
    a["L2_conv_proj_w"] = np.ascontiguousarray(a["L2_conv_proj_w"].T)
    a["dw_taps"] = np.ascontiguousarray(a.pop("L0_conv_dw_w")[:, 0, :].T)
    a["rpb"] = np.ascontiguousarray(a.pop("L2_conv_rpb_table")[position_index()].transpose(0, 2, 1))
    a["mask"] = np.ascontiguousarray(a.pop("L2_conv_mask_matrix").reshape(NROW, PAIRS, 2, TOK, TOK).transpose(2, 3, 0, 1, 4))
    a["dw_by_channel"] = np.ascontiguousarray(a.pop("L2_conv_dw_w").reshape(49, C).T)
    feeds = np.zeros((CG, CK, 7, CG, CR), np.float32)
    for kh in range(7):
        for a_ in range(CR):
            feeds[np.arange(CG), a_ + kh, kh, np.arange(CG), a_] = 1.0
    a["band_mask"] = feeds.reshape(CG * CK, 7, CG * CR)
    a["ident"] = np.eye(128, dtype=np.float32)
    a["head_mask"] = np.repeat(np.eye(HEADS, dtype=np.float32), HD, axis=0)
    nc = bacc.Bacc("TRN2", target_bir_lowering=False, num_devices=1)
    arrays, aps = {}, {}
    for name, v in a.items():
        arrays["in_" + name] = v
        aps[name] = nc.dram_tensor("in_" + name, v.shape, F32, kind="ExternalInput").ap()
    out = nc.dram_tensor("out", [B, H, W, C], F32, kind="ExternalOutput").ap()
    build(nc, aps, aps["x"], out)
    return run_bass_kernel_spmd(nc, [arrays], core_ids=[0]).results[0]["out"]
```
